# Optimizing a Trainium2 kernel written in Bass

```python
import numpy as np
import jax
import jax.numpy as jnp

def _softmax(x, axis=-1):
    return jax.nn.softmax(x, axis=axis)

def _gelu(x):
    return jax.nn.gelu(x, approximate=True)

def _silu(x):
    return jax.nn.silu(x)

def _sigmoid(x):
    return jax.nn.sigmoid(x)

def _layernorm(x, axis=-1, eps=1e-05):
    m = jnp.mean(x, axis=axis, keepdims=True)
    v = jnp.var(x, axis=axis, keepdims=True)
    return (x - m) / jnp.sqrt(v + eps)

def _scatter_add(tgt, idx, src, axis=0):
    return tgt.at[idx].add(src)

def _segment_sum(src, seg, n):
    return jax.ops.segment_sum(src, seg, n)
kernel_name = 'mk_flamingo_gated_d2_seqx_r4_396625'

def setup_inputs(seed: int=0):
    np.random.seed(seed)
    _w = jnp.asarray

    def _rec_inputs():
        import jax
        import jax.numpy as jnp
        _rk = jax.random.key(seed)
        x = -0.000125 + 0.9999 * jax.random.normal(jax.random.fold_in(_rk, 1), (16, 128, 1024), jnp.float32)
        _lenS = 128 - jax.random.randint(jax.random.fold_in(_rk, 7), (16,), 0, max(1, 128 // 4) + 1, jnp.int32)
        _lenS2 = 128 - jax.random.randint(jax.random.fold_in(_rk, 8), (16,), 0, max(1, 128 // 4) + 1, jnp.int32)
        _ctx_4096P = jax.random.normal(jax.random.fold_in(_rk, 11), (16, 16, 1024), jnp.float32)
        _ctx_4096c = jax.random.dirichlet(jax.random.fold_in(_rk, 511), 0.3 * jnp.ones((16,), jnp.float32), (16, 128))
        _ctx_4096t = jnp.einsum('bsk,bkd->bsd', _ctx_4096c, _ctx_4096P)
        _ctx_4096t = _ctx_4096t * jax.lax.rsqrt(jnp.mean(jnp.square(_ctx_4096t)) + 1e-12) * 0.953939
        ctx_4096 = -1.52775e-05 + 0.999936 * (_ctx_4096t + 0.3 * jax.random.normal(jax.random.fold_in(_rk, 611), (16, 128, 1024), jnp.float32))
        _g = jax.random.normal(jax.random.fold_in(_rk, 9001), (2, 2), jnp.float32)
        _g = jnp.sign(_g) * jnp.maximum(jnp.abs(_g), 1.0) + (_g == 0) * 1.0
        g_xattn = _g[0]
        g_ffn = _g[1]
        return (x, ctx_4096, g_xattn, g_ffn)
    x, ctx_4096, g_xattn, g_ffn = _rec_inputs()

    def _L0_xattn_setup():
        import jax, jax.numpy as jnp
        import numpy as np
        H = 8
        C = 2

        def _autocorrelation(Q, K, V):
            B, L, D = Q.shape
            d = D // H
            q = Q.reshape(B, L, H, d).transpose(0, 2, 1, 3)
            k = K.reshape(B, L, H, d).transpose(0, 2, 1, 3)
            v = V.reshape(B, L, H, d).transpose(0, 2, 1, 3)
            qf = jnp.fft.fft(q, axis=2)
            kf = jnp.fft.fft(k, axis=2)
            corr = jnp.fft.ifft(qf * jnp.conj(kf), axis=2).real
            topk = int(C * np.log(L))
            w, idx = jax.lax.top_k(corr.transpose(0, 1, 3, 2), topk)
            w = jax.nn.softmax(w, axis=-1)
            pos = jnp.arange(L)[:, None]
            out = jnp.zeros_like(v)
            for i in range(topk):
                g = jnp.minimum(idx[:, :, None, :, i] + pos, L - 1)
                out = out + w[:, :, None, :, i] * jnp.take_along_axis(v, g, axis=2)
            return out.transpose(0, 2, 1, 3).reshape(B, L, D)
        key = jax.random.key(seed)
        k1, k2, k3 = jax.random.split(key, 3)
        B, L, D = (16, 128, 1024)
        Q = jax.random.normal(k1, (B, L, D), dtype=jnp.float32)
        K = jax.random.normal(k2, (B, L, D), dtype=jnp.float32)
        V = jax.random.normal(k3, (B, L, D), dtype=jnp.float32)
        return {'Q': Q, 'K': K, 'V': V}
    _L0_xattn_all = _L0_xattn_setup()
    _L0_xattn_in = {k: v for k, v in _L0_xattn_all.items() if k in ()}
    del _L0_xattn_all

    def _L0_ffn_setup():
        import jax, jax.numpy as jnp
        import numpy as np
        SCALING = 32.0 / 16.0
        key = jax.random.key(seed)
        ks = jax.random.split(key, 7)
        B, T, D, O, R, E = (4, 512, 1024, 1024, 16, 8)
        x = jax.random.normal(ks[0], (B, T, D), dtype=jnp.float32)
        base_W = jax.random.normal(ks[1], (O, D), dtype=jnp.float32) * D ** (-0.5)
        base_b = jax.random.normal(ks[2], (O,), dtype=jnp.float32) * 0.01
        router_W = jax.random.normal(ks[3], (2 * E - 1, D), dtype=jnp.float32) * D ** (-0.5)
        router_b = jax.random.normal(ks[4], (2 * E - 1,), dtype=jnp.float32) * 0.01
        A = jax.random.normal(ks[5], (E, R, D), dtype=jnp.float32) * D ** (-0.5)
        Bm = jax.random.normal(ks[6], (E, O, R), dtype=jnp.float32) * R ** (-0.5)
        assigned_idx = 0
        others = [i for i in range(E) if i != assigned_idx]
        expert_map = jnp.array([assigned_idx] * E + others, dtype=jnp.int32)
        return {'x': x, 'base_W': base_W, 'base_b': base_b, 'router_W': router_W, 'router_b': router_b, 'A': A, 'B': Bm, 'expert_map': expert_map}
    _L0_ffn_all = _L0_ffn_setup()
    _L0_ffn_in = {k: v for k, v in _L0_ffn_all.items() if k in ('base_W', 'base_b', 'router_W', 'router_b', 'A', 'B', 'expert_map')}
    del _L0_ffn_all

    def _L1_xattn_setup():
        import jax, jax.numpy as jnp
        import numpy as np
        B, C, N = (8, 64, 1024)
        key = jax.random.key(seed)
        k1, k2, k3 = jax.random.split(key, 3)
        k = jax.random.normal(k1, (B, C, N), dtype=jnp.float32)
        q = jax.random.normal(k2, (B, C, N), dtype=jnp.float32)
        v = jax.random.normal(k3, (B, C, N), dtype=jnpp.float32) if False else jax.random.normal(k3, (B, C, N), dtype=jnp.float32)
        return {'k': k, 'q': q, 'v': v}
    _L1_xattn_all = _L1_xattn_setup()
    _L1_xattn_in = {k: v for k, v in _L1_xattn_all.items() if k in ()}
    del _L1_xattn_all

    def _L1_ffn_setup():
        import jax, jax.numpy as jnp
        import numpy as np
        C_CLAMP = 0.5
        EPS = 1e-06
        key = jax.random.key(seed)
        ks = jax.random.split(key, 6)
        B_, S, D, O, R, E = (4, 512, 1024, 1024, 16, 8)
        x = jax.random.normal(ks[0], (B_, S, D), dtype=jnp.float32)
        W = jax.random.normal(ks[1], (O, D), dtype=jnp.float32) * (1.0 / np.sqrt(D))
        b = jax.random.normal(ks[2], (O,), dtype=jnp.float32) * 0.01
        A = jax.random.normal(ks[3], (E, D, R), dtype=jnp.float32) * (1.0 / np.sqrt(D))
        Bm = jax.random.normal(ks[4], (E, R, O), dtype=jnp.float32) * (1.0 / np.sqrt(R))
        p_scores = jax.random.uniform(ks[5], (E,), dtype=jnp.float32)
        return {'x': x, 'W': W, 'b': b, 'A': A, 'B': Bm, 'p_scores': p_scores}
    _L1_ffn_all = _L1_ffn_setup()
    _L1_ffn_in = {k: v for k, v in _L1_ffn_all.items() if k in ('W', 'b', 'A', 'B', 'p_scores')}
    del _L1_ffn_all
    return {'x': x, 'ctx_4096': ctx_4096, 'g_xattn': g_xattn, 'g_ffn': g_ffn, 'L0_ffn_base_W': _L0_ffn_in['base_W'], 'L0_ffn_base_b': _L0_ffn_in['base_b'], 'L0_ffn_router_W': _L0_ffn_in['router_W'], 'L0_ffn_router_b': _L0_ffn_in['router_b'], 'L0_ffn_A': _L0_ffn_in['A'], 'L0_ffn_B': _L0_ffn_in['B'], 'L0_ffn_expert_map': _L0_ffn_in['expert_map'], 'L1_ffn_W': _L1_ffn_in['W'], 'L1_ffn_b': _L1_ffn_in['b'], 'L1_ffn_A': _L1_ffn_in['A'], 'L1_ffn_B': _L1_ffn_in['B'], 'L1_ffn_p_scores': _L1_ffn_in['p_scores']}

def reference(x, ctx_4096, g_xattn, g_ffn, L0_ffn_base_W, L0_ffn_base_b, L0_ffn_router_W, L0_ffn_router_b, L0_ffn_A, L0_ffn_B, L0_ffn_expert_map, L1_ffn_W, L1_ffn_b, L1_ffn_A, L1_ffn_B, L1_ffn_p_scores):
    import jax
    import jax.numpy as jnp

    def _L0_xattn_ref(Q, K, V):
        import jax, jax.numpy as jnp
        import numpy as np
        H = 8
        C = 2

        def _autocorrelation(Q, K, V):
            B, L, D = Q.shape
            d = D // H
            q = Q.reshape(B, L, H, d).transpose(0, 2, 1, 3)
            k = K.reshape(B, L, H, d).transpose(0, 2, 1, 3)
            v = V.reshape(B, L, H, d).transpose(0, 2, 1, 3)
            qf = jnp.fft.fft(q, axis=2)
            kf = jnp.fft.fft(k, axis=2)
            corr = jnp.fft.ifft(qf * jnp.conj(kf), axis=2).real
            topk = int(C * np.log(L))
            w, idx = jax.lax.top_k(corr.transpose(0, 1, 3, 2), topk)
            w = jax.nn.softmax(w, axis=-1)
            pos = jnp.arange(L)[:, None]
            out = jnp.zeros_like(v)
            for i in range(topk):
                g = jnp.minimum(idx[:, :, None, :, i] + pos, L - 1)
                out = out + w[:, :, None, :, i] * jnp.take_along_axis(v, g, axis=2)
            return out.transpose(0, 2, 1, 3).reshape(B, L, D)
        return _autocorrelation(Q, K, V)

    def _L0_ffn_ref(x, base_W, base_b, router_W, router_b, A, B, expert_map):
        import jax, jax.numpy as jnp
        import numpy as np
        SCALING = 32.0 / 16.0
        E = A.shape[0]
        base_out = jnp.einsum('btd,od->bto', x, base_W) + base_b
        logits = jnp.einsum('btd,nd->btn', x, router_W) + router_b
        probs = jax.nn.softmax(logits, axis=-1)
        topk_p, topk_i = jax.lax.top_k(probs, E)
        mapped = expert_map[topk_i]
        onehot = (mapped[..., None] == jnp.arange(E)).astype(x.dtype)
        w = jnp.einsum('btk,btke->bte', topk_p, onehot)
        h = jnp.einsum('btd,erd->bter', x, A)
        lora = jnp.einsum('bter,eor->bto', h * w[..., None], B) * SCALING
        return base_out + lora

    def _L1_xattn_ref(k, q, v):
        import jax, jax.numpy as jnp
        import numpy as np
        B, C, N = (8, 64, 1024)
        input_dim = k.shape[1]
        scores = jnp.einsum('bcn,bcm->bnm', k, q) / jnp.sqrt(jnp.float32(input_dim))
        attn = jax.nn.softmax(scores, axis=-1)
        out = jnp.einsum('bnm,bcm->bcn', attn, v)
        return out

    def _L1_ffn_ref(x, W, b, A, B, p_scores):
        import jax, jax.numpy as jnp
        import numpy as np
        C_CLAMP = 0.5
        EPS = 1e-06
        z = jnp.einsum('bsd,od->bso', x, W) + b
        u = jnp.einsum('bsd,edr->ebsr', x, A)
        m = jnp.einsum('ebsr,ero,e->bso', u, B, p_scores)
        norm_z = jnp.linalg.norm(z, axis=-1, keepdims=True)
        norm_m = jnp.linalg.norm(m, axis=-1, keepdims=True)
        gamma = jnp.minimum(C_CLAMP * norm_z / (norm_m + EPS), 1.0)
        return z + gamma * m
    x = x + jnp.tanh(g_xattn[0]) * _L0_xattn_ref(_layernorm(x, axis=-1), ctx_4096, ctx_4096)
    x = x + jnp.tanh(g_ffn[0]) * _L0_ffn_ref(_layernorm(x, axis=-1), L0_ffn_base_W, L0_ffn_base_b, L0_ffn_router_W, L0_ffn_router_b, L0_ffn_A, L0_ffn_B, L0_ffn_expert_map)
    x = x + jnp.tanh(g_xattn[1]) * _L1_xattn_ref(ctx_4096, _layernorm(x, axis=-1), ctx_4096)
    x = x + jnp.tanh(g_ffn[1]) * _L1_ffn_ref(_layernorm(x, axis=-1), L1_ffn_W, L1_ffn_b, L1_ffn_A, L1_ffn_B, L1_ffn_p_scores)
    return x

_drawn_inputs = setup_inputs


def setup_inputs(seed=0):
    import zlib

    import numpy as np

    out = dict(_drawn_inputs(seed))
    spreads = {'g_ffn': (-1.0, 0.2)}
    factors = {'L0_ffn_base_b': 8.0, 'L0_ffn_router_b': 8.0, 'L1_ffn_b': 8.0}
    for name, (base, spread) in spreads.items():
        noise = np.random.default_rng([zlib.crc32(name.encode()), seed]).standard_normal(out[name].shape)
        drawn = base * np.exp(spread * noise) if base else spread * noise
        out[name] = jnp.asarray(drawn.astype(out[name].dtype))
    for name, factor in factors.items():
        out[name] = (out[name] * factor).astype(out[name].dtype)
    return out
```

```python
import numpy as np
import concourse.bass as bass
from concourse import mybir
from contextlib import ExitStack

FP = mybir.dt.float32
FR = mybir.dt.float32r
ALU = mybir.AluOpType
ACT = mybir.ActivationFunctionType
AX = mybir.AxisListType

B, L, D = 16, 128, 1024
P = 128
KT = D // P
HALF = 512
E, R = 8, 16
ER = E * R
NR = 2 * E - 1
AR = ER + NR + 1
TOPK = int(2 * np.log(L))
assert TOPK == 9
LN_EPS, EPS, C_CLAMP, LORA_SCALE = 1e-5, 1e-6, 0.5, 2.0
NEG, NEG_TEST = -3.0e38, -1.0e38

(F_CYC, F_CYC_V, F_NEG, F_NEG_V, I_CORR_A, I_CORR_B, I_CYC_A, I_CYC_B, I_NEG_A, I_NEG_B, LAST_ROW,
 IDENT, ONES, N_CONST) = range(14)


def constants():
    l = np.arange(L)
    f = np.arange(L // 2)
    cyc = 2 * np.pi * np.outer(f, l) / L
    neg = 2 * np.pi * np.outer(f + 0.5, l) / L
    fc = np.concatenate([np.cos(cyc), np.sin(cyc)])
    fc[L // 2] = np.cos(np.pi * l)
    fn = np.concatenate([np.cos(neg), np.sin(neg)])
    less_last = np.eye(L)
    less_last[:, L - 1] -= 1.0
    ca = 2.0 / L * np.concatenate([np.cos(cyc), np.cos(cyc)])
    ca[0] = 1.0 / L
    ca[L // 2] = np.cos(np.pi * l) / L
    cb = 2.0 / L * np.concatenate([-np.sin(cyc), np.sin(cyc)])
    cb[0] = cb[L // 2] = 0.0
    na = 2.0 / L * np.concatenate([np.cos(neg), np.cos(neg)])
    nb = 2.0 / L * np.concatenate([-np.sin(neg), np.sin(neg)])
    last = np.zeros((L, L))
    last[L - 1] = 1.0
    mats = [fc.T, (fc @ less_last).T, fn.T, (fn @ less_last).T, ca, cb, ca / 2, -cb / 2, na / 2, -nb / 2,
            last, np.eye(L), np.ones((L, L))]
    return np.ascontiguousarray(np.stack(mats, axis=1), dtype=np.float32)


class Chain:

    def __init__(self, eng, sem, per):
        self.eng, self.sem, self.per = eng, sem, per

    def begin(self, b):
        self.base, self.n = b * self.per, 0

    def add(self, ins):
        self.n += 1
        ins.then_inc(self.sem, 1)

    def wait(self):
        self.eng.wait_ge(self.sem, self.base + self.n)

    def end(self):
        assert self.n == self.per, (self.n, self.per)


def exact3(nc, out, stat, mov, start, stop):
    nc.tensor.matmul(out, stat[1], mov[0], start=start, stop=False)
    nc.tensor.matmul(out, stat[0], mov[1], start=False, stop=False)
    return nc.tensor.matmul(out, stat[0], mov[0], start=False, stop=stop)


def correlation_and_routed_ffn(nc, x, ctx_in, g_x, g_f, w_t, bias, ar_t, rb, b_t, emap, consts, x2_dram):
    ctx = ExitStack()
    with ctx:
        def sb(name, shape, dt=FP):
            return ctx.enter_context(nc.sbuf_tensor(name, shape, dt))

        def pb(name, cols):
            return ctx.enter_context(nc.psum_tensor(name, [P, cols], FP))

        def sem(name):
            return ctx.enter_context(nc.semaphore(name))

        cst = sb("cst", [P, N_CONST, P])
        xs = [sb(f"x_{s}", [P, D]) for s in range(2)]
        cs = [sb(f"ctx_{s}", [P, D]) for s in range(2)]
        wh, wl = sb("w_hi", [P, KT, D], FR), sb("w_lo", [P, KT, D], FR)
        arh, arl = sb("ar_hi", [P, KT, AR], FR), sb("ar_lo", [P, KT, AR], FR)
        bh, bl = sb("b_hi", [P, D], FR), sb("b_lo", [P, D], FR)
        stage = [sb(f"w_stage_{s}", [P, D]) for s in range(2)]
        gbias = sb("gbias", [P, D])
        rbb = sb("router_bias", [P, NR])
        mapi = sb("expert_map", [P, NR], mybir.dt.int32)
        mapf = sb("expert_map_f", [P, NR])
        onehot = sb("onehot", [P, E, NR])
        gates = sb("gates", [P, 2])
        tg = sb("tanh_gates", [P, 2])
        pows = sb("pows", [P, 1])
        q = sb("q", [P, D])
        kc, kcs = sb("k_cyc", [P, D]), sb("k_cyc_swapped", [P, D])
        kn, kns = sb("k_neg", [P, D]), sb("k_neg_swapped", [P, D])
        pa, pbm = sb("prod_a", [P, D]), sb("prod_b", [P, D])
        pc, pd = sb("prod_c", [P, D]), sb("prod_d", [P, D])
        c1, c2 = sb("corr_less_8", [P, D]), sb("corr_less_9", [P, D])
        ew = sb("exp_w", [P, D])
        wm = sb("w_mask", [P, D])
        wts = sb("w_time", [P, D])
        mx = sb("top8", [P, KT, 8])
        mx9 = sb("next8", [P, KT, 8])
        nmx = sb("neg_max", [P, KT])
        md = sb("top_less_max", [P, KT, TOPK])
        me = sb("top_exp", [P, KT, TOPK])
        ms = sb("top_sum", [P, KT])
        x1 = [sb(f"x1_{s}", [P, D]) for s in range(2)]
        x1b = sb("x1_plus_bias", [P, D])
        x2 = sb("x2", [P, D])
        y = sb("ln_x1", [P, D])
        yh, yl = sb("ln_x1_t_hi", [P, KT, P], FR), sb("ln_x1_t_lo", [P, KT, P], FR)
        bn = sb("bn", [P, 2, 6])
        mv0, mv1 = sb("mean_var_x", [P, 2]), sb("mean_var_x1", [P, 2])
        rs0, rs1 = sb("rstd_x", [P, 1]), sb("rstd_x1", [P, 1])
        lg, lg2 = sb("logits", [P, NR]), sb("logits_less_8", [P, NR])
        lm = sb("logits_top8", [P, 8])
        nlm = sb("neg_logit_max", [P, 1])
        pe_, psum_ = sb("p_exp", [P, NR]), sb("p_sum", [P, 1])
        pinv = sb("p_inv", [P, 1])
        pm = sb("p_kept", [P, NR])
        poh = sb("p_onehot", [P, E, NR])
        ewt = sb("expert_w", [P, E])
        hw = sb("h_w", [P, ER])
        hth, htl = sb("h_t_hi", [P, P], FR), sb("h_t_lo", [P, P], FR)

        ps_f = pb("ps_ffn", D)
        ps_h = pb("ps_h", HALF)
        ps_x = pb("ps_x", D)
        ps_y = pb("ps_y", D)
        ps_t = pb("ps_t", HALF)

        consts_in, gates_in, small_in, gbias_in = sem("consts_in"), sem("gates_in"), sem("small_in"), sem("gbias_in")
        x_in, c_in = [sem("x_in0"), sem("x_in1")], [sem("c_in0"), sem("c_in1")]
        stage_in = [sem("stage_in0"), sem("stage_in1")]
        stage_hi, stage_lo = sem("stage_hi"), sem("stage_lo")
        swap_c, swap_n = sem("swap_c"), sem("swap_n")
        x2_out = sem("x2_out")
        setup_dve, tanh_done, pow_ready, gb_ready = sem("setup_dve"), sem("tanh_done"), sem("pow_ready"), sem("gb_ready")
        kc_mm, kn_mm, q_mm, corr_mm, wt_mm = sem("kc_mm"), sem("kn_mm"), sem("q_mm"), sem("corr_mm"), sem("wt_mm")
        wc_mm, wn_mm, out_mm = sem("wc_mm"), sem("wn_mm"), sem("out_mm")
        yt_mm, main_mm, ht_mm, lora_mm = sem("yt_mm"), sem("main_mm"), sem("ht_mm"), sem("lora_mm")
        kc_sb, kn_sb, e_done, te_done, wt_sb = sem("kc_sb"), sem("kn_sb"), sem("e_done"), sem("te_done"), sem("wt_sb")
        yt_hi, yt_lo, pexp, ht_hi, ht_lo = sem("yt_hi"), sem("yt_lo"), sem("pexp"), sem("ht_hi"), sem("ht_lo")
        q_ready, prod_ab, mx_ready, nd_ready, mask_ready = (sem("q_ready"), sem("prod_ab"), sem("mx_ready"),
                                                            sem("nd_ready"), sem("mask_ready"))
        corr_read = sem("corr_read")
        wc_prod, wn_prod, x1_ready, y_ready = sem("wc_prod"), sem("wn_prod"), sem("x1_ready"), sem("y_ready")
        mv0_ready, mv1_ready, rs0_ready, rs1_ready = sem("mv0_ready"), sem("mv1_ready"), sem("rs0_ready"), sem("rs1_ready")
        w_ready, x1b_ready = sem("w_ready"), sem("x1b_ready")
        lm_ready, hw_ready, x2_ready = sem("lm_ready"), sem("hw_ready"), sem("x2_ready")
        dve_l, dve_f, pool_l, pool_f = sem("dve_l"), sem("dve_f"), sem("pool_l"), sem("pool_f")

        SPLITS = [(w_t[k], D, wh[:, k, :], wl[:, k, :]) for k in range(KT)]
        SPLITS += [(b_t, D, bh[:, :], bl[:, :])]
        SPLITS += [(ar_t[:, 0:KT // 2, :], KT // 2 * AR, arh[:, 0:KT // 2, :], arl[:, 0:KT // 2, :]),
                   (ar_t[:, KT // 2:KT, :], KT // 2 * AR, arh[:, KT // 2:KT, :], arl[:, KT // 2:KT, :])]

        def staged(n):
            cols = SPLITS[n][1]
            v = stage[n % 2][:, 0:cols]
            return v if cols == D else v.rearrange("p (k a) -> p k a", a=AR)

        block = ctx.enter_context(nc.Block())

        def whole_loop(eng, first, body, last):
            first()
            with eng.Fori(0, (B - 2) // 2) as p:
                for s in (1, 2):
                    body(p * 2 + s, s % 2, p + (s // 2))
            body(B - 1, (B - 1) % 2, (B - 1) // 2)
            last()

        @block.sync
        def _(sp):
            sp.dma_start(cst[:, :, :], consts).then_inc(consts_in, 16)
            sp.dma_start(gates[:, 0:1], g_x[0:1].partition_broadcast(P)).then_inc(gates_in, 16)
            sp.dma_start(gates[:, 1:2], g_f[0:1].partition_broadcast(P)).then_inc(gates_in, 16)
            for s in range(2):
                sp.dma_start(cs[s][:, :], ctx_in[s]).then_inc(c_in[s], 16)
                sp.dma_start(xs[s][:, :], x[s]).then_inc(x_in[s], 16)
            sp.dma_start(gbias[:, :], bias.partition_broadcast(P)).then_inc(gbias_in, 16)
            sp.dma_start(rbb[:, :], rb.partition_broadcast(P)).then_inc(small_in, 16)
            sp.dma_start(mapi[:, :], emap.partition_broadcast(P)).then_inc(small_in, 16)
            for n in range(2):
                sp.dma_start(staged(n), SPLITS[n][0]).then_inc(stage_in[n], 16)

            def swaps(b):
                for src, dst, made, swap in ((kc, kcs, kc_sb, swap_c), (kn, kns, kn_sb, swap_n)):
                    sp.wait_ge(made, b + 1)
                    sp.dma_start(dst[0:P // 2, :], src[P // 2:P, :]).then_inc(swap, 16)
                    sp.dma_start(dst[P // 2:P, :], src[0:P // 2, :]).then_inc(swap, 16)

            def body(b, s, half):
                swaps(b)
                sp.wait_ge(x2_ready, b)
                sp.dma_start(x2_dram[b - 1], x2[:, :]).then_inc(x2_out, 16)

            def reload(b, s):
                sp.wait_ge(out_mm, b + 1)
                sp.dma_start(cs[s][:, :], ctx_in[b + 2]).then_inc(c_in[s], 16)
                sp.wait_ge(x1_ready, b + 1)
                sp.dma_start(xs[s][:, :], x[b + 2]).then_inc(x_in[s], 16)

            swaps(0)
            for n in range(2, len(SPLITS)):
                sp.wait_ge(stage_hi, n - 1)
                sp.wait_ge(stage_lo, n - 1)
                sp.dma_start(staged(n), SPLITS[n][0]).then_inc(stage_in[n % 2], 16)
            reload(0, 0)
            with sp.Fori(0, (B - 4) // 2) as p:
                for s in (1, 2):
                    body(p * 2 + s, s % 2, None)
                    reload(p * 2 + s, s % 2)
            body(B - 3, 1, None)
            reload(B - 3, 1)
            body(B - 2, 0, None)
            body(B - 1, 1, None)
            sp.wait_ge(x2_ready, B)
            sp.dma_start(x2_dram[B - 1], x2[:, :]).then_inc(x2_out, 16)
            sp.wait_ge(x2_out, 16 * B)

        @block.gpsimd
        def _(pool):
            chl, chf = Chain(pool, pool_l, 1), Chain(pool, pool_f, 1)
            nc.gpsimd.memset(pows[:, :], -0.5).then_inc(pow_ready, 1)

            def rstd(mv, rs, made, ready, ch, b):
                ch.begin(b)
                pool.wait_ge(made, b + 1)
                pool.nop(nofuse=True)
                ch.add(nc.gpsimd.tensor_scalar(rs[:, :], mv[:, 1:2], LN_EPS, None, ALU.add))
                ch.wait()
                nc.gpsimd.tensor_tensor(rs[:, :], rs[:, :], pows[:, :], ALU.pow).then_inc(ready, 1)
                ch.end()

            def l0(b):
                pool.wait_ge(mask_ready, b + 1)
                pool.wait_ge(e_done, b + 1)
                nc.gpsimd.tensor_tensor(wm[:, :], wm[:, :], ew[:, :], ALU.mult).then_inc(w_ready, 1)

            def x1_bias(b, s):
                pool.wait_ge(x1_ready, b + 1)
                pool.wait_ge(gb_ready, 1)
                if not (isinstance(b, int) and b == 0):
                    pool.wait_ge(x2_ready, b)
                nc.gpsimd.tensor_tensor(x1b[:, :], x1[s][:, :], gbias[:, :], ALU.add).then_inc(x1b_ready, 1)

            pool.wait_ge(pow_ready, 1)
            rstd(mv0, rs0, mv0_ready, rs0_ready, chl, 0)
            l0(0)
            rstd(mv0, rs0, mv0_ready, rs0_ready, chl, 1)
            with pool.Fori(0, (B - 2) // 2) as p:
                for s in (1, 2):
                    b = p * 2 + s
                    rstd(mv1, rs1, mv1_ready, rs1_ready, chf, b - 1)
                    x1_bias(b - 1, (s - 1) % 2)
                    l0(b)
                    rstd(mv0, rs0, mv0_ready, rs0_ready, chl, b + 1)
            for b in (B - 1, B):
                rstd(mv1, rs1, mv1_ready, rs1_ready, chf, b - 1)
                x1_bias(b - 1, (b - 1) % 2)
                if b < B:
                    l0(b)

        @block.scalar
        def _(act):
            def setup():
                act.wait_ge(gates_in, 32)
                nc.scalar.activation(tg[:, :], gates[:, :], ACT.Tanh).then_inc(tanh_done, 1)

            def split_weights():
                for n, (_, _, hi, _) in enumerate(SPLITS):
                    act.wait_ge(stage_in[n % 2], 16 * (n // 2 + 1))
                    nc.scalar.activation(hi, staged(n), ACT.Copy).then_inc(stage_hi, 1)

            def k_out(b):
                act.wait_ge(kc_mm, b + 1)
                if not (isinstance(b, int) and b == 0):
                    act.wait_ge(wc_prod, b)
                    act.wait_ge(swap_c, 32 * b)
                nc.scalar.activation(kc[:, :], ps_x[:, :], ACT.Copy).then_inc(kc_sb, 1)
                act.wait_ge(kn_mm, b + 1)
                if not (isinstance(b, int) and b == 0):
                    act.wait_ge(wn_prod, b)
                    act.wait_ge(swap_n, 32 * b)
                nc.scalar.activation(kn[:, :], ps_x[:, :], ACT.Copy).then_inc(kn_sb, 1)

            def corr_exp(b):
                act.wait_ge(mx_ready, b + 1)
                if not (isinstance(b, int) and b == 0):
                    act.wait_ge(w_ready, b)
                for g in range(KT):
                    ins = nc.scalar.activation(ew[:, g * L:(g + 1) * L], ps_y[:, g * L:(g + 1) * L], ACT.Exp,
                                               bias=nmx[:, g:g + 1])
                ins.then_inc(e_done, 1)
                act.wait_ge(nd_ready, b + 1)
                nc.scalar.activation(me[:, :, :], md[:, :, :], ACT.Exp).then_inc(te_done, 1)

            def wt_out(b):
                act.wait_ge(wt_mm, b + 1)
                nc.scalar.activation(wts[:, :], ps_x[:, :], ACT.Copy).then_inc(wt_sb, 1)

            def yt_out(b):
                act.wait_ge(yt_mm, b + 1)
                if not (isinstance(b, int) and b == 0):
                    act.wait_ge(main_mm, b)
                nc.scalar.activation(yh[:, :, :], ps_x[:, :].rearrange("p (k t) -> p k t", t=P),
                                     ACT.Copy).then_inc(yt_hi, 1)

            def router_exp(b):
                act.wait_ge(lm_ready, b + 1)
                nc.scalar.activation(pe_[:, :], lg[:, :], ACT.Exp, bias=nlm[:, 0:1],
                                     accum_out=psum_[:, 0:1]).then_inc(pexp, 1)

            def ht_out(b):
                act.wait_ge(ht_mm, b + 1)
                if not (isinstance(b, int) and b == 0):
                    act.wait_ge(lora_mm, b)
                nc.scalar.activation(hth[:, :], ps_t[:, 0:P], ACT.Copy).then_inc(ht_hi, 1)

            def first():
                setup()
                k_out(0)
                corr_exp(0)
                wt_out(0)
                split_weights()

            def body(b, s, half):
                k_out(b)
                yt_out(b - 1)
                corr_exp(b)
                wt_out(b)
                router_exp(b - 1)
                ht_out(b - 1)

            def last():
                yt_out(B - 1)
                router_exp(B - 1)
                ht_out(B - 1)

            whole_loop(act, first, body, last)

        @block.vector
        def _(dve):
            chl, chf = Chain(dve, dve_l, 12), Chain(dve, dve_f, 10)

            def setup():
                n = [0]

                def step(ins):
                    n[0] += 1
                    ins.then_inc(setup_dve, 1)

                dve.wait_ge(small_in, 32)
                step(nc.vector.tensor_copy(mapf[:, :], mapi[:, :]))
                dve.wait_ge(setup_dve, n[0])
                for e in range(E):
                    step(nc.vector.tensor_scalar(onehot[:, e, :], mapf[:, :], float(e), LORA_SCALE,
                                                 ALU.is_equal, ALU.mult))
                dve.wait_ge(gbias_in, 16)
                dve.wait_ge(tanh_done, 1)
                nc.vector.tensor_scalar(gbias[:, :], gbias[:, :], tg[:, 1:2], None, ALU.mult).then_inc(gb_ready, 1)
                dve.wait_ge(setup_dve, n[0])

            def split_weights():
                for n, (_, _, hi, lo) in enumerate(SPLITS):
                    dve.wait_ge(stage_hi, n + 1)
                    nc.vector.tensor_tensor(lo, staged(n), hi.bitcast(FP), ALU.subtract).then_inc(stage_lo, 1)

            def stats(src, mv, ready, ch):
                for h in range(2):
                    ch.add(nc.vector.bn_stats(bn[:, h, :], src[:, h * HALF:(h + 1) * HALF]))
                ch.wait()
                dve.nop(nofuse=True)
                nc.vector.bn_aggr(mv[:, :], bn[:, :, :]).then_inc(ready, 1)

            def ln_x(b, s, half):
                chl.begin(b)
                dve.wait_ge(x_in[s], 16 * (half + 1))
                stats(xs[s], mv0, mv0_ready, chl)
                dve.wait_ge(rs0_ready, b + 1)
                if not (isinstance(b, int) and b == 0):
                    dve.wait_ge(q_mm, b)
                nc.vector.tensor_scalar(q[:, :], xs[s][:, :], mv0[:, 0:1], rs0[:, 0:1],
                                        ALU.subtract, ALU.mult).then_inc(q_ready, 1)

            def ln_x1(b, s):
                chf.begin(b)
                dve.wait_ge(x1_ready, b + 1)
                stats(x1[s], mv1, mv1_ready, chf)
                dve.wait_ge(rs1_ready, b + 1)
                if not (isinstance(b, int) and b == 0):
                    dve.wait_ge(yt_mm, b)
                nc.vector.tensor_scalar(y[:, :], x1[s][:, :], mv1[:, 0:1], rs1[:, 0:1],
                                        ALU.subtract, ALU.mult).then_inc(y_ready, 1)

            def yt_low(b):
                dve.wait_ge(yt_hi, b + 1)
                nc.vector.tensor_tensor(yl[:, :, :], ps_x[:, :].rearrange("p (k t) -> p k t", t=P),
                                        yh[:, :, :].bitcast(FP), ALU.subtract).then_inc(yt_lo, 1)

            def products(b):
                dve.wait_ge(q_mm, b + 1)
                dve.wait_ge(kc_sb, b + 1)
                if not (isinstance(b, int) and b == 0):
                    dve.wait_ge(out_mm, b)
                chl.add(nc.vector.tensor_tensor(pa[:, :], ps_y[:, :], kc[:, :], ALU.mult))
                dve.wait_ge(swap_c, 32 * (b + 1))
                nc.vector.tensor_tensor(pbm[:, :], ps_y[:, :], kcs[:, :], ALU.mult).then_inc(prod_ab, 1)

            def top_lags(b):
                dve.wait_ge(corr_mm, b + 1)
                dve.nop(nofuse=True)
                blk = [slice(g * L, (g + 1) * L) for g in range(KT)]
                for g in range(KT):
                    ins = nc.vector.max(mx[:, g, :], ps_y[:, blk[g]])
                chl.add(ins)
                chl.wait()
                nc.vector.tensor_scalar(nmx[:, :], mx[:, :, 0], -1.0, None, ALU.mult).then_inc(mx_ready, 1)
                dve.wait_ge(e_done, b + 1)
                dve.nop(nofuse=True)
                for g in range(KT):
                    ins = nc.vector.match_replace(c1[:, blk[g]], mx[:, g, :], ps_y[:, blk[g]], NEG)
                ins.then_inc(corr_read, 1)
                dve.wait_ge(corr_read, b + 1)
                dve.nop(nofuse=True)
                for g in range(KT):
                    ins = nc.vector.max(mx9[:, g, :], c1[:, blk[g]])
                chl.add(ins)
                chl.wait()
                chl.add(nc.vector.memset(mx9[:, :, 1:8], NEG))
                chl.add(nc.vector.tensor_tensor(md[:, :, 0:8], mx[:, :, :],
                                                mx[:, :, 0:1].to_broadcast([P, KT, 8]), ALU.subtract))
                nc.vector.tensor_tensor(md[:, :, 8:9], mx9[:, :, 0:1], mx[:, :, 0:1],
                                        ALU.subtract).then_inc(nd_ready, 1)
                chl.wait()
                dve.nop(nofuse=True)
                for g in range(KT):
                    ins = nc.vector.match_replace(c2[:, blk[g]], mx9[:, g, :], c1[:, blk[g]], NEG)
                chl.add(ins)
                dve.wait_ge(te_done, b + 1)
                chl.add(nc.vector.tensor_reduce(ms[:, :], me[:, :, :], AX.X, ALU.add))
                chl.wait()
                chl.add(nc.vector.reciprocal(ms[:, :], ms[:, :]))
                chl.wait()
                if not (isinstance(b, int) and b == 0):
                    dve.wait_ge(wt_mm, b)
                for g in range(KT):
                    ins = nc.vector.tensor_scalar(wm[:, blk[g]], c2[:, blk[g]], NEG_TEST, ms[:, g:g + 1],
                                                  ALU.is_lt, ALU.mult)
                ins.then_inc(mask_ready, 1)

            def conv(b, s):
                dve.wait_ge(wc_mm, b + 1)
                dve.wait_ge(corr_mm, b + 1)
                chl.add(nc.vector.tensor_tensor(pa[:, :], ps_y[:, :], kc[:, :], ALU.mult))
                dve.wait_ge(swap_c, 32 * (b + 1))
                nc.vector.tensor_tensor(pbm[:, :], ps_y[:, :], kcs[:, :], ALU.mult).then_inc(wc_prod, 1)
                dve.wait_ge(wn_mm, b + 1)
                dve.wait_ge(kn_sb, b + 1)
                chl.add(nc.vector.tensor_tensor(pc[:, :], ps_x[:, :], kn[:, :], ALU.mult))
                dve.wait_ge(swap_n, 32 * (b + 1))
                nc.vector.tensor_tensor(pd[:, :], ps_x[:, :], kns[:, :], ALU.mult).then_inc(wn_prod, 1)
                dve.wait_ge(out_mm, b + 1)
                if not (isinstance(b, int) and b < 2):
                    dve.wait_ge(x1b_ready, b - 1)
                nc.vector.scalar_tensor_tensor(x1[s][:, :], ps_y[:, :], tg[:, 0:1], xs[s][:, :],
                                               ALU.mult, ALU.add).then_inc(x1_ready, 1)
                chl.end()

            def router(b):
                dve.wait_ge(main_mm, b + 1)
                chf.add(nc.vector.tensor_tensor(lg[:, :], ps_h[:, ER:ER + NR], rbb[:, :], ALU.add))
                chf.wait()
                dve.nop(nofuse=True)
                chf.add(nc.vector.max(lm[:, :], lg[:, :]))
                chf.wait()
                nc.vector.tensor_scalar(nlm[:, :], lm[:, 0:1], -1.0, None, ALU.mult).then_inc(lm_ready, 1)
                chf.add(nc.vector.match_replace(lg2[:, :], lm[:, :], lg[:, :], NEG))
                dve.wait_ge(pexp, b + 1)
                chf.add(nc.vector.reciprocal(pinv[:, :], psum_[:, :]))
                chf.wait()
                chf.add(nc.vector.tensor_scalar(pm[:, :], lg2[:, :], NEG_TEST, pinv[:, 0:1], ALU.is_lt, ALU.mult))
                chf.wait()
                chf.add(nc.vector.tensor_tensor(pm[:, :], pm[:, :], pe_[:, :], ALU.mult))
                chf.wait()
                chf.add(nc.vector.tensor_tensor(poh[:, :, :], onehot[:, :, :],
                                                pm[:, :].unsqueeze(1).to_broadcast([P, E, NR]), ALU.mult))
                chf.wait()
                chf.add(nc.vector.tensor_reduce(ewt[:, :], poh[:, :, :], AX.X, ALU.add))
                chf.wait()
                if not (isinstance(b, int) and b == 0):
                    dve.wait_ge(ht_mm, b)
                nc.vector.tensor_tensor(hw[:, :].rearrange("p (e r) -> p e r", r=R),
                                        ps_h[:, 0:ER].rearrange("p (e r) -> p e r", r=R),
                                        ewt[:, :].unsqueeze(2).to_broadcast([P, E, R]),
                                        ALU.mult).then_inc(hw_ready, 1)

            def ht_low(b):
                dve.wait_ge(ht_hi, b + 1)
                nc.vector.tensor_tensor(htl[:, :], ps_t[:, 0:P], hth[:, :].bitcast(FP),
                                        ALU.subtract).then_inc(ht_lo, 1)

            def x2_out_step(b):
                dve.wait_ge(lora_mm, b + 1)
                dve.wait_ge(x1b_ready, b + 1)
                if not (isinstance(b, int) and b == 0):
                    dve.wait_ge(x2_out, 16 * b)
                nc.vector.scalar_tensor_tensor(x2[:, :], ps_f[:, :], tg[:, 1:2], x1b[:, :],
                                               ALU.mult, ALU.add).then_inc(x2_ready, 1)
                chf.end()

            def first():
                setup()
                ln_x(0, 0, 0)
                products(0)
                top_lags(0)
                split_weights()
                conv(0, 0)
                ln_x(1, 1, 0)

            def body(b, s, half):
                ln_x1(b - 1, (s - 1) % 2)
                chl.begin(b)
                chl.n = 2
                products(b)
                yt_low(b - 1)
                top_lags(b)
                router(b - 1)
                ht_low(b - 1)
                conv(b, s)
                x2_out_step(b - 1)
                if not (isinstance(b, int) and b == B - 1):
                    ln_x(b + 1, (s + 1) % 2, half + s)

            def last():
                ln_x1(B - 1, (B - 1) % 2)
                yt_low(B - 1)
                router(B - 1)
                ht_low(B - 1)
                x2_out_step(B - 1)

            first()
            with dve.Fori(0, (B - 2) // 2) as p:
                for s in (1, 2):
                    b = p * 2 + s
                    body(b, s % 2, p + s // 2)
            body(B - 1, (B - 1) % 2, (B - 1) // 2)
            last()

        @block.tensor
        def _(pe):
            def cols(h):
                return slice(h * HALF, (h + 1) * HALF)

            def transform(out, mat, data, done):
                for h in range(2):
                    ins = nc.tensor.matmul(out[:, cols(h)], cst[:, mat, :], data[:, cols(h)], start=True, stop=True)
                ins.then_inc(done, 1)

            def forward(b, s, half):
                pe.wait_ge(c_in[s], 16 * (half + 1))
                if not (isinstance(b, int) and b == 0):
                    pe.wait_ge(wn_prod, b)
                transform(ps_x, F_CYC_V, cs[s], kc_mm)
                pe.wait_ge(q_ready, b + 1)
                if not (isinstance(b, int) and b == 0):
                    pe.wait_ge(x1_ready, b)
                transform(ps_y, F_CYC, q, q_mm)
                pe.wait_ge(kc_sb, b + 1)
                transform(ps_x, F_NEG_V, cs[s], kn_mm)

            def correlate(b):
                pe.wait_ge(prod_ab, b + 1)
                for g in range(KT):
                    blk = slice(g * P, (g + 1) * P)
                    nc.tensor.matmul(ps_y[:, blk], pa[:, blk], cst[:, I_CORR_A, :], start=True, stop=False)
                    ins = nc.tensor.matmul(ps_y[:, blk], pbm[:, blk], cst[:, I_CORR_B, :], start=False, stop=True)
                ins.then_inc(corr_mm, 1)

            def weights_back(b):
                pe.wait_ge(w_ready, b + 1)
                for g in range(KT):
                    blk = slice(g * P, (g + 1) * P)
                    ins = nc.tensor.transpose(ps_x[:, blk], wm[:, blk], cst[:, IDENT, :])
                ins.then_inc(wt_mm, 1)

            def convolve(b, s):
                pe.wait_ge(wt_sb, b + 1)
                pe.wait_ge(corr_read, b + 1)
                transform(ps_y, F_CYC, wts, wc_mm)
                transform(ps_x, F_NEG, wts, wn_mm)
                pe.wait_ge(wc_prod, b + 1)
                pe.wait_ge(wn_prod, b + 1)
                for h in range(2):
                    for n, (mat, data) in enumerate(((LAST_ROW, cs[s]), (I_CYC_A, pa), (I_CYC_B, pbm),
                                                     (I_NEG_A, pc), (I_NEG_B, pd))):
                        ins = nc.tensor.matmul(ps_y[:, cols(h)], cst[:, mat, :], data[:, cols(h)],
                                               start=(n == 0), stop=(n == 4))
                ins.then_inc(out_mm, 1)

            def transpose_y(b):
                pe.wait_ge(y_ready, b + 1)
                for g in range(KT):
                    blk = slice(g * P, (g + 1) * P)
                    ins = nc.tensor.transpose(ps_x[:, blk], y[:, blk], cst[:, IDENT, :])
                ins.then_inc(yt_mm, 1)

            def ffn_main(b):
                pe.wait_ge(yt_lo, b + 1)
                pe.wait_ge(stage_lo, len(SPLITS))
                if not (isinstance(b, int) and b == 0):
                    pe.wait_ge(x2_ready, b)
                    pe.wait_ge(hw_ready, b)
                for k in range(KT):
                    stat = (yh[:, k, :], yl[:, k, :])
                    for h in range(2):
                        exact3(nc, ps_f[:, cols(h)], stat, (wh[:, k, cols(h)], wl[:, k, cols(h)]), k == 0, False)
                    ins = exact3(nc, ps_h[:, 0:AR], stat, (arh[:, k, :], arl[:, k, :]), k == 0, k == KT - 1)
                ins.then_inc(main_mm, 1)

            def transpose_h(b):
                pe.wait_ge(hw_ready, b + 1)
                nc.tensor.transpose(ps_t[:, 0:P], hw[:, :], cst[:, IDENT, :]).then_inc(ht_mm, 1)

            def lora(b):
                pe.wait_ge(ht_lo, b + 1)
                for h in range(2):
                    ins = exact3(nc, ps_f[:, cols(h)], (hth[:, :], htl[:, :]), (bh[:, cols(h)], bl[:, cols(h)]),
                                 False, True)
                ins.then_inc(lora_mm, 1)

            def first():
                pe.wait_ge(consts_in, 16)
                forward(0, 0, 0)
                pe.wait_ge(kn_sb, 1)
                correlate(0)
                weights_back(0)
                convolve(0, 0)

            def body(b, s, half):
                forward(b, s, half)
                pe.wait_ge(kn_sb, b + 1)
                transpose_y(b - 1)
                correlate(b)
                ffn_main(b - 1)
                weights_back(b)
                transpose_h(b - 1)
                lora(b - 1)
                convolve(b, s)

            def last():
                pe.wait_ge(wn_prod, B)
                transpose_y(B - 1)
                ffn_main(B - 1)
                transpose_h(B - 1)
                lora(B - 1)

            whole_loop(pe, first, body, last)


def attention_and_clamped_ffn(nc, ctx_in, ctx_t, g_x, g_f, w_t, bias, a_t, b_t, pscores, consts, x2_dram, out):
    ctx = ExitStack()
    with ctx:
        def sb(name, shape, dt=FP):
            return ctx.enter_context(nc.sbuf_tensor(name, shape, dt))

        def pb(name, cols):
            return ctx.enter_context(nc.psum_tensor(name, [P, cols], FP))

        def sem(name):
            return ctx.enter_context(nc.semaphore(name))

        NG = 4
        TILES = D // P

        ident, ones = sb("ident2", [P, P]), sb("ones2", [P, P])
        wh, wl = sb("w1_hi", [P, KT, D], FR), sb("w1_lo", [P, KT, D], FR)
        ah, al = sb("a1_hi", [P, KT, ER], FR), sb("a1_lo", [P, KT, ER], FR)
        bh, bl = sb("b1_hi", [P, D], FR), sb("b1_lo", [P, D], FR)
        zbias = sb("z_bias", [P, D])
        pbc = sb("p_scores_b", [P, E])
        gates, tg = sb("gates2", [P, 2]), sb("tanh_gates2", [P, 2])
        pow_n, pow_p = sb("minus_half", [P, 1]), sb("plus_half", [P, 2])
        x2 = [sb(f"x2in_{s}", [P, D]) for s in range(2)]
        c, ct = sb("ctx_n", [P, D]), sb("ctx_tr", [P, D])
        q = sb("q2", [P, D])
        ch = [sb(f"c_hi_{s}", [P, D], FR) for s in range(2)]
        cl = [sb(f"c_lo_{s}", [P, D], FR) for s in range(2)]
        qh = sb("q_hi", [P, D], FR)
        ql = sb("q_lo", [P, D], FR)
        vh, vl = sb("v_t_hi", [P, KT, P], FR), sb("v_t_lo", [P, KT, P], FR)
        pr = [sb(f"probs_{s}", [P, D]) for s in range(2)]
        pth, ptl = sb("probs_t_hi", [P, KT, NG * P], FR), sb("probs_t_lo", [P, KT, NG * P], FR)
        nmx = sb("neg_row_max", [P, TILES])
        rsum = sb("row_sum", [P, TILES])
        rinv = sb("row_inv", [P, TILES])
        diag = sb("diag", [P, NG, P])
        rbc = sb("row_inv_b", [P, NG * P])
        x3 = sb("x3", [P, D])
        z = sb("z", [P, D])
        yh, yl = sb("y_t_hi", [P, KT, P], FR), sb("y_t_lo", [P, KT, P], FR)
        bn = sb("bn2", [P, 2, 6])
        mv2, mv3 = sb("mean_var_x2", [P, 2]), sb("mean_var_x3", [P, 2])
        rs2, rs3 = sb("rstd_x2", [P, 1]), sb("rstd_x3", [P, 1])
        us = sb("u_scaled", [P, ER])
        uth, utl = sb("u_t_hi", [P, P], FR), sb("u_t_lo", [P, P], FR)
        nrm = sb("norms", [P, 2])
        nrt = sb("norm_roots", [P, 2])
        gam = sb("gamma", [P, 1])
        x4 = sb("x4", [P, D])
        y = x4

        ps_s = [pb(f"ps_s{s}", D) for s in range(2)]
        ps_t = [pb(f"ps_t{s}", HALF) for s in range(2)]
        ps_o = pb("ps_o", HALF)
        ps_r = pb("ps_r", HALF)

        const_in, gates_in, small_in = sem("const2_in"), sem("gates2_in"), sem("small2_in")
        x2_in = [sem("x2_in0"), sem("x2_in1")]
        c_in, ct_in = sem("c2_in"), sem("ct2_in")
        stage_in = [sem("stage2_in0"), sem("stage2_in1")]
        stage_hi, stage_lo = sem("stage2_hi"), sem("stage2_lo")
        tanh_done, pow_ready = sem("tanh2_done"), sem("pow2_ready")
        out_done = sem("out_done")
        mv2_r, mv3_r, rs2_r, rs3_r = sem("mv2_r"), sem("mv3_r"), sem("rs2_r"), sem("rs3_r")
        q_r, q_hi, q_lo, c_hi, c_lo, v_hi, v_lo = (sem("q2_r"), sem("q2_hi"), sem("q2_lo"), sem("c2_hi"),
                                                   sem("c2_lo"), sem("v2_hi"), sem("v2_lo"))
        s_mm, t_mm, av_mm, r_mm = sem("s_mm"), sem("t_mm"), sem("av_mm"), sem("r_mm")
        yt_mm, z_mm, u_mm, ut_mm, m_mm = sem("yt2_mm"), sem("z_mm"), sem("u_mm"), sem("ut_mm"), sem("m_mm")
        max_r, exp_r, t_hi, t_lo = sem("max_r"), sem("exp_r"), sem("t_hi"), sem("t_lo")
        diag_r, rbc_r, att_r, x3_r = sem("diag_r"), sem("rbc_r"), sem("att_r"), sem("x3_r")
        y_r, yt_hi, yt_lo = sem("y2_r"), sem("yt2_hi"), sem("yt2_lo")
        z_r, u_r, ut_hi, ut_lo, sq_z, sq_m, root_r, x4_r = (sem("z_r"), sem("u_r"), sem("ut_hi"), sem("ut_lo"),
                                                            sem("sq_z"), sem("sq_m"), sem("root_r"), sem("x4_r"))
        rinv_r, rin0, zm_r = sem("rinv_r"), sem("row_inv_first"), sem("z_plus_m")
        dve_q, dve_y, dve_g, pool_q, pool_y = sem("dve_q"), sem("dve_y"), sem("dve_g"), sem("pool_q"), sem("pool_y")

        stage = [pr[0], pr[1]]
        SPLITS = [(w_t[k], wh[:, k, :], wl[:, k, :]) for k in range(KT)]
        SPLITS += [(b_t, bh[:, :], bl[:, :]), (a_t, ah[:, :, :].rearrange("p k a -> p (k a)"),
                                               al[:, :, :].rearrange("p k a -> p (k a)"))]
        block = ctx.enter_context(nc.Block())

        def first_batch(b):
            return isinstance(b, int) and b == 0

        @block.sync
        def _(sp):
            sp.dma_start(x2[0][:, :], x2_dram[0]).then_inc(x2_in[0], 16)
            sp.dma_start(c[:, :], ctx_in[0]).then_inc(c_in, 16)
            sp.dma_start(ct[:, :].rearrange("p (k c) -> p k c", c=P), ctx_t[0]).then_inc(ct_in, 16)
            sp.dma_start(gates[:, 0:1], g_x[1:2].partition_broadcast(P)).then_inc(gates_in, 16)
            sp.dma_start(gates[:, 1:2], g_f[1:2].partition_broadcast(P)).then_inc(gates_in, 16)
            sp.dma_start(ident[:, :], consts[:, IDENT, :]).then_inc(const_in, 16)
            sp.dma_start(ones[:, :], consts[:, ONES, :]).then_inc(const_in, 16)
            sp.dma_start(x2[1][:, :], x2_dram[1]).then_inc(x2_in[1], 16)
            sp.dma_start(zbias[:, :], bias.partition_broadcast(P)).then_inc(small_in, 16)
            sp.dma_start(pbc[:, :], pscores.partition_broadcast(P)).then_inc(small_in, 16)
            for n, (src, _, _) in enumerate(SPLITS):
                if n >= 2:
                    sp.wait_ge(stage_hi, n - 1)
                    sp.wait_ge(stage_lo, n - 1)
                sp.dma_start(stage[n % 2][:, :], src).then_inc(stage_in[n % 2], 16)

            def load_ctx(b):
                sp.wait_ge(c_lo, b)
                sp.dma_start(c[:, :], ctx_in[b]).then_inc(c_in, 16)
                sp.wait_ge(v_lo, b)
                sp.dma_start(ct[:, :].rearrange("p (k c) -> p k c", c=P), ctx_t[b]).then_inc(ct_in, 16)

            def load_x2(b, s):
                sp.wait_ge(x3_r, 2 * (b - 1))
                sp.dma_start(x2[s][:, :], x2_dram[b]).then_inc(x2_in[s], 16)

            def store(b):
                sp.wait_ge(x4_r, b + 1)
                sp.dma_start(out[b], x4[:, :]).then_inc(out_done, 16)

            load_ctx(1)
            load_x2(2, 0)
            with sp.Fori(0, (B - 4) // 2) as p:
                for s in (1, 2):
                    b = p * 2 + s
                    store(b - 1)
                    load_ctx(b + 1)
                    load_x2(b + 2, s % 2)
            store(B - 4)
            load_ctx(B - 2)
            load_x2(B - 1, 1)
            store(B - 3)
            load_ctx(B - 1)
            store(B - 2)
            store(B - 1)
            sp.wait_ge(out_done, 16 * B)

        @block.gpsimd
        def _(pool):
            chq, chy = Chain(pool, pool_q, 2), Chain(pool, pool_y, 1)
            nc.gpsimd.memset(pow_n[:, :], -0.5).then_inc(pow_ready, 1)
            nc.gpsimd.memset(pow_p[:, :], 0.5).then_inc(pow_ready, 1)
            pool.wait_ge(pow_ready, 2)

            def rstd_x2(b):
                chq.begin(b)
                pool.wait_ge(mv2_r, b + 1)
                pool.nop(nofuse=True)
                chq.add(nc.gpsimd.tensor_scalar(rs2[:, :], mv2[:, 1:2], LN_EPS, None, ALU.add))
                chq.wait()
                chq.add(nc.gpsimd.tensor_tensor(rs2[:, :], rs2[:, :], pow_n[:, :], ALU.pow))
                chq.wait()
                pool.nop(nofuse=True)
                nc.gpsimd.tensor_scalar(rs2[:, :], rs2[:, :], float(L) ** -0.5, None, ALU.mult).then_inc(rs2_r, 1)
                chq.end()

            def low_parts(b, s):
                pool.wait_ge(q_hi, b + 1)
                nc.gpsimd.tensor_tensor(ql[:, :], q[:, :], qh[:, :].bitcast(FP), ALU.subtract).then_inc(q_lo, 1)
                pool.wait_ge(c_hi, b + 1)
                nc.gpsimd.tensor_tensor(cl[s][:, :], c[:, :], ch[s][:, :].bitcast(FP),
                                        ALU.subtract).then_inc(c_lo, 1)

            def v_low(b):
                pool.wait_ge(v_hi, b + 1)
                nc.gpsimd.tensor_tensor(vl[:, :, :], ct[:, :].rearrange("p (k c) -> p k c", c=P),
                                        vh[:, :, :].bitcast(FP), ALU.subtract).then_inc(v_lo, 1)

            def diags(b, g):
                pool.wait_ge(rinv_r, 2 * b + g + 1)
                if not (first_batch(b) and g == 0):
                    pool.wait_ge(r_mm, 2 * b + g)
                pool.nop(nofuse=True)
                for t in range(NG):
                    n = NG * g + t
                    ins = nc.gpsimd.tensor_scalar(diag[:, t, :], ident[:, :], rinv[:, n:n + 1], None, ALU.mult)
                ins.then_inc(diag_r, 1)

            def residual(b, s, g):
                pool.wait_ge(att_r, 2 * b + g + 1)
                cols = slice(g * HALF, (g + 1) * HALF)
                nc.gpsimd.tensor_tensor(x3[:, cols], x3[:, cols], x2[s][:, cols], ALU.add).then_inc(x3_r, 1)

            def rstd_x3(b):
                chy.begin(b)
                pool.wait_ge(mv3_r, b + 1)
                pool.nop(nofuse=True)
                chy.add(nc.gpsimd.tensor_scalar(rs3[:, :], mv3[:, 1:2], LN_EPS, None, ALU.add))
                chy.wait()
                nc.gpsimd.tensor_tensor(rs3[:, :], rs3[:, :], pow_n[:, :], ALU.pow).then_inc(rs3_r, 1)
                chy.end()

            def roots(b):
                pool.wait_ge(sq_z, b + 1)
                pool.wait_ge(sq_m, b + 1)
                nc.gpsimd.tensor_tensor(nrt[:, :], nrm[:, :], pow_p[:, :], ALU.pow).then_inc(root_r, 1)

            def batch(b, s, ffn, more):
                if ffn:
                    rstd_x3(b - 1)
                diags(b, 0)
                if ffn:
                    roots(b - 1)
                residual(b, s, 0)
                if more:
                    rstd_x2(b + 1)
                diags(b, 1)
                if more:
                    low_parts(b + 1, 1 - s)
                residual(b, s, 1)
                if more:
                    v_low(b + 1)

            pool.wait_ge(const_in, 32)
            rstd_x2(0)
            low_parts(0, 0)
            v_low(0)
            batch(0, 0, False, True)
            with pool.Fori(0, (B - 2) // 2) as p:
                for s in (1, 2):
                    batch(p * 2 + s, s % 2, True, True)
            batch(B - 1, 1, True, False)
            rstd_x3(B - 1)
            roots(B - 1)

        @block.scalar
        def _(act):
            def high_parts(b, s):
                act.wait_ge(q_r, b + 1)
                if not first_batch(b):
                    act.wait_ge(s_mm, 8 * b)
                nc.scalar.activation(qh[:, :], q[:, :], ACT.Copy).then_inc(q_hi, 1)
                act.wait_ge(c_in, 16 * (b + 1))
                nc.scalar.activation(ch[s][:, :], c[:, :], ACT.Copy).then_inc(c_hi, 1)

            def v_high(b):
                act.wait_ge(ct_in, 16 * (b + 1))
                if not first_batch(b):
                    act.wait_ge(av_mm, 2 * b)
                nc.scalar.activation(vh[:, :, :], ct[:, :].rearrange("p (k c) -> p k c", c=P),
                                     ACT.Copy).then_inc(v_hi, 1)

            def exps(b, n):
                act.wait_ge(max_r, 8 * b + n + 1)
                if not (first_batch(b) and n < 2):
                    act.wait_ge(t_mm, 16 * b + 2 * (n - 1))
                nc.scalar.activation(pr[n % 2][:, :], ps_s[n % 2][:, :], ACT.Exp, bias=nmx[:, n:n + 1],
                                     accum_out=rsum[:, n:n + 1]).then_inc(exp_r, 1)

            def tile_high(b, n):
                for h in range(2):
                    act.wait_ge(t_mm, 16 * b + 2 * n + h + 1)
                    if n % NG == 0 and not (first_batch(b) and n == 0):
                        act.wait_ge(av_mm, 2 * b + n // NG)
                    nc.scalar.activation(pth[:, 4 * h:4 * h + 4, (n % NG) * P:(n % NG + 1) * P],
                                         ps_t[h][:, :].rearrange("p (k t) -> p k t", t=P),
                                         ACT.Copy).then_inc(t_hi, 1)

            def y_high(b):
                for h in range(2):
                    act.wait_ge(yt_mm, 2 * b + h + 1)
                    if not first_batch(b):
                        act.wait_ge(u_mm, b)
                    nc.scalar.activation(yh[:, 4 * h:4 * h + 4, :],
                                         ps_t[h][:, :].rearrange("p (k t) -> p k t", t=P),
                                         ACT.Copy).then_inc(yt_hi, 1)

            def z_norm(b):
                act.wait_ge(z_r, b + 1)
                if not first_batch(b):
                    act.wait_ge(root_r, b)
                    act.wait_ge(x4_r, b)
                nc.scalar.activation(x4[:, :], z[:, :], ACT.Square, accum_out=nrm[:, 0:1]).then_inc(sq_z, 1)

            def u_high(b):
                act.wait_ge(ut_mm, b + 1)
                if not first_batch(b):
                    act.wait_ge(m_mm, b)
                nc.scalar.activation(uth[:, :], ps_r[:, 0:P], ACT.Copy).then_inc(ut_hi, 1)

            def m_norm(b):
                act.wait_ge(m_mm, b + 1)
                act.wait_ge(sq_z, b + 1)
                nc.scalar.activation(x4[:, :], ps_s[1][:, :], ACT.Square, accum_out=nrm[:, 1:2]).then_inc(sq_m, 1)

            def spread(b, g):
                act.wait_ge(r_mm, 2 * b + g + 1)
                if not (first_batch(b) and g == 0):
                    act.wait_ge(att_r, 2 * b + g)
                nc.scalar.activation(rbc[:, :], ps_r[:, :], ACT.Copy).then_inc(rbc_r, 1)

            def ffn_alone(b):
                y_high(b)
                z_norm(b)
                u_high(b)
                m_norm(b)

            def batch(b, s, ffn, more):
                exps(b, 0)
                exps(b, 1)
                tile_high(b, 0)
                exps(b, 2)
                tile_high(b, 1)
                exps(b, 3)
                if ffn:
                    y_high(b - 1)
                tile_high(b, 2)
                if ffn:
                    z_norm(b - 1)
                tile_high(b, 3)
                if ffn:
                    u_high(b - 1)
                    m_norm(b - 1)
                spread(b, 0)
                exps(b, 4)
                exps(b, 5)
                tile_high(b, 4)
                exps(b, 6)
                tile_high(b, 5)
                exps(b, 7)
                tile_high(b, 6)
                tile_high(b, 7)
                if more:
                    high_parts(b + 1, 1 - s)
                spread(b, 1)
                if more:
                    v_high(b + 1)

            act.wait_ge(gates_in, 32)
            nc.scalar.activation(tg[:, :], gates[:, :], ACT.Tanh).then_inc(tanh_done, 1)
            for n, (_, hi, _) in enumerate(SPLITS):
                act.wait_ge(stage_in[n % 2], 16 * (n // 2 + 1))
                nc.scalar.activation(hi, stage[n % 2][:, :], ACT.Copy).then_inc(stage_hi, 1)
            high_parts(0, 0)
            v_high(0)
            act.wait_ge(stage_lo, len(SPLITS))
            batch(0, 0, False, True)
            with act.Fori(0, (B - 2) // 2) as p:
                for s in (1, 2):
                    batch(p * 2 + s, s % 2, True, True)
            batch(B - 1, 1, True, False)
            ffn_alone(B - 1)

        @block.vector
        def _(dve):
            chq, chy, chg = Chain(dve, dve_q, 2), Chain(dve, dve_y, 2), Chain(dve, dve_g, 4)

            def stats(src, mv, ready, ch):
                for h in range(2):
                    ch.add(nc.vector.bn_stats(bn[:, h, :], src[:, h * HALF:(h + 1) * HALF]))
                ch.wait()
                dve.nop(nofuse=True)
                nc.vector.bn_aggr(mv[:, :], bn[:, :, :]).then_inc(ready, 1)

            def ln_x2(b, s, half):
                chq.begin(b)
                dve.wait_ge(x2_in[s], 16 * (half + 1))
                stats(x2[s], mv2, mv2_r, chq)
                dve.wait_ge(rs2_r, b + 1)
                if not first_batch(b):
                    dve.wait_ge(q_lo, b)
                nc.vector.tensor_scalar(q[:, :], x2[s][:, :], mv2[:, 0:1], rs2[:, 0:1],
                                        ALU.subtract, ALU.mult).then_inc(q_r, 1)
                chq.end()

            def ln_x3(b):
                chy.begin(b)
                dve.wait_ge(x3_r, 2 * (b + 1))
                stats(x3, mv3, mv3_r, chy)
                dve.wait_ge(rs3_r, b + 1)
                if not first_batch(b):
                    dve.wait_ge(out_done, 16 * b)
                nc.vector.tensor_scalar(y[:, :], x3[:, :], mv3[:, 0:1], rs3[:, 0:1],
                                        ALU.subtract, ALU.mult).then_inc(y_r, 1)
                chy.end()

            def row_max(b, n):
                dve.wait_ge(s_mm, 8 * b + n + 1)
                if not first_batch(b):
                    dve.wait_ge(exp_r, 8 * (b - 1) + n + 1)
                nc.vector.tensor_reduce(nmx[:, n:n + 1], ps_s[n % 2][:, :], AX.X, ALU.max,
                                        negate=True).then_inc(max_r, 1)

            def tile_low(b, n):
                for h in range(2):
                    dve.wait_ge(t_hi, 16 * b + 2 * n + h + 1)
                    nc.vector.tensor_tensor(ptl[:, 4 * h:4 * h + 4, (n % NG) * P:(n % NG + 1) * P],
                                            ps_t[h][:, :].rearrange("p (k t) -> p k t", t=P),
                                            pth[:, 4 * h:4 * h + 4, (n % NG) * P:(n % NG + 1) * P].bitcast(FP),
                                            ALU.subtract).then_inc(t_lo, 1)

            def y_low(b):
                for h in range(2):
                    dve.wait_ge(yt_hi, 2 * b + h + 1)
                    nc.vector.tensor_tensor(yl[:, 4 * h:4 * h + 4, :],
                                            ps_t[h][:, :].rearrange("p (k t) -> p k t", t=P),
                                            yh[:, 4 * h:4 * h + 4, :].bitcast(FP), ALU.subtract).then_inc(yt_lo, 1)

            def add_bias(b):
                dve.wait_ge(z_mm, b + 1)
                if not first_batch(b):
                    dve.wait_ge(x4_r, b)
                nc.vector.tensor_tensor(z[:, :], ps_s[0][:, :], zbias[:, :], ALU.add).then_inc(z_r, 1)

            def scale_u(b):
                dve.wait_ge(u_mm, b + 1)
                if not first_batch(b):
                    dve.wait_ge(ut_mm, b)
                nc.vector.tensor_tensor(us[:, :].rearrange("p (e r) -> p e r", r=R),
                                        ps_r[:, 0:ER].rearrange("p (e r) -> p e r", r=R),
                                        pbc[:, :].unsqueeze(2).to_broadcast([P, E, R]), ALU.mult).then_inc(u_r, 1)

            def u_low(b):
                dve.wait_ge(ut_hi, b + 1)
                nc.vector.tensor_tensor(utl[:, :], ps_r[:, 0:P], uth[:, :].bitcast(FP),
                                        ALU.subtract).then_inc(ut_lo, 1)

            def finish(b):
                chg.begin(b)
                dve.wait_ge(root_r, b + 1)
                chg.add(nc.vector.tensor_scalar(gam[:, :], nrt[:, 1:2], EPS, None, ALU.add))
                chg.wait()
                chg.add(nc.vector.reciprocal(gam[:, :], gam[:, :]))
                chg.wait()
                chg.add(nc.vector.tensor_scalar(gam[:, :], gam[:, :], nrt[:, 0:1], C_CLAMP, ALU.mult, ALU.mult))
                chg.wait()
                chg.add(nc.vector.tensor_scalar(gam[:, :], gam[:, :], 1.0, None, ALU.min))
                chg.wait()
                nc.vector.scalar_tensor_tensor(z[:, :], ps_s[1][:, :], gam[:, 0:1], z[:, :],
                                               ALU.mult, ALU.add).then_inc(zm_r, 1)
                dve.wait_ge(zm_r, b + 1)
                dve.wait_ge(sq_m, b + 1)
                nc.vector.scalar_tensor_tensor(x4[:, :], z[:, :], tg[:, 1:2], x3[:, :],
                                               ALU.mult, ALU.add).then_inc(x4_r, 1)
                chg.end()

            def inverse_sums(b, g):
                dve.wait_ge(exp_r, 8 * b + NG * (g + 1))
                part = rinv[:, NG * g:NG * (g + 1)]
                if not first_batch(b):
                    dve.wait_ge(diag_r, 2 * (b - 1) + g + 1)
                nc.vector.reciprocal(part, rsum[:, NG * g:NG * (g + 1)]).then_inc(rin0, 1)
                dve.wait_ge(rin0, 2 * b + g + 1)
                nc.vector.tensor_scalar(part, part, tg[:, 0:1], None, ALU.mult).then_inc(rinv_r, 1)

            def attended(b, g):
                dve.wait_ge(rbc_r, 2 * b + g + 1)
                dve.wait_ge(av_mm, 2 * b + g + 1)
                if g == 0 and not first_batch(b):
                    dve.wait_ge(x4_r, b)
                nc.vector.tensor_tensor(x3[:, g * HALF:(g + 1) * HALF], ps_o[:, :], rbc[:, :],
                                        ALU.mult).then_inc(att_r, 1)

            def batch(b, s, half, ffn, more):
                if ffn:
                    ln_x3(b - 1)
                row_max(b, 0)
                row_max(b, 1)
                tile_low(b, 0)
                row_max(b, 2)
                tile_low(b, 1)
                row_max(b, 3)
                if ffn:
                    y_low(b - 1)
                tile_low(b, 2)
                inverse_sums(b, 0)
                if ffn:
                    add_bias(b - 1)
                tile_low(b, 3)
                if ffn:
                    scale_u(b - 1)
                    u_low(b - 1)
                    finish(b - 1)
                attended(b, 0)
                row_max(b, 4)
                row_max(b, 5)
                tile_low(b, 4)
                row_max(b, 6)
                tile_low(b, 5)
                if more:
                    ln_x2(b + 1, 1 - s, half)
                row_max(b, 7)
                tile_low(b, 6)
                inverse_sums(b, 1)
                tile_low(b, 7)
                attended(b, 1)

            ln_x2(0, 0, 0)
            dve.wait_ge(small_in, 32)
            for n, (_, hi, lo) in enumerate(SPLITS):
                dve.wait_ge(stage_hi, n + 1)
                nc.vector.tensor_tensor(lo, stage[n % 2][:, :], hi.bitcast(FP), ALU.subtract).then_inc(stage_lo, 1)
            dve.wait_ge(tanh_done, 1)
            batch(0, 0, 0, False, True)
            with dve.Fori(0, (B - 2) // 2) as p:
                for s in (1, 2):
                    batch(p * 2 + s, s % 2, p + 1, True, True)
            batch(B - 1, 1, None, True, False)
            ln_x3(B - 1)
            y_low(B - 1)
            add_bias(B - 1)
            scale_u(B - 1)
            u_low(B - 1)
            finish(B - 1)

        @block.tensor
        def _(pe):
            def cols(h):
                return slice(h * HALF, (h + 1) * HALF)

            def scores(b, s, n, after=None):
                if n == 0:
                    pe.wait_ge(q_lo, b + 1)
                    pe.wait_ge(c_lo, b + 1)
                if n >= 2 or not first_batch(b):
                    pe.wait_ge(exp_r, 8 * b + n - 1)
                if after is not None:
                    pe.wait_ge(*after)
                blk = slice(n * P, (n + 1) * P)
                for h in range(2):
                    ins = exact3(nc, ps_s[n % 2][:, cols(h)], (ch[s][:, blk], cl[s][:, blk]),
                                 (qh[:, cols(h)], ql[:, cols(h)]), True, True)
                ins.then_inc(s_mm, 1)

            def transposes(b, n, after=None):
                pe.wait_ge(exp_r, 8 * b + n + 1)
                for h in range(2):
                    if not (first_batch(b) and n == 0):
                        pe.wait_ge(t_lo, 16 * b + 2 * n + h - 1)
                    if after is not None:
                        pe.wait_ge(after[0], after[1] + h)
                    for k in range(4):
                        src = pr[n % 2][:, (4 * h + k) * P:(4 * h + k + 1) * P]
                        ins = nc.tensor.transpose(ps_t[h][:, k * P:(k + 1) * P], src, ident[:, :])
                    ins.then_inc(t_mm, 1)

            def transposes_y(b, tile_before):
                pe.wait_ge(y_r, b + 1)
                for h in range(2):
                    pe.wait_ge(t_lo, tile_before + h + 1)
                    for k in range(4):
                        ins = nc.tensor.transpose(ps_t[h][:, k * P:(k + 1) * P],
                                                  y[:, (4 * h + k) * P:(4 * h + k + 1) * P], ident[:, :])
                    ins.then_inc(yt_mm, 1)

            def z_product(b, exps_before):
                pe.wait_ge(yt_lo, 2 * (b + 1))
                pe.wait_ge(exp_r, exps_before)
                for k in range(KT):
                    for h in range(2):
                        ins = exact3(nc, ps_s[0][:, cols(h)], (yh[:, k, :], yl[:, k, :]),
                                     (wh[:, k, cols(h)], wl[:, k, cols(h)]), k == 0, k == KT - 1)
                ins.then_inc(z_mm, 1)

            def u_product(b):
                pe.wait_ge(rbc_r, 2 * (b + 1))
                for k in range(KT):
                    ins = exact3(nc, ps_r[:, 0:ER], (yh[:, k, :], yl[:, k, :]), (ah[:, k, :], al[:, k, :]),
                                 k == 0, k == KT - 1)
                ins.then_inc(u_mm, 1)

            def m_product(b, exps_before):
                pe.wait_ge(u_r, b + 1)
                nc.tensor.transpose(ps_r[:, 0:P], us[:, :], ident[:, :]).then_inc(ut_mm, 1)
                pe.wait_ge(ut_lo, b + 1)
                pe.wait_ge(exp_r, exps_before)
                for h in range(2):
                    ins = exact3(nc, ps_s[1][:, cols(h)], (uth[:, :], utl[:, :]), (bh[:, cols(h)], bl[:, cols(h)]),
                                 True, True)
                ins.then_inc(m_mm, 1)

            def row_factors(b, g):
                pe.wait_ge(diag_r, 2 * b + g + 1)
                if not (first_batch(b) and g == 0):
                    pe.wait_ge(rbc_r, 2 * b + g)
                for t in range(NG):
                    ins = nc.tensor.matmul(ps_r[:, t * P:(t + 1) * P], ones[:, :], diag[:, t, :], start=True, stop=True)
                ins.then_inc(r_mm, 1)

            def values(b, g):
                pe.wait_ge(v_lo, b + 1)
                pe.wait_ge(t_lo, 16 * b + 2 * NG * (g + 1))
                if not (first_batch(b) and g == 0):
                    pe.wait_ge(att_r, 2 * b + g)
                for k in range(KT):
                    ins = exact3(nc, ps_o[:, :], (vh[:, k, :], vl[:, k, :]), (pth[:, k, :], ptl[:, k, :]),
                                 k == 0, k == KT - 1)
                ins.then_inc(av_mm, 1)

            def batch(b, s, ffn):
                scores(b, s, 0)
                scores(b, s, 1)
                transposes(b, 0)
                scores(b, s, 2)
                transposes(b, 1)
                scores(b, s, 3)
                if ffn:
                    transposes_y(b - 1, 16 * b + 2)
                transposes(b, 2, (yt_lo, 2 * b - 1) if ffn else None)
                if ffn:
                    z_product(b - 1, 8 * b + 3)
                transposes(b, 3)
                if ffn:
                    u_product(b - 1)
                    m_product(b - 1, 8 * b + 4)
                row_factors(b, 0)
                values(b, 0)
                scores(b, s, 4, (z_r, b) if ffn else None)
                scores(b, s, 5, (x4_r, b) if ffn else None)
                transposes(b, 4)
                scores(b, s, 6)
                transposes(b, 5)
                scores(b, s, 7)
                transposes(b, 6)
                transposes(b, 7)
                row_factors(b, 1)
                values(b, 1)

            pe.wait_ge(const_in, 32)
            pe.wait_ge(stage_lo, len(SPLITS))
            batch(0, 0, False)
            with pe.Fori(0, (B - 2) // 2) as p:
                for s in (1, 2):
                    batch(p * 2 + s, s % 2, True)
            batch(B - 1, 1, True)
            transposes_y(B - 1, 16 * B - 2)
            z_product(B - 1, 8 * B)
            u_product(B - 1)
            m_product(B - 1, 8 * B)


def build(nc, t):
    x2_dram = nc.dram_tensor("x2_dram", [B, L, D], FP, kind="Internal").ap()
    correlation_and_routed_ffn(nc, t["x"], t["ctx"], t["g_xattn"], t["g_ffn"],
                               t["w0"].rearrange("(k p) o -> k p o", p=P), t["b0"],
                               t["ar0"].rearrange("(k p) a -> p k a", p=P), t["rb0"], t["B0"], t["emap"],
                               t["consts"], x2_dram)
    attention_and_clamped_ffn(nc, t["ctx"], t["ctx_t"].rearrange("b (k p) c -> b p k c", p=P), t["g_xattn"],
                              t["g_ffn"], t["w1"].rearrange("(k p) o -> k p o", p=P), t["b1"], t["A1"],
                              t["B1"], t["p_scores"], t["consts"], x2_dram, t["out"])


def kernel(x, ctx_4096, g_xattn, g_ffn, L0_ffn_base_W, L0_ffn_base_b, L0_ffn_router_W, L0_ffn_router_b, L0_ffn_A,
           L0_ffn_B, L0_ffn_expert_map, L1_ffn_W, L1_ffn_b, L1_ffn_A, L1_ffn_B, L1_ffn_p_scores):
    import concourse.bacc as _bacc
    from concourse.bass_utils import run_bass_kernel_spmd as _run

    a0 = np.asarray(L0_ffn_A).reshape(ER, D).T
    pad = np.zeros((D, 1), np.float32)
    a1 = np.asarray(L1_ffn_A).transpose(1, 0, 2).reshape(KT, P, ER)
    lay = {
        "x": x, "ctx": ctx_4096, "ctx_t": np.asarray(ctx_4096).transpose(0, 2, 1),
        "g_xattn": g_xattn, "g_ffn": g_ffn,
        "w0": np.asarray(L0_ffn_base_W).T, "b0": L0_ffn_base_b,
        "ar0": np.concatenate([a0, np.asarray(L0_ffn_router_W).T, pad], axis=1), "rb0": L0_ffn_router_b,
        "B0": np.asarray(L0_ffn_B).transpose(0, 2, 1).reshape(ER, D), "emap": L0_ffn_expert_map,
        "w1": np.asarray(L1_ffn_W).T, "b1": L1_ffn_b,
        "A1": a1.transpose(1, 0, 2).reshape(P, KT * ER), "B1": np.asarray(L1_ffn_B).reshape(ER, D),
        "p_scores": L1_ffn_p_scores, "consts": constants(),
    }
    nc = _bacc.Bacc("TRN2", target_bir_lowering=False, num_devices=1)
    arrays, t = {}, {}
    for name, a in lay.items():
        a = np.ascontiguousarray(a)
        arrays[f"in_{name}"] = a
        t[name] = nc.dram_tensor(f"in_{name}", a.shape, mybir.dt.from_np(a.dtype), kind="ExternalInput").ap()
    t["out"] = nc.dram_tensor("out_0", (B, L, D), FP, kind="ExternalOutput").ap()
    build(nc, t)
    r = _run(nc, [arrays], core_ids=[0])
    return r.results[0]["out_0"]
```

```python
import numpy as np
import concourse.bass as bass
from concourse import mybir
from contextlib import ExitStack

FP = mybir.dt.float32
FR = mybir.dt.float32r
ALU = mybir.AluOpType
ACT = mybir.ActivationFunctionType
AX = mybir.AxisListType

B, L, D = 16, 128, 1024
P = 128
KT = D // P
HALF = 512
E, R = 8, 16
ER = E * R
NR = 2 * E - 1
AR = ER + NR + 1
TOPK = int(2 * np.log(L))
assert TOPK == 9
LN_EPS, EPS, C_CLAMP, LORA_SCALE = 1e-5, 1e-6, 0.5, 2.0
NEG, NEG_TEST = -3.0e38, -1.0e38

(F_CYC, F_CYC_V, F_NEG, F_NEG_V, I_CORR_A, I_CORR_B, I_CYC_A, I_CYC_B, I_NEG_A, I_NEG_B, LAST_ROW,
 IDENT, ONES, N_CONST) = range(14)


def constants():
    l = np.arange(L)
    f = np.arange(L // 2)
    cyc = 2 * np.pi * np.outer(f, l) / L
    neg = 2 * np.pi * np.outer(f + 0.5, l) / L
    fc = np.concatenate([np.cos(cyc), np.sin(cyc)])
    fc[L // 2] = np.cos(np.pi * l)
    fn = np.concatenate([np.cos(neg), np.sin(neg)])
    less_last = np.eye(L)
    less_last[:, L - 1] -= 1.0
    ca = 2.0 / L * np.concatenate([np.cos(cyc), np.cos(cyc)])
    ca[0] = 1.0 / L
    ca[L // 2] = np.cos(np.pi * l) / L
    cb = 2.0 / L * np.concatenate([-np.sin(cyc), np.sin(cyc)])
    cb[0] = cb[L // 2] = 0.0
    na = 2.0 / L * np.concatenate([np.cos(neg), np.cos(neg)])
    nb = 2.0 / L * np.concatenate([-np.sin(neg), np.sin(neg)])
    last = np.zeros((L, L))
    last[L - 1] = 1.0
    mats = [fc.T, (fc @ less_last).T, fn.T, (fn @ less_last).T, ca, cb, ca / 2, -cb / 2, na / 2, -nb / 2,
            last, np.eye(L), np.ones((L, L))]
    return np.ascontiguousarray(np.stack(mats, axis=1), dtype=np.float32)


class Chain:

    def __init__(self, eng, sem, per):
        self.eng, self.sem, self.per = eng, sem, per

    def begin(self, b):
        self.base, self.n = b * self.per, 0

    def add(self, ins):
        self.n += 1
        ins.then_inc(self.sem, 1)

    def wait(self):
        self.eng.wait_ge(self.sem, self.base + self.n)

    def end(self):
        assert self.n == self.per, (self.n, self.per)


def exact3(nc, out, stat, mov, start, stop):
    nc.tensor.matmul(out, stat[1], mov[0], start=start, stop=False)
    nc.tensor.matmul(out, stat[0], mov[1], start=False, stop=False)
    return nc.tensor.matmul(out, stat[0], mov[0], start=False, stop=stop)


def correlation_and_routed_ffn(nc, x, ctx_in, g_x, g_f, w_t, bias, ar_t, rb, b_t, emap, consts, x2_dram):
    ctx = ExitStack()
    with ctx:
        def sb(name, shape, dt=FP):
            return ctx.enter_context(nc.sbuf_tensor(name, shape, dt))

        def pb(name, cols):
            return ctx.enter_context(nc.psum_tensor(name, [P, cols], FP))

        def sem(name):
            return ctx.enter_context(nc.semaphore(name))

        cst = sb("cst", [P, N_CONST, P])
        xs = [sb(f"x_{s}", [P, D]) for s in range(2)]
        cs = [sb(f"ctx_{s}", [P, D]) for s in range(2)]
        wh, wl = sb("w_hi", [P, KT, D], FR), sb("w_lo", [P, KT, D], FR)
        arh, arl = sb("ar_hi", [P, KT, AR], FR), sb("ar_lo", [P, KT, AR], FR)
        bh, bl = sb("b_hi", [P, D], FR), sb("b_lo", [P, D], FR)
        stage = [sb(f"w_stage_{s}", [P, D]) for s in range(2)]
        gbias = sb("gbias", [P, D])
        rbb = sb("router_bias", [P, NR])
        mapi = sb("expert_map", [P, NR], mybir.dt.int32)
        mapf = sb("expert_map_f", [P, NR])
        onehot = sb("onehot", [P, E, NR])
        gates = sb("gates", [P, 2])
        tg = sb("tanh_gates", [P, 2])
        pows = sb("pows", [P, 1])
        q = sb("q", [P, D])
        kc, kcs = sb("k_cyc", [P, D]), sb("k_cyc_swapped", [P, D])
        kn, kns = sb("k_neg", [P, D]), sb("k_neg_swapped", [P, D])
        pa, pbm = sb("prod_a", [P, D]), sb("prod_b", [P, D])
        pc, pd = sb("prod_c", [P, D]), sb("prod_d", [P, D])
        c1, c2 = sb("corr_less_8", [P, D]), sb("corr_less_9", [P, D])
        ew = sb("exp_w", [P, D])
        wm = sb("w_mask", [P, D])
        wts = sb("w_time", [P, D])
        mx = sb("top8", [P, KT, 8])
        mx9 = sb("next8", [P, KT, 8])
        nmx = sb("neg_max", [P, KT])
        md = sb("top_less_max", [P, KT, TOPK])
        me = sb("top_exp", [P, KT, TOPK])
        ms = sb("top_sum", [P, KT])
        x1 = [sb(f"x1_{s}", [P, D]) for s in range(2)]
        x1b = sb("x1_plus_bias", [P, D])
        x2 = sb("x2", [P, D])
        y = sb("ln_x1", [P, D])
        yh, yl = sb("ln_x1_t_hi", [P, KT, P], FR), sb("ln_x1_t_lo", [P, KT, P], FR)
        bn = sb("bn", [P, 2, 6])
        mv0, mv1 = sb("mean_var_x", [P, 2]), sb("mean_var_x1", [P, 2])
        rs0, rs1 = sb("rstd_x", [P, 1]), sb("rstd_x1", [P, 1])
        lg, lg2 = sb("logits", [P, NR]), sb("logits_less_8", [P, NR])
        lm = sb("logits_top8", [P, 8])
        nlm = sb("neg_logit_max", [P, 1])
        pe_, psum_ = sb("p_exp", [P, NR]), sb("p_sum", [P, 1])
        pinv = sb("p_inv", [P, 1])
        pm = sb("p_kept", [P, NR])
        poh = sb("p_onehot", [P, E, NR])
        ewt = sb("expert_w", [P, E])
        hw = sb("h_w", [P, ER])
        hth, htl = sb("h_t_hi", [P, P], FR), sb("h_t_lo", [P, P], FR)

        ps_f = pb("ps_ffn", D)
        ps_h = pb("ps_h", HALF)
        ps_x = pb("ps_x", D)
        ps_y = pb("ps_y", D)
        ps_t = pb("ps_t", HALF)

        consts_in, gates_in, small_in, gbias_in = sem("consts_in"), sem("gates_in"), sem("small_in"), sem("gbias_in")
        x_in, c_in = [sem("x_in0"), sem("x_in1")], [sem("c_in0"), sem("c_in1")]
        stage_in = [sem("stage_in0"), sem("stage_in1")]
        stage_hi, stage_lo = sem("stage_hi"), sem("stage_lo")
        swap_c, swap_n = sem("swap_c"), sem("swap_n")
        x2_out = sem("x2_out")
        setup_dve, tanh_done, pow_ready, gb_ready = sem("setup_dve"), sem("tanh_done"), sem("pow_ready"), sem("gb_ready")
        kc_mm, kn_mm, q_mm, corr_mm, wt_mm = sem("kc_mm"), sem("kn_mm"), sem("q_mm"), sem("corr_mm"), sem("wt_mm")
        wc_mm, wn_mm, out_mm = sem("wc_mm"), sem("wn_mm"), sem("out_mm")
        yt_mm, main_mm, ht_mm, lora_mm = sem("yt_mm"), sem("main_mm"), sem("ht_mm"), sem("lora_mm")
        kc_sb, kn_sb, e_done, te_done, wt_sb = sem("kc_sb"), sem("kn_sb"), sem("e_done"), sem("te_done"), sem("wt_sb")
        yt_hi, yt_lo, pexp, ht_hi, ht_lo = sem("yt_hi"), sem("yt_lo"), sem("pexp"), sem("ht_hi"), sem("ht_lo")
        q_ready, prod_ab, mx_ready, nd_ready, mask_ready = (sem("q_ready"), sem("prod_ab"), sem("mx_ready"),
                                                            sem("nd_ready"), sem("mask_ready"))
        corr_read = sem("corr_read")
        wc_prod, wn_prod, x1_ready, y_ready = sem("wc_prod"), sem("wn_prod"), sem("x1_ready"), sem("y_ready")
        mv0_ready, mv1_ready, rs0_ready, rs1_ready = sem("mv0_ready"), sem("mv1_ready"), sem("rs0_ready"), sem("rs1_ready")
        w_ready, x1b_ready = sem("w_ready"), sem("x1b_ready")
        lm_ready, hw_ready, x2_ready = sem("lm_ready"), sem("hw_ready"), sem("x2_ready")
        dve_l, dve_f, pool_l, pool_f = sem("dve_l"), sem("dve_f"), sem("pool_l"), sem("pool_f")

        SPLITS = [(w_t[k], D, wh[:, k, :], wl[:, k, :]) for k in range(KT)]
        SPLITS += [(b_t, D, bh[:, :], bl[:, :])]
        SPLITS += [(ar_t[:, 0:KT // 2, :], KT // 2 * AR, arh[:, 0:KT // 2, :], arl[:, 0:KT // 2, :]),
                   (ar_t[:, KT // 2:KT, :], KT // 2 * AR, arh[:, KT // 2:KT, :], arl[:, KT // 2:KT, :])]

        def staged(n):
            cols = SPLITS[n][1]
            v = stage[n % 2][:, 0:cols]
            return v if cols == D else v.rearrange("p (k a) -> p k a", a=AR)

        block = ctx.enter_context(nc.Block())

        def whole_loop(eng, first, body, last):
            first()
            with eng.Fori(0, (B - 2) // 2) as p:
                for s in (1, 2):
                    body(p * 2 + s, s % 2, p + (s // 2))
            body(B - 1, (B - 1) % 2, (B - 1) // 2)
            last()

        @block.sync
        def _(sp):
            sp.dma_start(cst[:, :, :], consts).then_inc(consts_in, 16)
            sp.dma_start(gates[:, 0:1], g_x[0:1].partition_broadcast(P)).then_inc(gates_in, 16)
            sp.dma_start(gates[:, 1:2], g_f[0:1].partition_broadcast(P)).then_inc(gates_in, 16)
            for s in range(2):
                sp.dma_start(cs[s][:, :], ctx_in[s]).then_inc(c_in[s], 16)
                sp.dma_start(xs[s][:, :], x[s]).then_inc(x_in[s], 16)
            sp.dma_start(gbias[:, :], bias.partition_broadcast(P)).then_inc(gbias_in, 16)
            sp.dma_start(rbb[:, :], rb.partition_broadcast(P)).then_inc(small_in, 16)
            sp.dma_start(mapi[:, :], emap.partition_broadcast(P)).then_inc(small_in, 16)
            for n in range(2):
                sp.dma_start(staged(n), SPLITS[n][0]).then_inc(stage_in[n], 16)

            def swaps(b):
                for src, dst, made, swap in ((kc, kcs, kc_sb, swap_c), (kn, kns, kn_sb, swap_n)):
                    sp.wait_ge(made, b + 1)
                    sp.dma_start(dst[0:P // 2, :], src[P // 2:P, :]).then_inc(swap, 16)
                    sp.dma_start(dst[P // 2:P, :], src[0:P // 2, :]).then_inc(swap, 16)

            def body(b, s, half):
                swaps(b)
                sp.wait_ge(x2_ready, b)
                sp.dma_start(x2_dram[b - 1], x2[:, :]).then_inc(x2_out, 16)

            def reload(b, s):
                sp.wait_ge(out_mm, b + 1)
                sp.dma_start(cs[s][:, :], ctx_in[b + 2]).then_inc(c_in[s], 16)
                sp.wait_ge(x1_ready, b + 1)
                sp.dma_start(xs[s][:, :], x[b + 2]).then_inc(x_in[s], 16)

            swaps(0)
            for n in range(2, len(SPLITS)):
                sp.wait_ge(stage_hi, n - 1)
                sp.wait_ge(stage_lo, n - 1)
                sp.dma_start(staged(n), SPLITS[n][0]).then_inc(stage_in[n % 2], 16)
            reload(0, 0)
            with sp.Fori(0, (B - 4) // 2) as p:
                for s in (1, 2):
                    body(p * 2 + s, s % 2, None)
                    reload(p * 2 + s, s % 2)
            body(B - 3, 1, None)
            reload(B - 3, 1)
            body(B - 2, 0, None)
            body(B - 1, 1, None)
            sp.wait_ge(x2_ready, B)
            sp.dma_start(x2_dram[B - 1], x2[:, :]).then_inc(x2_out, 16)
            sp.wait_ge(x2_out, 16 * B)

        @block.gpsimd
        def _(pool):
            chl, chf = Chain(pool, pool_l, 1), Chain(pool, pool_f, 1)
            nc.gpsimd.memset(pows[:, :], -0.5).then_inc(pow_ready, 1)

            def rstd(mv, rs, made, ready, ch, b):
                ch.begin(b)
                pool.wait_ge(made, b + 1)
                pool.nop(nofuse=True)
                ch.add(nc.gpsimd.tensor_scalar(rs[:, :], mv[:, 1:2], LN_EPS, None, ALU.add))
                ch.wait()
                nc.gpsimd.tensor_tensor(rs[:, :], rs[:, :], pows[:, :], ALU.pow).then_inc(ready, 1)
                ch.end()

            def l0(b):
                pool.wait_ge(mask_ready, b + 1)
                pool.wait_ge(e_done, b + 1)
                nc.gpsimd.tensor_tensor(wm[:, :], wm[:, :], ew[:, :], ALU.mult).then_inc(w_ready, 1)

            def x1_bias(b, s):
                pool.wait_ge(x1_ready, b + 1)
                pool.wait_ge(gb_ready, 1)
                if not (isinstance(b, int) and b == 0):
                    pool.wait_ge(x2_ready, b)
                nc.gpsimd.tensor_tensor(x1b[:, :], x1[s][:, :], gbias[:, :], ALU.add).then_inc(x1b_ready, 1)

            pool.wait_ge(pow_ready, 1)
            rstd(mv0, rs0, mv0_ready, rs0_ready, chl, 0)
            l0(0)
            rstd(mv0, rs0, mv0_ready, rs0_ready, chl, 1)
            with pool.Fori(0, (B - 2) // 2) as p:
                for s in (1, 2):
                    b = p * 2 + s
                    rstd(mv1, rs1, mv1_ready, rs1_ready, chf, b - 1)
                    x1_bias(b - 1, (s - 1) % 2)
                    l0(b)
                    rstd(mv0, rs0, mv0_ready, rs0_ready, chl, b + 1)
            for b in (B - 1, B):
                rstd(mv1, rs1, mv1_ready, rs1_ready, chf, b - 1)
                x1_bias(b - 1, (b - 1) % 2)
                if b < B:
                    l0(b)

        @block.scalar
        def _(act):
            def setup():
                act.wait_ge(gates_in, 32)
                nc.scalar.activation(tg[:, :], gates[:, :], ACT.Tanh).then_inc(tanh_done, 1)

            def split_weights():
                for n, (_, _, hi, _) in enumerate(SPLITS):
                    act.wait_ge(stage_in[n % 2], 16 * (n // 2 + 1))
                    nc.scalar.activation(hi, staged(n), ACT.Copy).then_inc(stage_hi, 1)

            def k_out(b):
                act.wait_ge(kc_mm, b + 1)
                if not (isinstance(b, int) and b == 0):
                    act.wait_ge(wc_prod, b)
                    act.wait_ge(swap_c, 32 * b)
                nc.scalar.activation(kc[:, :], ps_x[:, :], ACT.Copy).then_inc(kc_sb, 1)
                act.wait_ge(kn_mm, b + 1)
                if not (isinstance(b, int) and b == 0):
                    act.wait_ge(wn_prod, b)
                    act.wait_ge(swap_n, 32 * b)
                nc.scalar.activation(kn[:, :], ps_x[:, :], ACT.Copy).then_inc(kn_sb, 1)

            def corr_exp(b):
                act.wait_ge(mx_ready, b + 1)
                if not (isinstance(b, int) and b == 0):
                    act.wait_ge(w_ready, b)
                for g in range(KT):
                    ins = nc.scalar.activation(ew[:, g * L:(g + 1) * L], ps_y[:, g * L:(g + 1) * L], ACT.Exp,
                                               bias=nmx[:, g:g + 1])
                ins.then_inc(e_done, 1)
                act.wait_ge(nd_ready, b + 1)
                nc.scalar.activation(me[:, :, :], md[:, :, :], ACT.Exp).then_inc(te_done, 1)

            def wt_out(b):
                act.wait_ge(wt_mm, b + 1)
                nc.scalar.activation(wts[:, :], ps_x[:, :], ACT.Copy).then_inc(wt_sb, 1)

            def yt_out(b):
                act.wait_ge(yt_mm, b + 1)
                if not (isinstance(b, int) and b == 0):
                    act.wait_ge(main_mm, b)
                nc.scalar.activation(yh[:, :, :], ps_x[:, :].rearrange("p (k t) -> p k t", t=P),
                                     ACT.Copy).then_inc(yt_hi, 1)

            def router_exp(b):
                act.wait_ge(lm_ready, b + 1)
                nc.scalar.activation(pe_[:, :], lg[:, :], ACT.Exp, bias=nlm[:, 0:1],
                                     accum_out=psum_[:, 0:1]).then_inc(pexp, 1)

            def ht_out(b):
                act.wait_ge(ht_mm, b + 1)
                if not (isinstance(b, int) and b == 0):
                    act.wait_ge(lora_mm, b)
                nc.scalar.activation(hth[:, :], ps_t[:, 0:P], ACT.Copy).then_inc(ht_hi, 1)

            def first():
                setup()
                k_out(0)
                corr_exp(0)
                wt_out(0)
                split_weights()

            def body(b, s, half):
                k_out(b)
                yt_out(b - 1)
                corr_exp(b)
                wt_out(b)
                router_exp(b - 1)
                ht_out(b - 1)

            def last():
                yt_out(B - 1)
                router_exp(B - 1)
                ht_out(B - 1)

            whole_loop(act, first, body, last)

        @block.vector
        def _(dve):
            chl, chf = Chain(dve, dve_l, 12), Chain(dve, dve_f, 10)

            def setup():
                n = [0]

                def step(ins):
                    n[0] += 1
                    ins.then_inc(setup_dve, 1)

                dve.wait_ge(small_in, 32)
                step(nc.vector.tensor_copy(mapf[:, :], mapi[:, :]))
                dve.wait_ge(setup_dve, n[0])
                for e in range(E):
                    step(nc.vector.tensor_scalar(onehot[:, e, :], mapf[:, :], float(e), LORA_SCALE,
                                                 ALU.is_equal, ALU.mult))
                dve.wait_ge(gbias_in, 16)
                dve.wait_ge(tanh_done, 1)
                nc.vector.tensor_scalar(gbias[:, :], gbias[:, :], tg[:, 1:2], None, ALU.mult).then_inc(gb_ready, 1)
                dve.wait_ge(setup_dve, n[0])

            def split_weights():
                for n, (_, _, hi, lo) in enumerate(SPLITS):
                    dve.wait_ge(stage_hi, n + 1)
                    nc.vector.tensor_tensor(lo, staged(n), hi.bitcast(FP), ALU.subtract).then_inc(stage_lo, 1)

            def stats(src, mv, ready, ch):
                for h in range(2):
                    ch.add(nc.vector.bn_stats(bn[:, h, :], src[:, h * HALF:(h + 1) * HALF]))
                ch.wait()
                dve.nop(nofuse=True)
                nc.vector.bn_aggr(mv[:, :], bn[:, :, :]).then_inc(ready, 1)

            def ln_x(b, s, half):
                chl.begin(b)
                dve.wait_ge(x_in[s], 16 * (half + 1))
                stats(xs[s], mv0, mv0_ready, chl)
                dve.wait_ge(rs0_ready, b + 1)
                if not (isinstance(b, int) and b == 0):
                    dve.wait_ge(q_mm, b)
                nc.vector.tensor_scalar(q[:, :], xs[s][:, :], mv0[:, 0:1], rs0[:, 0:1],
                                        ALU.subtract, ALU.mult).then_inc(q_ready, 1)

            def ln_x1(b, s):
                chf.begin(b)
                dve.wait_ge(x1_ready, b + 1)
                stats(x1[s], mv1, mv1_ready, chf)
                dve.wait_ge(rs1_ready, b + 1)
                if not (isinstance(b, int) and b == 0):
                    dve.wait_ge(yt_mm, b)
                nc.vector.tensor_scalar(y[:, :], x1[s][:, :], mv1[:, 0:1], rs1[:, 0:1],
                                        ALU.subtract, ALU.mult).then_inc(y_ready, 1)

            def yt_low(b):
                dve.wait_ge(yt_hi, b + 1)
                nc.vector.tensor_tensor(yl[:, :, :], ps_x[:, :].rearrange("p (k t) -> p k t", t=P),
                                        yh[:, :, :].bitcast(FP), ALU.subtract).then_inc(yt_lo, 1)

            def products(b):
                dve.wait_ge(q_mm, b + 1)
                dve.wait_ge(kc_sb, b + 1)
                if not (isinstance(b, int) and b == 0):
                    dve.wait_ge(out_mm, b)
                chl.add(nc.vector.tensor_tensor(pa[:, :], ps_y[:, :], kc[:, :], ALU.mult))
                dve.wait_ge(swap_c, 32 * (b + 1))
                nc.vector.tensor_tensor(pbm[:, :], ps_y[:, :], kcs[:, :], ALU.mult).then_inc(prod_ab, 1)

            def top_lags(b):
                dve.wait_ge(corr_mm, b + 1)
                dve.nop(nofuse=True)
                blk = [slice(g * L, (g + 1) * L) for g in range(KT)]
                for g in range(KT):
                    ins = nc.vector.max(mx[:, g, :], ps_y[:, blk[g]])
                chl.add(ins)
                chl.wait()
                nc.vector.tensor_scalar(nmx[:, :], mx[:, :, 0], -1.0, None, ALU.mult).then_inc(mx_ready, 1)
                dve.wait_ge(e_done, b + 1)
                dve.nop(nofuse=True)
                for g in range(KT):
                    ins = nc.vector.match_replace(c1[:, blk[g]], mx[:, g, :], ps_y[:, blk[g]], NEG)
                ins.then_inc(corr_read, 1)
                dve.wait_ge(corr_read, b + 1)
                dve.nop(nofuse=True)
                for g in range(KT):
                    ins = nc.vector.max(mx9[:, g, :], c1[:, blk[g]])
                chl.add(ins)
                chl.wait()
                chl.add(nc.vector.memset(mx9[:, :, 1:8], NEG))
                chl.add(nc.vector.tensor_tensor(md[:, :, 0:8], mx[:, :, :],
                                                mx[:, :, 0:1].to_broadcast([P, KT, 8]), ALU.subtract))
                nc.vector.tensor_tensor(md[:, :, 8:9], mx9[:, :, 0:1], mx[:, :, 0:1],
                                        ALU.subtract).then_inc(nd_ready, 1)
                chl.wait()
                dve.nop(nofuse=True)
                for g in range(KT):
                    ins = nc.vector.match_replace(c2[:, blk[g]], mx9[:, g, :], c1[:, blk[g]], NEG)
                chl.add(ins)
                dve.wait_ge(te_done, b + 1)
                chl.add(nc.vector.tensor_reduce(ms[:, :], me[:, :, :], AX.X, ALU.add))
                chl.wait()
                chl.add(nc.vector.reciprocal(ms[:, :], ms[:, :]))
                chl.wait()
                if not (isinstance(b, int) and b == 0):
                    dve.wait_ge(wt_mm, b)
                for g in range(KT):
                    ins = nc.vector.tensor_scalar(wm[:, blk[g]], c2[:, blk[g]], NEG_TEST, ms[:, g:g + 1],
                                                  ALU.is_lt, ALU.mult)
                ins.then_inc(mask_ready, 1)

            def conv(b, s):
                dve.wait_ge(wc_mm, b + 1)
                dve.wait_ge(corr_mm, b + 1)
                chl.add(nc.vector.tensor_tensor(pa[:, :], ps_y[:, :], kc[:, :], ALU.mult))
                dve.wait_ge(swap_c, 32 * (b + 1))
                nc.vector.tensor_tensor(pbm[:, :], ps_y[:, :], kcs[:, :], ALU.mult).then_inc(wc_prod, 1)
                dve.wait_ge(wn_mm, b + 1)
                dve.wait_ge(kn_sb, b + 1)
                chl.add(nc.vector.tensor_tensor(pc[:, :], ps_x[:, :], kn[:, :], ALU.mult))
                dve.wait_ge(swap_n, 32 * (b + 1))
                nc.vector.tensor_tensor(pd[:, :], ps_x[:, :], kns[:, :], ALU.mult).then_inc(wn_prod, 1)
                dve.wait_ge(out_mm, b + 1)
                if not (isinstance(b, int) and b < 2):
                    dve.wait_ge(x1b_ready, b - 1)
                nc.vector.scalar_tensor_tensor(x1[s][:, :], ps_y[:, :], tg[:, 0:1], xs[s][:, :],
                                               ALU.mult, ALU.add).then_inc(x1_ready, 1)
                chl.end()

            def router(b):
                dve.wait_ge(main_mm, b + 1)
                chf.add(nc.vector.tensor_tensor(lg[:, :], ps_h[:, ER:ER + NR], rbb[:, :], ALU.add))
                chf.wait()
                dve.nop(nofuse=True)
                chf.add(nc.vector.max(lm[:, :], lg[:, :]))
                chf.wait()
                nc.vector.tensor_scalar(nlm[:, :], lm[:, 0:1], -1.0, None, ALU.mult).then_inc(lm_ready, 1)
                chf.add(nc.vector.match_replace(lg2[:, :], lm[:, :], lg[:, :], NEG))
                dve.wait_ge(pexp, b + 1)
                chf.add(nc.vector.reciprocal(pinv[:, :], psum_[:, :]))
                chf.wait()
                chf.add(nc.vector.tensor_scalar(pm[:, :], lg2[:, :], NEG_TEST, pinv[:, 0:1], ALU.is_lt, ALU.mult))
                chf.wait()
                chf.add(nc.vector.tensor_tensor(pm[:, :], pm[:, :], pe_[:, :], ALU.mult))
                chf.wait()
                chf.add(nc.vector.tensor_tensor(poh[:, :, :], onehot[:, :, :],
                                                pm[:, :].unsqueeze(1).to_broadcast([P, E, NR]), ALU.mult))
                chf.wait()
                chf.add(nc.vector.tensor_reduce(ewt[:, :], poh[:, :, :], AX.X, ALU.add))
                chf.wait()
                if not (isinstance(b, int) and b == 0):
                    dve.wait_ge(ht_mm, b)
                nc.vector.tensor_tensor(hw[:, :].rearrange("p (e r) -> p e r", r=R),
                                        ps_h[:, 0:ER].rearrange("p (e r) -> p e r", r=R),
                                        ewt[:, :].unsqueeze(2).to_broadcast([P, E, R]),
                                        ALU.mult).then_inc(hw_ready, 1)

            def ht_low(b):
                dve.wait_ge(ht_hi, b + 1)
                nc.vector.tensor_tensor(htl[:, :], ps_t[:, 0:P], hth[:, :].bitcast(FP),
                                        ALU.subtract).then_inc(ht_lo, 1)

            def x2_out_step(b):
                dve.wait_ge(lora_mm, b + 1)
                dve.wait_ge(x1b_ready, b + 1)
                if not (isinstance(b, int) and b == 0):
                    dve.wait_ge(x2_out, 16 * b)
                nc.vector.scalar_tensor_tensor(x2[:, :], ps_f[:, :], tg[:, 1:2], x1b[:, :],
                                               ALU.mult, ALU.add).then_inc(x2_ready, 1)
                chf.end()

            def first():
                setup()
                ln_x(0, 0, 0)
                products(0)
                top_lags(0)
                split_weights()
                conv(0, 0)
                ln_x(1, 1, 0)

            def body(b, s, half):
                ln_x1(b - 1, (s - 1) % 2)
                chl.begin(b)
                chl.n = 2
                products(b)
                yt_low(b - 1)
                top_lags(b)
                router(b - 1)
                ht_low(b - 1)
                conv(b, s)
                x2_out_step(b - 1)
                if not (isinstance(b, int) and b == B - 1):
                    ln_x(b + 1, (s + 1) % 2, half + s)

            def last():
                ln_x1(B - 1, (B - 1) % 2)
                yt_low(B - 1)
                router(B - 1)
                ht_low(B - 1)
                x2_out_step(B - 1)

            first()
            with dve.Fori(0, (B - 2) // 2) as p:
                for s in (1, 2):
                    b = p * 2 + s
                    body(b, s % 2, p + s // 2)
            body(B - 1, (B - 1) % 2, (B - 1) // 2)
            last()

        @block.tensor
        def _(pe):
            def cols(h):
                return slice(h * HALF, (h + 1) * HALF)

            def transform(out, mat, data, done):
                for h in range(2):
                    ins = nc.tensor.matmul(out[:, cols(h)], cst[:, mat, :], data[:, cols(h)], start=True, stop=True)
                ins.then_inc(done, 1)

            def forward(b, s, half):
                pe.wait_ge(c_in[s], 16 * (half + 1))
                if not (isinstance(b, int) and b == 0):
                    pe.wait_ge(wn_prod, b)
                transform(ps_x, F_CYC_V, cs[s], kc_mm)
                pe.wait_ge(q_ready, b + 1)
                if not (isinstance(b, int) and b == 0):
                    pe.wait_ge(x1_ready, b)
                transform(ps_y, F_CYC, q, q_mm)
                pe.wait_ge(kc_sb, b + 1)
                transform(ps_x, F_NEG_V, cs[s], kn_mm)

            def correlate(b):
                pe.wait_ge(prod_ab, b + 1)
                for g in range(KT):
                    blk = slice(g * P, (g + 1) * P)
                    nc.tensor.matmul(ps_y[:, blk], pa[:, blk], cst[:, I_CORR_A, :], start=True, stop=False)
                    ins = nc.tensor.matmul(ps_y[:, blk], pbm[:, blk], cst[:, I_CORR_B, :], start=False, stop=True)
                ins.then_inc(corr_mm, 1)

            def weights_back(b):
                pe.wait_ge(w_ready, b + 1)
                for g in range(KT):
                    blk = slice(g * P, (g + 1) * P)
                    ins = nc.tensor.transpose(ps_x[:, blk], wm[:, blk], cst[:, IDENT, :])
                ins.then_inc(wt_mm, 1)

            def convolve(b, s):
                pe.wait_ge(wt_sb, b + 1)
                pe.wait_ge(corr_read, b + 1)
                transform(ps_y, F_CYC, wts, wc_mm)
                transform(ps_x, F_NEG, wts, wn_mm)
                pe.wait_ge(wc_prod, b + 1)
                pe.wait_ge(wn_prod, b + 1)
                for h in range(2):
                    for n, (mat, data) in enumerate(((LAST_ROW, cs[s]), (I_CYC_A, pa), (I_CYC_B, pbm),
                                                     (I_NEG_A, pc), (I_NEG_B, pd))):
                        ins = nc.tensor.matmul(ps_y[:, cols(h)], cst[:, mat, :], data[:, cols(h)],
                                               start=(n == 0), stop=(n == 4))
                ins.then_inc(out_mm, 1)

            def transpose_y(b):
                pe.wait_ge(y_ready, b + 1)
                for g in range(KT):
                    blk = slice(g * P, (g + 1) * P)
                    ins = nc.tensor.transpose(ps_x[:, blk], y[:, blk], cst[:, IDENT, :])
                ins.then_inc(yt_mm, 1)

            def ffn_main(b):
                pe.wait_ge(yt_lo, b + 1)
                pe.wait_ge(stage_lo, len(SPLITS))
                if not (isinstance(b, int) and b == 0):
                    pe.wait_ge(x2_ready, b)
                    pe.wait_ge(hw_ready, b)
                for k in range(KT):
                    stat = (yh[:, k, :], yl[:, k, :])
                    for h in range(2):
                        exact3(nc, ps_f[:, cols(h)], stat, (wh[:, k, cols(h)], wl[:, k, cols(h)]), k == 0, False)
                    ins = exact3(nc, ps_h[:, 0:AR], stat, (arh[:, k, :], arl[:, k, :]), k == 0, k == KT - 1)
                ins.then_inc(main_mm, 1)

            def transpose_h(b):
                pe.wait_ge(hw_ready, b + 1)
                nc.tensor.transpose(ps_t[:, 0:P], hw[:, :], cst[:, IDENT, :]).then_inc(ht_mm, 1)

            def lora(b):
                pe.wait_ge(ht_lo, b + 1)
                for h in range(2):
                    ins = exact3(nc, ps_f[:, cols(h)], (hth[:, :], htl[:, :]), (bh[:, cols(h)], bl[:, cols(h)]),
                                 False, True)
                ins.then_inc(lora_mm, 1)

            def first():
                pe.wait_ge(consts_in, 16)
                forward(0, 0, 0)
                pe.wait_ge(kn_sb, 1)
                correlate(0)
                weights_back(0)
                convolve(0, 0)

            def body(b, s, half):
                forward(b, s, half)
                pe.wait_ge(kn_sb, b + 1)
                transpose_y(b - 1)
                correlate(b)
                ffn_main(b - 1)
                weights_back(b)
                transpose_h(b - 1)
                lora(b - 1)
                convolve(b, s)

            def last():
                pe.wait_ge(wn_prod, B)
                transpose_y(B - 1)
                ffn_main(B - 1)
                transpose_h(B - 1)
                lora(B - 1)

            whole_loop(pe, first, body, last)


def attention_and_clamped_ffn(nc, ctx_in, ctx_t, g_x, g_f, w_t, bias, a_t, b_t, pscores, consts, x2_dram, out):
    ctx = ExitStack()
    with ctx:
        def sb(name, shape, dt=FP):
            return ctx.enter_context(nc.sbuf_tensor(name, shape, dt))

        def pb(name, cols):
            return ctx.enter_context(nc.psum_tensor(name, [P, cols], FP))

        def sem(name):
            return ctx.enter_context(nc.semaphore(name))

        TILES = D // P
        GT = 2
        GROUPS = TILES // GT
        GC = GT * P

        ident = sb("ident2", [P, P])
        wh, wl = sb("w1_hi", [P, KT, D], FR), sb("w1_lo", [P, KT, D], FR)
        ah, al = sb("a1_hi", [P, KT, ER], FR), sb("a1_lo", [P, KT, ER], FR)
        bh, bl = sb("b1_hi", [P, D], FR), sb("b1_lo", [P, D], FR)
        zbias = sb("z_bias", [P, D])
        pbc = sb("p_scores_b", [P, E])
        gates, tg = sb("gates2", [P, 2]), sb("tanh_gates2", [P, 2])
        pow_n, pow_p = sb("minus_half", [P, 1]), sb("plus_half", [P, 2])
        x2 = [sb(f"x2in_{s}", [P, D]) for s in range(2)]
        c = sb("ctx_stage", [P, D])
        q = sb("ln_out", [P, D])
        ch = [sb(f"c_hi_{s}", [P, D], FR) for s in range(2)]
        cl = [sb(f"c_lo_{s}", [P, D], FR) for s in range(2)]
        qh = [sb(f"q_hi_{s}", [P, D], FR) for s in range(2)]
        ql = [sb(f"q_lo_{s}", [P, D], FR) for s in range(2)]
        vh, vl = sb("v_t_hi", [P, KT, P], FR), sb("v_t_lo", [P, KT, P], FR)
        pr = [sb(f"probs_{s}", [P, D]) for s in range(2)]
        pth = [sb(f"probs_t_hi_{s}", [P, KT, GC], FR) for s in range(2)]
        ptl = [sb(f"probs_t_lo_{s}", [P, KT, GC], FR) for s in range(2)]
        nmx = sb("neg_row_max", [P, TILES])
        rsum = sb("row_sum", [P, TILES])
        rinv = sb("row_inv", [P, TILES])
        x3 = [sb(f"x3_{s}", [P, D]) for s in range(2)]
        z = sb("z", [P, D])
        yh, yl = sb("y_t_hi", [P, KT, P], FR), sb("y_t_lo", [P, KT, P], FR)
        bn = sb("bn2", [P, 2, 6])
        mv2, mv3 = sb("mean_var_x2", [P, 2]), sb("mean_var_x3", [P, 2])
        rs2, rs3 = sb("rstd_x2", [P, 1]), sb("rstd_x3", [P, 1])
        us = sb("u_scaled", [P, ER])
        uth, utl = sb("u_t_hi", [P, P], FR), sb("u_t_lo", [P, P], FR)
        nrm = sb("square_sums", [P, 4])
        nrt = sb("norm_roots", [P, 2])
        gam = sb("gamma", [P, 1])
        m = sb("m", [P, D])

        ps_s = [pb(f"ps_s{s}", D) for s in range(2)]
        ps_t = [pb(f"ps_t{s}", HALF) for s in range(2)]
        ps_o = pb("ps_o", HALF)
        ps_f = pb("ps_f2", HALF)

        const_in, gates_in, small_in = sem("const2_in"), sem("gates2_in"), sem("small2_in")
        x2_in = [sem("x2_in0"), sem("x2_in1")]
        c_in, ct_in = sem("c2_in"), sem("ct2_in")
        stage_in = [sem("stage2_in0"), sem("stage2_in1")]
        stage_hi, stage_lo = sem("stage2_hi"), sem("stage2_lo")
        tanh_done, pow_ready, out_done = sem("tanh2_done"), sem("pow2_ready"), sem("out_done")
        mv2_r, mv3_r, rs2_r, rs3_r = sem("mv2_r"), sem("mv3_r"), sem("rs2_r"), sem("rs3_r")
        q_r, q_hi, q_lo = sem("q2_r"), sem("q2_hi"), sem("q2_lo")
        c_hi, c_lo, v_hi, v_lo = sem("c2_hi"), sem("c2_lo"), sem("v2_hi"), sem("v2_lo")
        s_mm, t_mm, av_mm = sem("s_mm"), sem("t_mm"), sem("av_mm")
        yt_mm, z_mm, u_mm, ut_mm, m_mm = sem("yt2_mm"), sem("z_mm"), sem("u_mm"), sem("ut_mm"), sem("m_mm")
        max_r, exp_r, inv_r, prob_r = sem("max_r"), sem("exp_r"), sem("inv_r"), sem("prob_r")
        t_hi, t_lo, x3_r = sem("t_hi"), sem("t_lo"), sem("x3_r")
        y_r, yt_hi, yt_lo = sem("y2_r"), sem("yt2_hi"), sem("yt2_lo")
        u_r, ut_hi, ut_lo = sem("u_r"), sem("ut_hi"), sem("ut_lo")
        m_sb, sq_m, z_r, sq_z, root_r, zm_r, x4_r = (sem("m_sb"), sem("sq_m"), sem("z_r"), sem("sq_z"),
                                                     sem("root_r"), sem("z_plus_m"), sem("x4_r"))
        dve_q, dve_y, dve_g = sem("dve_q"), sem("dve_y"), sem("dve_g")
        pool_q, pool_y, pool_n = sem("pool_q"), sem("pool_y"), sem("pool_n")

        stage = [m, z]
        SPLITS = [(w_t[k], wh[:, k, :], wl[:, k, :]) for k in range(KT)]
        SPLITS += [(b_t, bh[:, :], bl[:, :]), (a_t, ah[:, :, :].rearrange("p k a -> p (k a)"),
                                               al[:, :, :].rearrange("p k a -> p (k a)"))]
        block = ctx.enter_context(nc.Block())

        def fixed(b, below):
            return isinstance(b, int) and b < below

        def cols(h):
            return slice(h * HALF, (h + 1) * HALF)

        def all_batches(eng, batch):
            batch(0, 0, 0, False, False, True)
            batch(1, 1, 1, True, False, True)
            with eng.Fori(0, (B - 4) // 2) as p:
                for s in (0, 1):
                    batch(p * 2 + (s + 2), s, p + (s + 1), True, True, True)
            batch(B - 2, 0, (B - 1) // 2, True, True, True)
            batch(B - 1, 1, B // 2, True, True, False)

        @block.sync
        def _(sp):
            sp.dma_start(x2[0][:, :], x2_dram[0]).then_inc(x2_in[0], 16)
            sp.dma_start(c[:, :], ctx_in[0]).then_inc(c_in, 16)
            sp.dma_start(gates[:, 0:1], g_x[1:2].partition_broadcast(P)).then_inc(gates_in, 16)
            sp.dma_start(gates[:, 1:2], g_f[1:2].partition_broadcast(P)).then_inc(gates_in, 16)
            sp.dma_start(ident[:, :], consts[:, IDENT, :]).then_inc(const_in, 16)
            sp.dma_start(x2[1][:, :], x2_dram[1]).then_inc(x2_in[1], 16)
            for n in range(2):
                sp.dma_start(stage[n][:, :], SPLITS[n][0]).then_inc(stage_in[n], 16)
            sp.dma_start(zbias[:, :], bias.partition_broadcast(P)).then_inc(small_in, 16)
            sp.dma_start(pbc[:, :], pscores.partition_broadcast(P)).then_inc(small_in, 16)

            def load_ctx_t(b):
                sp.wait_ge(c_lo, b + 1)
                sp.dma_start(c[:, :].rearrange("p (k c) -> p k c", c=P), ctx_t[b]).then_inc(ct_in, 16)

            def load_ctx(b):
                sp.wait_ge(v_lo, b)
                sp.dma_start(c[:, :], ctx_in[b]).then_inc(c_in, 16)

            def load_x2(b, s):
                sp.wait_ge(x3_r, GROUPS * (b - 1))
                sp.dma_start(x2[s][:, :], x2_dram[b]).then_inc(x2_in[s], 16)

            def store(b):
                sp.wait_ge(x4_r, b + 1)
                sp.dma_start(out[b], z[:, :]).then_inc(out_done, 16)

            load_ctx_t(0)
            for n in range(2, len(SPLITS)):
                if n == 3:
                    load_ctx(1)
                if n == 6:
                    load_ctx_t(1)
                sp.wait_ge(stage_hi, n - 1)
                sp.wait_ge(stage_lo, n - 1)
                sp.dma_start(stage[n % 2][:, :], SPLITS[n][0]).then_inc(stage_in[n % 2], 16)

            def batch(b, s, half_next, ffn, fin, more):
                if ffn and more:
                    load_x2(b + 1, 1 - s)
                    load_ctx(b + 1)
                if ffn and more:
                    load_ctx_t(b + 1)
                if fin:
                    store(b - 2)

            all_batches(sp, batch)
            store(B - 2)
            store(B - 1)
            sp.wait_ge(out_done, 16 * B)

        @block.gpsimd
        def _(pool):
            chq, chy, chn = Chain(pool, pool_q, 2), Chain(pool, pool_y, 1), Chain(pool, pool_n, 1)
            nc.gpsimd.memset(pow_n[:, :], -0.5).then_inc(pow_ready, 1)
            nc.gpsimd.memset(pow_p[:, :], 0.5).then_inc(pow_ready, 1)
            pool.wait_ge(pow_ready, 2)

            def rstd_x2(b):
                chq.begin(b)
                pool.wait_ge(mv2_r, b + 1)
                pool.nop(nofuse=True)
                chq.add(nc.gpsimd.tensor_scalar(rs2[:, :], mv2[:, 1:2], LN_EPS, None, ALU.add))
                chq.wait()
                chq.add(nc.gpsimd.tensor_tensor(rs2[:, :], rs2[:, :], pow_n[:, :], ALU.pow))
                chq.wait()
                pool.nop(nofuse=True)
                nc.gpsimd.tensor_scalar(rs2[:, :], rs2[:, :], float(L) ** -0.5, None, ALU.mult).then_inc(rs2_r, 1)
                chq.end()

            def q_low(b, s):
                pool.wait_ge(q_hi, b + 1)
                nc.gpsimd.tensor_tensor(ql[s][:, :], q[:, :], qh[s][:, :].bitcast(FP), ALU.subtract).then_inc(q_lo, 1)

            def c_low(b, s):
                pool.wait_ge(c_hi, b + 1)
                nc.gpsimd.tensor_tensor(cl[s][:, :], c[:, :], ch[s][:, :].bitcast(FP),
                                        ALU.subtract).then_inc(c_lo, 1)

            def v_low(b):
                pool.wait_ge(v_hi, b + 1)
                nc.gpsimd.tensor_tensor(vl[:, :, :], c[:, :].rearrange("p (k c) -> p k c", c=P),
                                        vh[:, :, :].bitcast(FP), ALU.subtract).then_inc(v_lo, 1)

            def normalise(b, n):
                pool.wait_ge(inv_r, TILES * b + n + 1)
                pool.nop(nofuse=True)
                nc.gpsimd.tensor_scalar(pr[n % 2][:, :], pr[n % 2][:, :], rinv[:, n:n + 1], tg[:, 0:1],
                                        ALU.mult, ALU.mult).then_inc(prob_r, 1)

            def rstd_x3(b):
                chy.begin(b)
                pool.wait_ge(mv3_r, b + 1)
                pool.nop(nofuse=True)
                chy.add(nc.gpsimd.tensor_scalar(rs3[:, :], mv3[:, 1:2], LN_EPS, None, ALU.add))
                chy.wait()
                nc.gpsimd.tensor_tensor(rs3[:, :], rs3[:, :], pow_n[:, :], ALU.pow).then_inc(rs3_r, 1)
                chy.end()

            def roots(b):
                chn.begin(b)
                pool.wait_ge(sq_z, 2 * (b + 1))
                pool.wait_ge(sq_m, 2 * (b + 1))
                chn.add(nc.gpsimd.tensor_tensor(nrt[:, :], nrm[:, 0:2], nrm[:, 2:4], ALU.add))
                chn.wait()
                nc.gpsimd.tensor_tensor(nrt[:, :], nrt[:, :], pow_p[:, :], ALU.pow).then_inc(root_r, 1)
                chn.end()

            def batch(b, s, half_next, ffn, fin, more):
                for n in range(TILES - 1):
                    normalise(b, n + 1)
                    if n == 1:
                        v_low(b)
                    if n == 2 and ffn:
                        rstd_x3(b - 1)
                    if n == 2 and fin:
                        roots(b - 2)
                    if n == 3 and more:
                        c_low(b + 1, 1 - s)
                        rstd_x2(b + 1)
                    if n == 4 and more:
                        q_low(b + 1, 1 - s)
                if more:
                    normalise(b + 1, 0)

            rstd_x2(0)
            q_low(0, 0)
            c_low(0, 0)
            pool.wait_ge(tanh_done, 1)
            normalise(0, 0)
            all_batches(pool, batch)
            rstd_x3(B - 1)
            roots(B - 2)
            roots(B - 1)

        @block.scalar
        def _(act):
            def q_high(b, s):
                act.wait_ge(q_r, b + 1)
                if not fixed(b, 2):
                    act.wait_ge(s_mm, TILES * (b - 1))
                nc.scalar.activation(qh[s][:, :], q[:, :], ACT.Copy).then_inc(q_hi, 1)

            def c_high(b, s):
                act.wait_ge(c_in, 16 * (b + 1))
                if not fixed(b, 2):
                    act.wait_ge(s_mm, TILES * (b - 1))
                nc.scalar.activation(ch[s][:, :], c[:, :], ACT.Copy).then_inc(c_hi, 1)

            def v_high(b):
                act.wait_ge(ct_in, 16 * (b + 1))
                if not fixed(b, 1):
                    act.wait_ge(av_mm, GROUPS * b)
                nc.scalar.activation(vh[:, :, :], c[:, :].rearrange("p (k c) -> p k c", c=P),
                                     ACT.Copy).then_inc(v_hi, 1)

            def exps(b, n):
                act.wait_ge(max_r, TILES * b + n + 1)
                if not (fixed(b, 1) and n < 2):
                    act.wait_ge(t_mm, 2 * TILES * b + 2 * (n - 1))
                nc.scalar.activation(pr[n % 2][:, :], ps_s[n % 2][:, :], ACT.Exp, bias=nmx[:, n:n + 1],
                                     accum_out=rsum[:, n:n + 1]).then_inc(exp_r, 1)

            def tile_high(b, n):
                g = n // GT
                for h in range(2):
                    act.wait_ge(t_mm, 2 * (TILES * b + n) + h + 1)
                    if n % GT == 0 and not (fixed(b, 1) and g < 2):
                        act.wait_ge(av_mm, GROUPS * b + g - 1)
                    nc.scalar.activation(pth[g % 2][:, 4 * h:4 * h + 4, (n % GT) * P:(n % GT + 1) * P],
                                         ps_t[h][:, :].rearrange("p (k t) -> p k t", t=P),
                                         ACT.Copy).then_inc(t_hi, 1)

            def y_high(b):
                for h in range(2):
                    act.wait_ge(yt_mm, 2 * b + h + 1)
                    if not fixed(b, 1):
                        act.wait_ge(z_mm, 2 * b)
                    nc.scalar.activation(yh[:, 4 * h:4 * h + 4, :],
                                         ps_t[h][:, :].rearrange("p (k t) -> p k t", t=P),
                                         ACT.Copy).then_inc(yt_hi, 1)

            def u_high(b):
                act.wait_ge(ut_mm, b + 1)
                if not fixed(b, 1):
                    act.wait_ge(m_mm, 2 * b)
                nc.scalar.activation(uth[:, :], ps_f[:, 0:P], ACT.Copy).then_inc(ut_hi, 1)

            def m_out(b, h):
                act.wait_ge(m_mm, 2 * b + h + 1)
                if not fixed(b, 1) and h == 0:
                    act.wait_ge(zm_r, b)
                    act.wait_ge(root_r, b)
                nc.scalar.activation(m[:, cols(h)], ps_f[:, :], ACT.Copy).then_inc(m_sb, 1)
                act.wait_ge(m_sb, 2 * b + h + 1)
                nc.scalar.activation(ps_f[:, :], ps_f[:, :], ACT.Square,
                                     accum_out=nrm[:, 2 * h + 1:2 * h + 2]).then_inc(sq_m, 1)

            def z_squares(b, h):
                act.wait_ge(z_r, 2 * b + h + 1)
                nc.scalar.activation(ps_f[:, :], z[:, cols(h)], ACT.Square,
                                     accum_out=nrm[:, 2 * h:2 * h + 1]).then_inc(sq_z, 1)

            def split(n):
                act.wait_ge(stage_in[n % 2], 16 * (n // 2 + 1))
                nc.scalar.activation(SPLITS[n][1], stage[n % 2][:, :], ACT.Copy).then_inc(stage_hi, 1)

            def batch(b, s, half_next, ffn, fin, more):
                for n in range(TILES):
                    if n == 0 and fin:
                        z_squares(b - 2, 0)
                    tile_high(b, n)
                    if n == 5 and ffn:
                        m_out(b - 1, 0)
                    if n < TILES - 2:
                        exps(b, n + 2)
                    elif more:
                        exps(b + 1, n + 2 - TILES)
                    if n == 2 and fin:
                        z_squares(b - 2, 1)
                    if n == 1:
                        v_high(b)
                    if n == 3 and ffn:
                        y_high(b - 1)
                    if n == 3 and more:
                        c_high(b + 1, 1 - s)
                    if n == 4 and ffn:
                        u_high(b - 1)
                    if n == 4 and more:
                        q_high(b + 1, 1 - s)
                    if n == 5 and ffn:
                        m_out(b - 1, 1)
                    if not ffn:
                        for m in range(n, n + 1 if n < TILES - 1 else len(SPLITS)):
                            split(m)

            act.wait_ge(gates_in, 32)
            nc.scalar.activation(tg[:, :], gates[:, :], ACT.Tanh).then_inc(tanh_done, 1)
            q_high(0, 0)
            c_high(0, 0)
            exps(0, 0)
            exps(0, 1)
            all_batches(act, batch)
            z_squares(B - 2, 0)
            z_squares(B - 2, 1)
            y_high(B - 1)
            u_high(B - 1)
            m_out(B - 1, 0)
            m_out(B - 1, 1)
            z_squares(B - 1, 0)
            z_squares(B - 1, 1)

        @block.vector
        def _(dve):
            chq, chy, chg = Chain(dve, dve_q, 2), Chain(dve, dve_y, 2), Chain(dve, dve_g, 4)

            def stats(src, mv, ready, ch):
                for h in range(2):
                    ch.add(nc.vector.bn_stats(bn[:, h, :], src[:, cols(h)]))
                ch.wait()
                dve.nop(nofuse=True)
                nc.vector.bn_aggr(mv[:, :], bn[:, :, :]).then_inc(ready, 1)

            def x2_stats(b, s, half):
                chq.begin(b)
                dve.wait_ge(x2_in[s], 16 * (half + 1))
                stats(x2[s], mv2, mv2_r, chq)
                chq.end()

            def ln_x2(b, s):
                dve.wait_ge(rs2_r, b + 1)
                if not fixed(b, 2):
                    dve.wait_ge(yt_mm, 2 * (b - 1))
                nc.vector.tensor_scalar(q[:, :], x2[s][:, :], mv2[:, 0:1], rs2[:, 0:1],
                                        ALU.subtract, ALU.mult).then_inc(q_r, 1)

            def x3_stats(b, s):
                chy.begin(b)
                dve.wait_ge(x3_r, GROUPS * (b + 1))
                stats(x3[s], mv3, mv3_r, chy)
                chy.end()

            def ln_x3(b, s, last):
                dve.wait_ge(rs3_r, b + 1)
                dve.wait_ge(q_lo, b + 1 if last else b + 2)
                nc.vector.tensor_scalar(q[:, :], x3[s][:, :], mv3[:, 0:1], rs3[:, 0:1],
                                        ALU.subtract, ALU.mult).then_inc(y_r, 1)

            def row_max(b, n):
                dve.wait_ge(s_mm, TILES * b + n + 1)
                if not fixed(b, 1):
                    dve.wait_ge(exp_r, TILES * (b - 1) + n + 1)
                nc.vector.tensor_reduce(nmx[:, n:n + 1], ps_s[n % 2][:, :], AX.X, ALU.max,
                                        negate=True).then_inc(max_r, 1)

            def inverse_sum(b, n):
                dve.wait_ge(exp_r, TILES * b + n + 1)
                if not fixed(b, 1):
                    dve.wait_ge(prob_r, TILES * (b - 1) + n + 1)
                nc.vector.reciprocal(rinv[:, n:n + 1], rsum[:, n:n + 1]).then_inc(inv_r, 1)

            def tile_low(b, n):
                g = n // GT
                for h in range(2):
                    dve.wait_ge(t_hi, 2 * (TILES * b + n) + h + 1)
                    part = (slice(None), slice(4 * h, 4 * h + 4), slice((n % GT) * P, (n % GT + 1) * P))
                    nc.vector.tensor_tensor(ptl[g % 2][part], ps_t[h][:, :].rearrange("p (k t) -> p k t", t=P),
                                            pth[g % 2][part].bitcast(FP), ALU.subtract).then_inc(t_lo, 1)

            def residual(b, s, g):
                dve.wait_ge(av_mm, GROUPS * b + g + 1)
                if g == 0 and not fixed(b, 2):
                    dve.wait_ge(x4_r, b - 1)
                part = slice(g * GC, (g + 1) * GC)
                nc.vector.tensor_tensor(x3[s][:, part], ps_o[:, 0:GC], x2[s][:, part], ALU.add).then_inc(x3_r, 1)

            def y_low(b):
                for h in range(2):
                    dve.wait_ge(yt_hi, 2 * b + h + 1)
                    nc.vector.tensor_tensor(yl[:, 4 * h:4 * h + 4, :],
                                            ps_t[h][:, :].rearrange("p (k t) -> p k t", t=P),
                                            yh[:, 4 * h:4 * h + 4, :].bitcast(FP), ALU.subtract).then_inc(yt_lo, 1)

            def add_bias(b, h):
                dve.wait_ge(z_mm, 2 * b + h + 1)
                if not fixed(b, 1) and h == 0:
                    dve.wait_ge(out_done, 16 * b)
                nc.vector.tensor_tensor(z[:, cols(h)], ps_f[:, :], zbias[:, cols(h)], ALU.add).then_inc(z_r, 1)

            def scale_u(b):
                dve.wait_ge(u_mm, b + 1)
                nc.vector.tensor_tensor(us[:, :].rearrange("p (e r) -> p e r", r=R),
                                        ps_f[:, 0:ER].rearrange("p (e r) -> p e r", r=R),
                                        pbc[:, :].unsqueeze(2).to_broadcast([P, E, R]), ALU.mult).then_inc(u_r, 1)

            def u_low(b):
                dve.wait_ge(ut_hi, b + 1)
                nc.vector.tensor_tensor(utl[:, :], ps_f[:, 0:P], uth[:, :].bitcast(FP),
                                        ALU.subtract).then_inc(ut_lo, 1)

            def clamp_m(b):
                chg.begin(b)
                dve.wait_ge(root_r, b + 1)
                chg.add(nc.vector.tensor_scalar(gam[:, :], nrt[:, 1:2], EPS, None, ALU.add))
                chg.wait()
                chg.add(nc.vector.reciprocal(gam[:, :], gam[:, :]))
                chg.wait()
                chg.add(nc.vector.tensor_scalar(gam[:, :], gam[:, :], nrt[:, 0:1], C_CLAMP, ALU.mult, ALU.mult))
                chg.wait()
                chg.add(nc.vector.tensor_scalar(gam[:, :], gam[:, :], 1.0, None, ALU.min))
                chg.wait()
                chg.end()
                nc.vector.scalar_tensor_tensor(z[:, :], m[:, :], gam[:, 0:1], z[:, :],
                                               ALU.mult, ALU.add).then_inc(zm_r, 1)

            def finish(b, s):
                dve.wait_ge(zm_r, b + 1)
                nc.vector.scalar_tensor_tensor(z[:, :], z[:, :], tg[:, 1:2], x3[s][:, :],
                                               ALU.mult, ALU.add).then_inc(x4_r, 1)

            def split(n):
                dve.wait_ge(stage_hi, n + 1)
                nc.vector.tensor_tensor(SPLITS[n][2], stage[n % 2][:, :], SPLITS[n][1].bitcast(FP),
                                        ALU.subtract).then_inc(stage_lo, 1)

            def batch(b, s, half_next, ffn, fin, more):
                for n in range(TILES):
                    if n == 0 and fin:
                        add_bias(b - 2, 0)
                    if n == 2 and fin:
                        add_bias(b - 2, 1)
                    if n == 4 and fin:
                        finish(b - 2, s)
                    if n in (4, 6):
                        residual(b, s, n // 2 - 2)
                    if n == 0 and ffn:
                        residual(b - 1, 1 - s, 2)
                    if n < TILES - 1:
                        inverse_sum(b, n + 1)
                    elif more:
                        inverse_sum(b + 1, 0)
                    if n < TILES - 2:
                        row_max(b, n + 2)
                    elif more:
                        row_max(b + 1, n + 2 - TILES)
                    tile_low(b, n)
                    if n == 1 and ffn:
                        residual(b - 1, 1 - s, 3)
                        x3_stats(b - 1, 1 - s)
                    if n == 2 and ffn:
                        ln_x3(b - 1, 1 - s, False)
                    if n == 3 and fin:
                        clamp_m(b - 2)
                    if n == 3 and ffn:
                        y_low(b - 1)
                    if n == 4 and more:
                        x2_stats(b + 1, 1 - s, half_next)
                    if n == 4 and ffn:
                        scale_u(b - 1)
                    if n == 4 and more:
                        ln_x2(b + 1, 1 - s)
                    if n == 4 and ffn:
                        u_low(b - 1)
                    if not ffn:
                        for m in range(n, n + 1 if n < TILES - 1 else len(SPLITS)):
                            split(m)

            x2_stats(0, 0, 0)
            ln_x2(0, 0)
            row_max(0, 0)
            row_max(0, 1)
            inverse_sum(0, 0)
            dve.wait_ge(tanh_done, 1)
            dve.wait_ge(small_in, 32)
            all_batches(dve, batch)
            add_bias(B - 2, 0)
            residual(B - 1, 1, 2)
            residual(B - 1, 1, 3)
            add_bias(B - 2, 1)
            x3_stats(B - 1, 1)
            ln_x3(B - 1, 1, True)
            y_low(B - 1)
            clamp_m(B - 2)
            finish(B - 2, 0)
            scale_u(B - 1)
            u_low(B - 1)
            add_bias(B - 1, 0)
            add_bias(B - 1, 1)
            clamp_m(B - 1)
            finish(B - 1, 1)

        @block.tensor
        def _(pe):
            def scores(b, s, n):
                if n == 0:
                    pe.wait_ge(q_lo, b + 1)
                    pe.wait_ge(c_lo, b + 1)
                if not (fixed(b, 1) and n < 2):
                    pe.wait_ge(exp_r, TILES * b + n - 1)
                blk = slice(n * P, (n + 1) * P)
                for h in range(2):
                    ins = exact3(nc, ps_s[n % 2][:, cols(h)], (ch[s][:, blk], cl[s][:, blk]),
                                 (qh[s][:, cols(h)], ql[s][:, cols(h)]), True, True)
                ins.then_inc(s_mm, 1)

            def transposes(b, n, behind_y):
                pe.wait_ge(prob_r, TILES * b + n + 1)
                for h in range(2):
                    if behind_y:
                        pe.wait_ge(yt_lo, 2 * (b - 1) + h + 1)
                    elif not (fixed(b, 1) and n == 0):
                        pe.wait_ge(t_lo, 2 * (TILES * b + n) + h - 1)
                    for k in range(4):
                        src = pr[n % 2][:, (4 * h + k) * P:(4 * h + k + 1) * P]
                        ins = nc.tensor.transpose(ps_t[h][:, k * P:(k + 1) * P], src, ident[:, :])
                    ins.then_inc(t_mm, 1)

            def values(b, g, part):
                if part == 0:
                    pe.wait_ge(v_lo, b + 1)
                    pe.wait_ge(t_lo, 2 * (TILES * b + GT * (g + 1)))
                    if not (fixed(b, 1) and g == 0):
                        pe.wait_ge(x3_r, GROUPS * b + g)
                for k in range(4 * part, 4 * part + 4):
                    ins = exact3(nc, ps_o[:, 0:GC], (vh[:, k, :], vl[:, k, :]),
                                 (pth[g % 2][:, k, :], ptl[g % 2][:, k, :]), k == 0, k == KT - 1)
                if part == 1:
                    ins.then_inc(av_mm, 1)

            def transposes_y(b, tiles_before):
                pe.wait_ge(y_r, b + 1)
                for h in range(2):
                    pe.wait_ge(t_lo, 2 * tiles_before + h - 1)
                    for k in range(4):
                        ins = nc.tensor.transpose(ps_t[h][:, k * P:(k + 1) * P],
                                                  q[:, (4 * h + k) * P:(4 * h + k + 1) * P], ident[:, :])
                    ins.then_inc(yt_mm, 1)

            def u_product(b):
                pe.wait_ge(yt_lo, 2 * (b + 1))
                pe.wait_ge(stage_lo, len(SPLITS))
                if not fixed(b, 1):
                    pe.wait_ge(sq_z, 2 * b)
                for k in range(KT):
                    ins = exact3(nc, ps_f[:, 0:ER], (yh[:, k, :], yl[:, k, :]), (ah[:, k, :], al[:, k, :]),
                                 k == 0, k == KT - 1)
                ins.then_inc(u_mm, 1)

            def transpose_u(b):
                pe.wait_ge(u_r, b + 1)
                nc.tensor.transpose(ps_f[:, 0:P], us[:, :], ident[:, :]).then_inc(ut_mm, 1)

            def m_product(b, h):
                if h == 0:
                    pe.wait_ge(ut_lo, b + 1)
                else:
                    pe.wait_ge(sq_m, 2 * b + 1)
                exact3(nc, ps_f[:, :], (uth[:, :], utl[:, :]), (bh[:, cols(h)], bl[:, cols(h)]),
                       True, True).then_inc(m_mm, 1)

            def z_product(b, h, ks):
                if ks[0] == 0:
                    if h == 0:
                        pe.wait_ge(sq_m, 2 * b + 2)
                    else:
                        pe.wait_ge(sq_z, 2 * b + 1)
                for k in ks:
                    ins = exact3(nc, ps_f[:, :], (yh[:, k, :], yl[:, k, :]),
                                 (wh[:, k, cols(h)], wl[:, k, cols(h)]), k == 0, k == KT - 1)
                if ks[-1] == KT - 1:
                    ins.then_inc(z_mm, 1)

            def batch(b, s, half_next, ffn, fin, more):
                for n in range(TILES):
                    if n < TILES - 2:
                        scores(b, s, n + 2)
                    elif more:
                        scores(b + 1, 1 - s, n + 2 - TILES)
                    transposes(b, n, ffn and n == 4)
                    if ffn and n == 3:
                        transposes_y(b - 1, TILES * b + 4)
                    if ffn and n == 4:
                        u_product(b - 1)
                    if ffn and n == 5:
                        m_product(b - 1, 0)
                    if fin and n < 2:
                        z_product(b - 2, 1, range(4 * n, 4 * n + 4))
                    if ffn and n >= 6:
                        z_product(b - 1, 0, range(4 * n - 24, 4 * n - 20))
                    if n < 2:
                        if ffn:
                            values(b - 1, GROUPS - 1, n)
                    else:
                        values(b, (n - 2) // 2, n % 2)
                    if ffn and n == 4:
                        transpose_u(b - 1)
                    if ffn and n == 5:
                        m_product(b - 1, 1)

            pe.wait_ge(const_in, 16)
            scores(0, 0, 0)
            scores(0, 0, 1)
            all_batches(pe, batch)
            values(B - 1, GROUPS - 1, 0)
            values(B - 1, GROUPS - 1, 1)
            z_product(B - 2, 1, range(KT))
            transposes_y(B - 1, TILES * B)
            u_product(B - 1)
            transpose_u(B - 1)
            m_product(B - 1, 0)
            m_product(B - 1, 1)
            z_product(B - 1, 0, range(KT))
            z_product(B - 1, 1, range(KT))


def build(nc, t):
    x2_dram = nc.dram_tensor("x2_dram", [B, L, D], FP, kind="Internal").ap()
    correlation_and_routed_ffn(nc, t["x"], t["ctx"], t["g_xattn"], t["g_ffn"],
                               t["w0"].rearrange("(k p) o -> k p o", p=P), t["b0"],
                               t["ar0"].rearrange("(k p) a -> p k a", p=P), t["rb0"], t["B0"], t["emap"],
                               t["consts"], x2_dram)
    attention_and_clamped_ffn(nc, t["ctx"], t["ctx_t"].rearrange("b (k p) c -> b p k c", p=P), t["g_xattn"],
                              t["g_ffn"], t["w1"].rearrange("(k p) o -> k p o", p=P), t["b1"], t["A1"],
                              t["B1"], t["p_scores"], t["consts"], x2_dram, t["out"])


def kernel(x, ctx_4096, g_xattn, g_ffn, L0_ffn_base_W, L0_ffn_base_b, L0_ffn_router_W, L0_ffn_router_b, L0_ffn_A,
           L0_ffn_B, L0_ffn_expert_map, L1_ffn_W, L1_ffn_b, L1_ffn_A, L1_ffn_B, L1_ffn_p_scores):
    import concourse.bacc as _bacc
    from concourse.bass_utils import run_bass_kernel_spmd as _run

    a0 = np.asarray(L0_ffn_A).reshape(ER, D).T
    pad = np.zeros((D, 1), np.float32)
    a1 = np.asarray(L1_ffn_A).transpose(1, 0, 2).reshape(KT, P, ER)
    lay = {
        "x": x, "ctx": ctx_4096, "ctx_t": np.asarray(ctx_4096).transpose(0, 2, 1),
        "g_xattn": g_xattn, "g_ffn": g_ffn,
        "w0": np.asarray(L0_ffn_base_W).T, "b0": L0_ffn_base_b,
        "ar0": np.concatenate([a0, np.asarray(L0_ffn_router_W).T, pad], axis=1), "rb0": L0_ffn_router_b,
        "B0": np.asarray(L0_ffn_B).transpose(0, 2, 1).reshape(ER, D), "emap": L0_ffn_expert_map,
        "w1": np.asarray(L1_ffn_W).T, "b1": L1_ffn_b,
        "A1": a1.transpose(1, 0, 2).reshape(P, KT * ER), "B1": np.asarray(L1_ffn_B).reshape(ER, D),
        "p_scores": L1_ffn_p_scores, "consts": constants(),
    }
    nc = _bacc.Bacc("TRN2", target_bir_lowering=False, num_devices=1)
    arrays, t = {}, {}
    for name, a in lay.items():
        a = np.ascontiguousarray(a)
        arrays[f"in_{name}"] = a
        t[name] = nc.dram_tensor(f"in_{name}", a.shape, mybir.dt.from_np(a.dtype), kind="ExternalInput").ap()
    t["out"] = nc.dram_tensor("out_0", (B, L, D), FP, kind="ExternalOutput").ap()
    build(nc, t)
    r = _run(nc, [arrays], core_ids=[0])
    return r.results[0]["out_0"]
```

```python
import numpy as np
import concourse.bass as bass
from concourse import mybir
from contextlib import ExitStack

FP = mybir.dt.float32
FR = mybir.dt.float32r
ALU = mybir.AluOpType
ACT = mybir.ActivationFunctionType
AX = mybir.AxisListType

B, L, D = 16, 128, 1024
P = 128
KT = D // P
HALF = 512
E, R = 8, 16
ER = E * R
NR = 2 * E - 1
AR = ER + NR + 1
TOPK = int(2 * np.log(L))
assert TOPK == 9
LN_EPS, EPS, C_CLAMP, LORA_SCALE = 1e-5, 1e-6, 0.5, 2.0
NEG, NEG_TEST = -3.0e38, -1.0e38

(F_CYC, F_CYC_V, F_NEG, F_NEG_V, I_CORR_A, I_CORR_B, I_CYC_A, I_CYC_B, I_NEG_A, I_NEG_B,
 IDENT, N_CONST) = range(12)


def constants():
    l = np.arange(L)
    f = np.arange(L // 2)
    cyc = 2 * np.pi * np.outer(f, l) / L
    neg = 2 * np.pi * np.outer(f + 0.5, l) / L
    fc = np.concatenate([np.cos(cyc), np.sin(cyc)])
    fc[L // 2] = np.cos(np.pi * l)
    fn = np.concatenate([np.cos(neg), np.sin(neg)])
    less_last = np.eye(L)
    less_last[:, L - 1] -= 1.0
    ca = 2.0 / L * np.concatenate([np.cos(cyc), np.cos(cyc)])
    ca[0] = 1.0 / L
    ca[L // 2] = np.cos(np.pi * l) / L
    cb = 2.0 / L * np.concatenate([-np.sin(cyc), np.sin(cyc)])
    cb[0] = cb[L // 2] = 0.0
    na = 2.0 / L * np.concatenate([np.cos(neg), np.cos(neg)])
    nb = 2.0 / L * np.concatenate([-np.sin(neg), np.sin(neg)])
    fc_v = fc @ less_last
    fc_v[0, L - 1] += 2 * L
    mats = [fc.T, fc_v.T, fn.T, (fn @ less_last).T, ca, cb, ca / 2, -cb / 2, na / 2, -nb / 2, np.eye(L)]
    return np.ascontiguousarray(np.stack(mats, axis=1), dtype=np.float32)


class Chain:

    def __init__(self, eng, sem, per):
        self.eng, self.sem, self.per = eng, sem, per

    def begin(self, b):
        self.base, self.n = b * self.per, 0

    def add(self, ins):
        self.n += 1
        ins.then_inc(self.sem, 1)

    def wait(self):
        self.eng.wait_ge(self.sem, self.base + self.n)

    def end(self):
        assert self.n == self.per, (self.n, self.per)


def exact3(nc, out, stat, mov, start, stop):
    nc.tensor.matmul(out, stat[1], mov[0], start=start, stop=False)
    nc.tensor.matmul(out, stat[0], mov[1], start=False, stop=False)
    return nc.tensor.matmul(out, stat[0], mov[0], start=False, stop=stop)


def correlation_and_routed_ffn(nc, x, ctx_in, g_x, g_f, w_t, bias, ar_t, rb, b_t, emap, consts, x2_dram):
    ctx = ExitStack()
    with ctx:
        def sb(name, shape, dt=FP):
            return ctx.enter_context(nc.sbuf_tensor(name, shape, dt))

        def pb(name, cols):
            return ctx.enter_context(nc.psum_tensor(name, [P, cols], FP))

        def sem(name):
            return ctx.enter_context(nc.semaphore(name))

        cst = sb("cst", [P, N_CONST, P])
        xs = [sb(f"x_{s}", [P, D]) for s in range(2)]
        fh, fl = sb("f_hi", [P, I_CORR_A, P], FR), sb("f_lo", [P, I_CORR_A, P], FR)
        c = sb("ctx", [P, D])
        ch, cl = sb("ctx_hi", [P, D], FR), sb("ctx_lo", [P, D], FR)
        wh, wl = sb("w_hi", [P, KT, D], FR), sb("w_lo", [P, KT, D], FR)
        arh, arl = sb("ar_hi", [P, KT, AR], FR), sb("ar_lo", [P, KT, AR], FR)
        bh, bl = sb("b_hi", [P, D], FR), sb("b_lo", [P, D], FR)
        gbias = sb("gbias", [P, D])
        rbb = sb("router_bias", [P, NR])
        mapi = sb("expert_map", [P, NR], mybir.dt.int32)
        mapf = sb("expert_map_f", [P, NR])
        onehot = sb("onehot", [P, E, NR])
        gates = sb("gates", [P, 2])
        tg = sb("tanh_gates", [P, 2])
        pows = sb("pows", [P, 1])
        ln = sb("ln", [P, D])
        qh, ql = sb("q_hi", [P, D], FR), sb("q_lo", [P, D], FR)
        kc, kcs = sb("k_cyc", [P, D]), sb("k_cyc_swapped", [P, D])
        kn, kns = sb("k_neg", [P, D]), sb("k_neg_swapped", [P, D])
        pa, pbm = sb("prod_a", [P, D]), sb("prod_b", [P, D])
        pc, pd = sb("prod_c", [P, D]), sb("prod_d", [P, D])
        c1, c2 = sb("corr_less_8", [P, D]), sb("corr_less_9", [P, D])
        ew = sb("exp_w", [P, D])
        wm = sb("w_mask", [P, D])
        wth, wtl = sb("w_time_hi", [P, D], FR), sb("w_time_lo", [P, D], FR)
        mx = sb("top8", [P, KT, 8])
        mx9 = sb("next8", [P, KT, 8])
        nmx = sb("neg_max", [P, KT])
        md = sb("top_less_max", [P, KT, TOPK])
        me = sb("top_exp", [P, KT, TOPK])
        ms = sb("top_sum", [P, KT])
        x1 = [sb(f"x1_{s}", [P, D]) for s in range(2)]
        x2 = sb("x2", [P, D])
        yh, yl = sb("ln_x1_t_hi", [P, KT, P], FR), sb("ln_x1_t_lo", [P, KT, P], FR)
        bn0, bn1 = sb("bn_x", [P, 2, 6]), sb("bn_x1", [P, 2, 6])
        mv0, mv1 = sb("mean_var_x", [P, 2]), sb("mean_var_x1", [P, 2])
        rs0, rs1 = sb("rstd_x", [P, 1]), sb("rstd_x1", [P, 1])
        lg, lg2 = sb("logits", [P, NR]), sb("logits_less_8", [P, NR])
        lm = sb("logits_top8", [P, 8])
        nlm = sb("neg_logit_max", [P, 1])
        pe_, psum_ = sb("p_exp", [P, NR]), sb("p_sum", [P, 1])
        pinv = sb("p_inv", [P, 1])
        pm = sb("p_kept", [P, NR])
        poh = sb("p_onehot", [P, E, NR])
        ewt = sb("expert_w", [P, E])
        hw = sb("h_w", [P, ER])
        hth, htl = sb("h_t_hi", [P, P], FR), sb("h_t_lo", [P, P], FR)

        ps_f = pb("ps_ffn", D)
        ps_h = pb("ps_h", HALF)
        ps_c = [pb(f"ps_c{s}", D) for s in range(2)]
        ps_t = pb("ps_t", HALF)

        consts_in, gates_in, small_in, gbias_in = sem("consts_in"), sem("gates_in"), sem("small_in"), sem("gbias_in")
        x_in, c_in = [sem("x_in0"), sem("x_in1")], sem("c_in")
        f_hi, f_lo, c_hi, c_lo = sem("f_hi"), sem("f_lo"), sem("c_hi"), sem("c_lo")
        q_hi, q_lo, wt_hi, wt_lo = sem("q_hi"), sem("q_lo"), sem("wt_hi"), sem("wt_lo")
        stage_in = [sem(f"stage_in{n}") for n in range(KT + 3)]
        stage_hi, stage_lo = sem("stage_hi"), sem("stage_lo")
        swap_c, swap_n = sem("swap_c"), sem("swap_n")
        x2_out = sem("x2_out")
        setup_dve, tanh_done, pow_ready, gb_ready = sem("setup_dve"), sem("tanh_done"), sem("pow_ready"), sem("gb_ready")
        kc_mm, kn_mm, q_mm, corr_mm, wt_mm = sem("kc_mm"), sem("kn_mm"), sem("q_mm"), sem("corr_mm"), sem("wt_mm")
        wc_mm, wn_mm, out_mm = sem("wc_mm"), sem("wn_mm"), sem("out_mm")
        yt_mm, ar_mm, main_mm, ht_mm, lora_mm = sem("yt_mm"), sem("ar_mm"), sem("main_mm"), sem("ht_mm"), sem("lora_mm")
        kc_sb, kn_sb, e_done, te_done = sem("kc_sb"), sem("kn_sb"), sem("e_done"), sem("te_done")
        yt_hi, yt_lo, pexp, ht_hi, ht_lo = sem("yt_hi"), sem("yt_lo"), sem("pexp"), sem("ht_hi"), sem("ht_lo")
        q_ready, prod_ab, mx_ready, nd_ready = sem("q_ready"), sem("prod_ab"), sem("mx_ready"), sem("nd_ready")
        corr_read, ms_ready, scaled = sem("corr_read"), sem("ms_ready"), sem("scaled")
        wc_prod, wn_prod, x1_ready, y_ready = sem("wc_prod"), sem("wn_prod"), sem("x1_ready"), sem("y_ready")
        mv0_ready, mv1_ready, rs0_ready, rs1_ready = sem("mv0_ready"), sem("mv1_ready"), sem("rs0_ready"), sem("rs1_ready")
        w_ready, x1b_ready = sem("w_ready"), sem("x1b_ready")
        lm_ready, hw_ready, x2_ready = sem("lm_ready"), sem("hw_ready"), sem("x2_ready")
        dve_x, dve_y, dve_t, dve_r = sem("dve_x"), sem("dve_y1"), sem("dve_t"), sem("dve_r")
        pool_x, pool_y = sem("pool_x"), sem("pool_y1")

        SPLITS = [(w_t[k], D, wh[:, k, :], wl[:, k, :]) for k in range(KT)]
        SPLITS += [(b_t, D, bh[:, :], bl[:, :])]
        SPLITS += [(ar_t[:, 0:KT // 2, :], KT // 2 * AR, arh[:, 0:KT // 2, :], arl[:, 0:KT // 2, :]),
                   (ar_t[:, KT // 2:KT, :], KT // 2 * AR, arh[:, KT // 2:KT, :], arl[:, KT // 2:KT, :])]

        SPLITS_AT = (3, 6)
        STAGES = [ew, wm, pa, pbm, pc, pd, x1[1], x1[0], x2, ew, wm]

        def staged(n):
            cols = SPLITS[n][1]
            v = STAGES[n][:, 0:cols]
            return v if cols == D else v.rearrange("p (k a) -> p k a", a=AR)

        block = ctx.enter_context(nc.Block())

        def fixed(b, below):
            return isinstance(b, int) and b < below

        def has_next(b):
            return not (isinstance(b, int) and b == B - 1)

        def cols(h):
            return slice(h * HALF, (h + 1) * HALF)

        def blocks(h):
            return range(h * KT // 2, (h + 1) * KT // 2)

        def blk(g):
            return slice(g * P, (g + 1) * P)

        def batches(eng, first, body, last):
            first()
            with eng.Fori(0, (B - 2) // 2) as p:
                for s in (1, 2):
                    body(p * 2 + s, s % 2, p + 1)
            body(B - 1, (B - 1) % 2, B // 2)
            last()

        @block.sync
        def _(sp):
            sp.dma_start(c[:, :], ctx_in[0]).then_inc(c_in, 16)
            sp.dma_start(xs[0][:, :], x[0]).then_inc(x_in[0], 16)
            sp.dma_start(cst[:, :, :], consts).then_inc(consts_in, 16)
            sp.dma_start(gates[:, 0:1], g_x[0:1].partition_broadcast(P)).then_inc(gates_in, 16)
            sp.dma_start(gates[:, 1:2], g_f[0:1].partition_broadcast(P)).then_inc(gates_in, 16)
            sp.dma_start(rbb[:, :], rb.partition_broadcast(P)).then_inc(small_in, 16)
            sp.dma_start(mapi[:, :], emap.partition_broadcast(P)).then_inc(small_in, 16)

            def load_stages(parts):
                for n in parts:
                    if n == 9:
                        sp.wait_ge(w_ready, 2)
                    if n == 10:
                        sp.wait_ge(wt_mm, 2)
                    sp.dma_start(staged(n), SPLITS[n][0]).then_inc(stage_in[n], 16)

            load_stages(range(0, 3))
            sp.dma_start(gbias[:, :], bias.partition_broadcast(P)).then_inc(gbias_in, 16)

            def swap_cyc(b):
                sp.wait_ge(kc_sb, b + 1)
                sp.dma_start(kcs[0:P // 2, :], kc[P // 2:P, :]).then_inc(swap_c, 16)
                sp.dma_start(kcs[P // 2:P, :], kc[0:P // 2, :]).then_inc(swap_c, 16)

            def swap_neg(b):
                sp.wait_ge(kn_sb, b + 1)
                sp.dma_start(kns[0:P // 2, :], kn[P // 2:P, :]).then_inc(swap_n, 16)
                sp.dma_start(kns[P // 2:P, :], kn[0:P // 2, :]).then_inc(swap_n, 16)

            def load_ctx(b):
                sp.wait_ge(c_lo, b)
                sp.dma_start(c[:, :], ctx_in[b]).then_inc(c_in, 16)

            def load_x(b, s):
                sp.wait_ge(x1_ready, 2 * (b - 1))
                sp.dma_start(xs[s][:, :], x[b]).then_inc(x_in[s], 16)

            def store(b):
                sp.wait_ge(x2_ready, b + 1)
                sp.dma_start(x2_dram[b], x2[:, :]).then_inc(x2_out, 16)

            swap_cyc(0)
            swap_neg(0)
            load_stages(range(3, 7))
            load_ctx(1)
            sp.dma_start(xs[1][:, :], x[1]).then_inc(x_in[1], 16)
            load_stages(range(7, len(SPLITS)))
            load_ctx(2)
            swap_cyc(1)
            load_x(2, 0)
            with sp.Fori(0, (B - 4) // 2) as p:
                for s in (1, 2):
                    b = p * 2 + s
                    swap_neg(b)
                    load_ctx(b + 2)
                    store(b - 1)
                    swap_cyc(b + 1)
                    load_x(b + 2, s % 2)
            swap_neg(B - 3)
            load_ctx(B - 1)
            store(B - 4)
            swap_cyc(B - 2)
            load_x(B - 1, 1)
            swap_neg(B - 2)
            store(B - 3)
            swap_cyc(B - 1)
            swap_neg(B - 1)
            store(B - 2)
            store(B - 1)
            sp.wait_ge(x2_out, 16 * B)

        @block.gpsimd
        def _(pool):
            chx, chy = Chain(pool, pool_x, 1), Chain(pool, pool_y, 1)
            nc.gpsimd.memset(pows[:, :], -0.5).then_inc(pow_ready, 1)

            def rstd(mv, rs, made, ready, ch, b):
                ch.begin(b)
                pool.wait_ge(made, b + 1)
                pool.nop(nofuse=True)
                ch.add(nc.gpsimd.tensor_scalar(rs[:, :], mv[:, 1:2], LN_EPS, None, ALU.add))
                ch.wait()
                nc.gpsimd.tensor_tensor(rs[:, :], rs[:, :], pows[:, :], ALU.pow).then_inc(ready, 1)
                ch.end()

            def x1_bias(b, s):
                if fixed(b, 1):
                    pool.wait_ge(gb_ready, 1)
                else:
                    pool.wait_ge(x2_out, 16 * b)
                nc.gpsimd.tensor_tensor(x2[:, :], x1[s][:, :], gbias[:, :], ALU.add).then_inc(x1b_ready, 1)

            def c_low(b):
                pool.wait_ge(c_hi, b + 1)
                nc.gpsimd.tensor_tensor(cl[:, :], c[:, :], ch[:, :].bitcast(FP), ALU.subtract).then_inc(c_lo, 1)

            def q_low(b):
                pool.wait_ge(q_hi, b + 1)
                nc.gpsimd.tensor_tensor(ql[:, :], ln[:, :], qh[:, :].bitcast(FP), ALU.subtract).then_inc(q_lo, 1)

            def first():
                pool.wait_ge(pow_ready, 1)
                c_low(0)
                rstd(mv0, rs0, mv0_ready, rs0_ready, chx, 0)
                q_low(0)
                c_low(1)
                rstd(mv0, rs0, mv0_ready, rs0_ready, chx, 1)
                q_low(1)

            def ffn(b, s):
                rstd(mv1, rs1, mv1_ready, rs1_ready, chy, b)
                x1_bias(b, s)

            def body(b, s, half_next):
                ffn(b - 1, 1 - s)
                if has_next(b):
                    c_low(b + 1)
                    rstd(mv0, rs0, mv0_ready, rs0_ready, chx, b + 1)
                    q_low(b + 1)

            batches(pool, first, body, lambda: ffn(B - 1, (B - 1) % 2))

        @block.scalar
        def _(act):
            def split_weights(part):
                for n in range(*part):
                    act.wait_ge(stage_in[n], 16)
                    nc.scalar.activation(SPLITS[n][2], staged(n), ACT.Copy).then_inc(stage_hi, 1)

            def c_high(b):
                act.wait_ge(c_in, 16 * (b + 1))
                if not fixed(b, 1):
                    act.wait_ge(kn_mm, b)
                nc.scalar.activation(ch[:, :], c[:, :], ACT.Copy).then_inc(c_hi, 1)

            def q_high(b):
                act.wait_ge(q_ready, b + 1)
                if not fixed(b, 1):
                    act.wait_ge(q_mm, b)
                nc.scalar.activation(qh[:, :], ln[:, :], ACT.Copy).then_inc(q_hi, 1)

            def kc_out(b, s):
                act.wait_ge(kc_mm, b + 1)
                if not fixed(b, 1):
                    act.wait_ge(wc_prod, 2 * b)
                    act.wait_ge(swap_c, 32 * b)
                nc.scalar.activation(kc[:, :], ps_c[s][:, :], ACT.Copy).then_inc(kc_sb, 1)

            def kn_out(b):
                act.wait_ge(kn_mm, b + 1)
                if not fixed(b, 1):
                    act.wait_ge(wn_prod, 2 * b)
                    act.wait_ge(swap_n, 32 * b)
                nc.scalar.activation(kn[:, :], ps_f[:, :], ACT.Copy).then_inc(kn_sb, 1)

            def corr_exp(b, s, h):
                act.wait_ge(mx_ready, 2 * b + h + 1)
                if not fixed(b, 1):
                    act.wait_ge(w_ready, 2 * b)
                for g in blocks(h):
                    ins = nc.scalar.activation(ew[:, blk(g)], ps_c[s][:, blk(g)], ACT.Exp, bias=nmx[:, g:g + 1])
                ins.then_inc(e_done, 1)

            def top_exp(b):
                act.wait_ge(nd_ready, b + 1)
                nc.scalar.activation(me[:, :, :], md[:, :, :], ACT.Exp).then_inc(te_done, 1)

            def scale_exp(b, h):
                act.wait_ge(ms_ready, b + 1)
                act.wait_ge(e_done, 2 * b + h + 1)
                for g in blocks(h):
                    ins = nc.scalar.activation(ew[:, blk(g)], ew[:, blk(g)], ACT.Copy, scale=ms[:, g:g + 1])
                ins.then_inc(scaled, 1)

            def wt_out(b, s, h):
                act.wait_ge(wt_mm, 2 * b + h + 1)
                if not fixed(b, 1):
                    act.wait_ge(wn_mm, b)
                nc.scalar.activation(wth[:, cols(h)], ps_c[s][:, cols(h)], ACT.Copy).then_inc(wt_hi, 1)

            def yt_out(b, s, h):
                act.wait_ge(yt_mm, 2 * b + h + 1)
                if not fixed(b, 1):
                    act.wait_ge(main_mm, b)
                nc.scalar.activation(yh[:, blocks(h).start:blocks(h).stop, :],
                                     ps_c[s][:, cols(h)].rearrange("p (k t) -> p k t", t=P),
                                     ACT.Copy).then_inc(yt_hi, 1)

            def router_exp(b):
                act.wait_ge(lm_ready, b + 1)
                nc.scalar.activation(pe_[:, :], lg[:, :], ACT.Exp, bias=nlm[:, 0:1],
                                     accum_out=psum_[:, 0:1]).then_inc(pexp, 1)

            def ht_out(b):
                act.wait_ge(ht_mm, b + 1)
                if not fixed(b, 1):
                    act.wait_ge(lora_mm, b)
                nc.scalar.activation(hth[:, :], ps_t[:, 0:P], ACT.Copy).then_inc(ht_hi, 1)

            def first():
                c_high(0)
                act.wait_ge(consts_in, 16)
                nc.scalar.activation(fh[:, :, :], cst[:, 0:I_CORR_A, :], ACT.Copy).then_inc(f_hi, 1)
                q_high(0)
                act.wait_ge(gates_in, 32)
                nc.scalar.activation(tg[:, :], gates[:, :], ACT.Tanh).then_inc(tanh_done, 1)
                split_weights((0, 1))
                kc_out(0, 0)
                split_weights((1, SPLITS_AT[0]))
                kn_out(0)
                split_weights((SPLITS_AT[0], SPLITS_AT[1]))
                corr_exp(0, 0, 0)
                corr_exp(0, 0, 1)
                top_exp(0)
                scale_exp(0, 0)
                scale_exp(0, 1)
                wt_out(0, 0, 0)
                wt_out(0, 0, 1)
                c_high(1)
                q_high(1)
                split_weights((SPLITS_AT[1], len(SPLITS)))
                kc_out(1, 1)

            def body(b, s, half_next):
                yt_out(b - 1, 1 - s, 0)
                yt_out(b - 1, 1 - s, 1)
                corr_exp(b, s, 0)
                kn_out(b)
                corr_exp(b, s, 1)
                if has_next(b):
                    c_high(b + 1)
                router_exp(b - 1)
                top_exp(b)
                scale_exp(b, 0)
                scale_exp(b, 1)
                wt_out(b, s, 0)
                wt_out(b, s, 1)
                ht_out(b - 1)
                if has_next(b):
                    q_high(b + 1)
                    kc_out(b + 1, 1 - s)

            def last():
                yt_out(B - 1, (B - 1) % 2, 0)
                yt_out(B - 1, (B - 1) % 2, 1)
                router_exp(B - 1)
                ht_out(B - 1)

            batches(act, first, body, last)

        @block.vector
        def _(dve):
            chx, chy = Chain(dve, dve_x, 2), Chain(dve, dve_y, 2)
            cht, chr_ = Chain(dve, dve_t, 9), Chain(dve, dve_r, 8)

            def setup():
                n = [0]

                def step(ins):
                    n[0] += 1
                    ins.then_inc(setup_dve, 1)

                dve.wait_ge(small_in, 32)
                step(nc.vector.tensor_copy(mapf[:, :], mapi[:, :]))
                dve.wait_ge(setup_dve, n[0])
                for e in range(E):
                    step(nc.vector.tensor_scalar(onehot[:, e, :], mapf[:, :], float(e), LORA_SCALE,
                                                 ALU.is_equal, ALU.mult))
                dve.wait_ge(gbias_in, 16)
                dve.wait_ge(tanh_done, 1)
                nc.vector.tensor_scalar(gbias[:, :], gbias[:, :], tg[:, 1:2], None, ALU.mult).then_inc(gb_ready, 1)
                dve.wait_ge(setup_dve, n[0])

            def split_weights(part):
                for n in range(*part):
                    dve.wait_ge(stage_hi, n + 1)
                    nc.vector.tensor_tensor(SPLITS[n][3], staged(n), SPLITS[n][2].bitcast(FP),
                                            ALU.subtract).then_inc(stage_lo, 1)

            def half_stats(src, bn, h, ch):
                ch.add(nc.vector.bn_stats(bn[:, h, :], src[:, cols(h)]))

            def stats(bn, mv, ready, ch):
                ch.wait()
                dve.nop(nofuse=True)
                nc.vector.bn_aggr(mv[:, :], bn[:, :, :]).then_inc(ready, 1)
                ch.end()

            def x_half_stats(b, s, half, h):
                if h == 0:
                    chx.begin(b)
                    dve.wait_ge(x_in[s], 16 * (half + 1))
                half_stats(xs[s], bn0, h, chx)
                if h == 1:
                    stats(bn0, mv0, mv0_ready, chx)

            def ln_x(b, s):
                dve.wait_ge(rs0_ready, b + 1)
                if not fixed(b, 2):
                    dve.wait_ge(yt_mm, 2 * (b - 1))
                nc.vector.tensor_scalar(ln[:, :], xs[s][:, :], mv0[:, 0:1], rs0[:, 0:1],
                                        ALU.subtract, ALU.mult).then_inc(q_ready, 1)

            def x1_half(b, s, h):
                dve.wait_ge(out_mm, 2 * b + h + 1)
                if not fixed(b, 2):
                    dve.wait_ge(x1b_ready, b - 1)
                nc.vector.scalar_tensor_tensor(x1[s][:, cols(h)], ps_c[s][:, cols(h)], tg[:, 0:1], xs[s][:, cols(h)],
                                               ALU.mult, ALU.add).then_inc(x1_ready, 1)

            def x1_half_stats(b, s, h):
                if h == 0:
                    chy.begin(b)
                dve.wait_ge(x1_ready, 2 * b + h + 1)
                half_stats(x1[s], bn1, h, chy)
                if h == 1:
                    stats(bn1, mv1, mv1_ready, chy)

            def ln_x1(b, s):
                dve.wait_ge(rs1_ready, b + 1)
                dve.wait_ge(q_lo, b + 2 if has_next(b) else B)
                for h in range(2):
                    nc.vector.tensor_scalar(ln[:, cols(h)], x1[s][:, cols(h)], mv1[:, 0:1], rs1[:, 0:1],
                                            ALU.subtract, ALU.mult).then_inc(y_ready, 1)

            def yt_low(b, s, h):
                dve.wait_ge(yt_hi, 2 * b + h + 1)
                part = slice(blocks(h).start, blocks(h).stop)
                nc.vector.tensor_tensor(yl[:, part, :], ps_c[s][:, cols(h)].rearrange("p (k t) -> p k t", t=P),
                                        yh[:, part, :].bitcast(FP), ALU.subtract).then_inc(yt_lo, 1)

            def products(b, s):
                dve.wait_ge(q_mm, b + 1)
                dve.wait_ge(kc_sb, b + 1)
                if not fixed(b, 1):
                    dve.wait_ge(w_ready, 2 * b)
                for h in range(2):
                    nc.vector.tensor_tensor(c1[:, cols(h)], ps_c[s][:, cols(h)], kc[:, cols(h)],
                                            ALU.mult).then_inc(prod_ab, 1)
                    if h == 0:
                        dve.wait_ge(swap_c, 32 * (b + 1))
                    nc.vector.tensor_tensor(c2[:, cols(h)], ps_c[s][:, cols(h)], kcs[:, cols(h)],
                                            ALU.mult).then_inc(prod_ab, 1)

            def top_8(b, s, h):
                dve.wait_ge(corr_mm, 2 * b + h + 1)
                dve.nop(nofuse=True)
                for g in blocks(h):
                    ins = nc.vector.max(mx[:, g, :], ps_c[s][:, blk(g)])
                cht.add(ins)
                cht.wait()
                nc.vector.tensor_scalar(nmx[:, blocks(h).start:blocks(h).stop],
                                        mx[:, blocks(h).start:blocks(h).stop, 0], -1.0, None,
                                        ALU.mult).then_inc(mx_ready, 1)

            def less_8(b, s, h):
                dve.wait_ge(e_done, 2 * b + h + 1)
                dve.nop(nofuse=True)
                for g in blocks(h):
                    ins = nc.vector.match_replace(c1[:, blk(g)], mx[:, g, :], ps_c[s][:, blk(g)], NEG)
                ins.then_inc(corr_read, 1)

            def ninth(b, h):
                dve.wait_ge(corr_read, 2 * b + h + 1)
                dve.nop(nofuse=True)
                for g in blocks(h):
                    ins = nc.vector.max(mx9[:, g, :], c1[:, blk(g)])
                cht.add(ins)

            def top_differences(b):
                cht.wait()
                cht.add(nc.vector.memset(mx9[:, :, 1:8], NEG))
                cht.add(nc.vector.tensor_tensor(md[:, :, 0:8], mx[:, :, :],
                                                mx[:, :, 0:1].to_broadcast([P, KT, 8]), ALU.subtract))
                nc.vector.tensor_tensor(md[:, :, 8:9], mx9[:, :, 0:1], mx[:, :, 0:1],
                                        ALU.subtract).then_inc(nd_ready, 1)

            def less_9(h):
                if h == 0:
                    cht.wait()
                    dve.nop(nofuse=True)
                for g in blocks(h):
                    ins = nc.vector.match_replace(c2[:, blk(g)], mx9[:, g, :], c1[:, blk(g)], NEG)
                cht.add(ins)

            def top_sums(b):
                dve.wait_ge(te_done, b + 1)
                cht.add(nc.vector.tensor_reduce(ms[:, :], me[:, :, :], AX.X, ALU.add))

            def inverse_sums(b):
                cht.wait()
                nc.vector.reciprocal(ms[:, :], ms[:, :]).then_inc(ms_ready, 1)

            def weights(b, h):
                cht.wait()
                dve.wait_ge(scaled, 2 * b + h + 1)
                if not fixed(b, 1):
                    dve.wait_ge(wt_mm, 2 * b)
                nc.vector.scalar_tensor_tensor(wm[:, cols(h)], c2[:, cols(h)], NEG_TEST, ew[:, cols(h)],
                                               ALU.is_lt, ALU.mult).then_inc(w_ready, 1)

            def wt_low(b, s, h):
                dve.wait_ge(wt_hi, 2 * b + h + 1)
                nc.vector.tensor_tensor(wtl[:, cols(h)], ps_c[s][:, cols(h)], wth[:, cols(h)].bitcast(FP),
                                        ALU.subtract).then_inc(wt_lo, 1)

            def conv_cyc(b, s):
                dve.wait_ge(wc_mm, b + 1)
                if not fixed(b, 1):
                    dve.wait_ge(out_mm, 2 * b)
                nc.vector.tensor_tensor(pa[:, :], ps_c[s][:, :], kc[:, :], ALU.mult).then_inc(wc_prod, 1)
                nc.vector.tensor_tensor(pbm[:, :], ps_c[s][:, :], kcs[:, :], ALU.mult).then_inc(wc_prod, 1)

            def conv_neg(b, s):
                dve.wait_ge(wn_mm, b + 1)
                dve.wait_ge(kn_sb, b + 1)
                nc.vector.tensor_tensor(pc[:, :], ps_c[1 - s][:, :], kn[:, :], ALU.mult).then_inc(wn_prod, 1)
                dve.wait_ge(swap_n, 32 * (b + 1))
                nc.vector.tensor_tensor(pd[:, :], ps_c[1 - s][:, :], kns[:, :], ALU.mult).then_inc(wn_prod, 1)

            def logits(b):
                chr_.begin(b)
                dve.wait_ge(ar_mm, b + 1)
                chr_.add(nc.vector.tensor_tensor(lg[:, :], ps_h[:, ER:ER + NR], rbb[:, :], ALU.add))

            def top_logits():
                chr_.wait()
                dve.nop(nofuse=True)
                chr_.add(nc.vector.max(lm[:, :], lg[:, :]))

            def mark_logits():
                chr_.wait()
                nc.vector.tensor_scalar(nlm[:, :], lm[:, 0:1], -1.0, None, ALU.mult).then_inc(lm_ready, 1)
                chr_.add(nc.vector.match_replace(lg2[:, :], lm[:, :], lg[:, :], NEG))

            def inverse_exp_sum(b):
                dve.wait_ge(pexp, b + 1)
                chr_.add(nc.vector.reciprocal(pinv[:, :], psum_[:, :]))

            def keep_probs():
                chr_.wait()
                chr_.add(nc.vector.tensor_scalar(pm[:, :], lg2[:, :], NEG_TEST, pinv[:, 0:1], ALU.is_lt, ALU.mult))

            def kept_probs():
                chr_.wait()
                chr_.add(nc.vector.tensor_tensor(pm[:, :], pm[:, :], pe_[:, :], ALU.mult))

            def probs_of_experts():
                chr_.wait()
                chr_.add(nc.vector.tensor_tensor(poh[:, :, :], onehot[:, :, :],
                                                 pm[:, :].unsqueeze(1).to_broadcast([P, E, NR]), ALU.mult))

            def expert_weights():
                chr_.wait()
                chr_.add(nc.vector.tensor_reduce(ewt[:, :], poh[:, :, :], AX.X, ALU.add))

            def weigh_h(b):
                chr_.wait()
                chr_.end()
                if not fixed(b, 1):
                    dve.wait_ge(ht_mm, b)
                nc.vector.tensor_tensor(hw[:, :].rearrange("p (e r) -> p e r", r=R),
                                        ps_h[:, 0:ER].rearrange("p (e r) -> p e r", r=R),
                                        ewt[:, :].unsqueeze(2).to_broadcast([P, E, R]),
                                        ALU.mult).then_inc(hw_ready, 1)

            def ht_low(b):
                dve.wait_ge(ht_hi, b + 1)
                nc.vector.tensor_tensor(htl[:, :], ps_t[:, 0:P], hth[:, :].bitcast(FP),
                                        ALU.subtract).then_inc(ht_lo, 1)

            def x2_step(b):
                dve.wait_ge(lora_mm, b + 1)
                dve.wait_ge(x1b_ready, b + 1)
                nc.vector.scalar_tensor_tensor(x2[:, :], ps_f[:, :], tg[:, 1:2], x2[:, :],
                                               ALU.mult, ALU.add).then_inc(x2_ready, 1)

            def x1_and_products(b, s):
                x1_half(b, s, 0)
                x1_half_stats(b, s, 0)
                if has_next(b):
                    products(b + 1, 1 - s)
                x1_half(b, s, 1)
                x1_half_stats(b, s, 1)

            def first():
                x_half_stats(0, 0, 0, 0)
                x_half_stats(0, 0, 0, 1)
                ln_x(0, 0)
                dve.wait_ge(f_hi, 1)
                nc.vector.tensor_tensor(fl[:, :, :], cst[:, 0:I_CORR_A, :], fh[:, :, :].bitcast(FP),
                                        ALU.subtract).then_inc(f_lo, 1)
                setup()
                split_weights((0, SPLITS_AT[0]))
                products(0, 0)
                split_weights((SPLITS_AT[0], SPLITS_AT[1]))
                cht.begin(0)
                for h in range(2):
                    top_8(0, 0, h)
                for h in range(2):
                    less_8(0, 0, h)
                for h in range(2):
                    ninth(0, h)
                top_differences(0)
                less_9(0)
                top_sums(0)
                inverse_sums(0)
                less_9(1)
                for h in range(2):
                    weights(0, h)
                cht.end()
                for h in range(2):
                    wt_low(0, 0, h)
                    x_half_stats(1, 1, 0, h)
                ln_x(1, 1)
                dve.wait_ge(stage_lo, SPLITS_AT[1])
                conv_cyc(0, 0)
                conv_neg(0, 0)
                split_weights((SPLITS_AT[1], len(SPLITS)))
                dve.wait_ge(stage_lo, len(SPLITS))
                x1_and_products(0, 0)

            def body(b, s, half_next):
                ln_x1(b - 1, 1 - s)
                cht.begin(b)
                top_8(b, s, 0)
                yt_low(b - 1, 1 - s, 0)
                yt_low(b - 1, 1 - s, 1)
                top_8(b, s, 1)
                less_8(b, s, 0)
                less_8(b, s, 1)
                ninth(b, 0)
                logits(b - 1)
                ninth(b, 1)
                top_logits()
                top_differences(b)
                mark_logits()
                less_9(0)
                top_sums(b)
                inverse_exp_sum(b - 1)
                inverse_sums(b)
                less_9(1)
                keep_probs()
                kept_probs()
                weights(b, 0)
                probs_of_experts()
                weights(b, 1)
                cht.end()
                expert_weights()
                weigh_h(b - 1)
                for h in range(2):
                    wt_low(b, s, h)
                    if has_next(b):
                        x_half_stats(b + 1, 1 - s, half_next, h)
                ht_low(b - 1)
                if has_next(b):
                    ln_x(b + 1, 1 - s)
                conv_cyc(b, s)
                conv_neg(b, s)
                x2_step(b - 1)
                x1_and_products(b, s)

            def last():
                ln_x1(B - 1, (B - 1) % 2)
                for h in range(2):
                    yt_low(B - 1, (B - 1) % 2, h)
                logits(B - 1)
                top_logits()
                mark_logits()
                inverse_exp_sum(B - 1)
                keep_probs()
                kept_probs()
                probs_of_experts()
                expert_weights()
                weigh_h(B - 1)
                ht_low(B - 1)
                x2_step(B - 1)

            batches(dve, first, body, last)

        @block.tensor
        def _(pe):
            def transform(out, mat, hi, lo, done):
                for h in range(2):
                    ins = exact3(nc, out[:, cols(h)], (fh[:, mat, :], fl[:, mat, :]), (hi[:, cols(h)], lo[:, cols(h)]),
                                 True, True)
                ins.then_inc(done, 1)

            def k_cyc(b, s):
                pe.wait_ge(c_lo, b + 1)
                if not fixed(b, 1):
                    pe.wait_ge(wn_prod, 2 * b)
                transform(ps_c[s], F_CYC_V, ch, cl, kc_mm)

            def k_neg(b):
                if not fixed(b, 2):
                    pe.wait_ge(x2_ready, b - 1)
                transform(ps_f, F_NEG_V, ch, cl, kn_mm)

            def q_cyc(b, s):
                pe.wait_ge(q_lo, b + 1)
                pe.wait_ge(kc_sb, b + 1)
                transform(ps_c[s], F_CYC, qh, ql, q_mm)

            def correlate(b, s):
                for h in range(2):
                    pe.wait_ge(prod_ab, 4 * b + 2 * (h + 1))
                    for g in blocks(h):
                        nc.tensor.matmul(ps_c[s][:, blk(g)], c1[:, blk(g)], cst[:, I_CORR_A, :],
                                         start=True, stop=False)
                        ins = nc.tensor.matmul(ps_c[s][:, blk(g)], c2[:, blk(g)], cst[:, I_CORR_B, :],
                                               start=False, stop=True)
                    ins.then_inc(corr_mm, 1)

            def weights_back(b, s, h):
                pe.wait_ge(w_ready, 2 * b + h + 1)
                for g in blocks(h):
                    ins = nc.tensor.transpose(ps_c[s][:, blk(g)], wm[:, blk(g)], cst[:, IDENT, :])
                ins.then_inc(wt_mm, 1)

            def transform_weights(b, s):
                pe.wait_ge(wt_lo, 2 * (b + 1))
                transform(ps_c[s], F_CYC, wth, wtl, wc_mm)
                if not fixed(b, 1):
                    pe.wait_ge(yt_lo, 2 * b)
                transform(ps_c[1 - s], F_NEG, wth, wtl, wn_mm)

            def out_cyc(b, s, h):
                pe.wait_ge(wc_prod, 2 * (b + 1))
                nc.tensor.matmul(ps_c[s][:, cols(h)], cst[:, I_CYC_A, :], pa[:, cols(h)], start=True, stop=False)
                nc.tensor.matmul(ps_c[s][:, cols(h)], cst[:, I_CYC_B, :], pbm[:, cols(h)], start=False, stop=False)

            def out_neg(b, s, h):
                pe.wait_ge(wn_prod, 2 * (b + 1))
                nc.tensor.matmul(ps_c[s][:, cols(h)], cst[:, I_NEG_A, :], pc[:, cols(h)], start=False, stop=False)
                ins = nc.tensor.matmul(ps_c[s][:, cols(h)], cst[:, I_NEG_B, :], pd[:, cols(h)],
                                       start=False, stop=True)
                ins.then_inc(out_mm, 1)

            def out_and_next(b, s):
                out_cyc(b, s, 0)
                if has_next(b):
                    k_cyc(b + 1, 1 - s)
                out_cyc(b, s, 1)
                out_neg(b, s, 0)
                if has_next(b):
                    q_cyc(b + 1, 1 - s)
                out_neg(b, s, 1)

            def transpose_y(b, s):
                for h in range(2):
                    pe.wait_ge(y_ready, 2 * b + h + 1)
                    for g in blocks(h):
                        ins = nc.tensor.transpose(ps_c[s][:, blk(g)], ln[:, blk(g)], cst[:, IDENT, :])
                    ins.then_inc(yt_mm, 1)

            def a_and_router(b):
                pe.wait_ge(stage_lo, len(SPLITS))
                if not fixed(b, 1):
                    pe.wait_ge(hw_ready, b)
                for k in range(KT):
                    if k % (KT // 2) == 0:
                        pe.wait_ge(yt_lo, 2 * b + k // (KT // 2) + 1)
                    ins = exact3(nc, ps_h[:, 0:AR], (yh[:, k, :], yl[:, k, :]), (arh[:, k, :], arl[:, k, :]),
                                 k == 0, k == KT - 1)
                ins.then_inc(ar_mm, 1)

            def ffn_main(b, ks):
                if ks[0] == 0:
                    if has_next(b):
                        pe.wait_ge(kn_sb, b + 2)
                    else:
                        pe.wait_ge(x2_ready, b)
                for k in ks:
                    for h in range(2):
                        ins = exact3(nc, ps_f[:, cols(h)], (yh[:, k, :], yl[:, k, :]),
                                     (wh[:, k, cols(h)], wl[:, k, cols(h)]), k == 0, False)
                if ks[-1] == KT - 1:
                    ins.then_inc(main_mm, 1)

            def transpose_h(b):
                pe.wait_ge(hw_ready, b + 1)
                if not fixed(b, 1):
                    pe.wait_ge(ht_lo, b)
                nc.tensor.transpose(ps_t[:, 0:P], hw[:, :], cst[:, IDENT, :]).then_inc(ht_mm, 1)

            def lora(b):
                pe.wait_ge(ht_lo, b + 1)
                for h in range(2):
                    ins = exact3(nc, ps_f[:, cols(h)], (hth[:, :], htl[:, :]), (bh[:, cols(h)], bl[:, cols(h)]),
                                 False, True)
                ins.then_inc(lora_mm, 1)

            def first():
                pe.wait_ge(consts_in, 16)
                pe.wait_ge(f_lo, 1)
                k_cyc(0, 0)
                k_neg(0)
                q_cyc(0, 0)
                correlate(0, 0)
                weights_back(0, 0, 0)
                weights_back(0, 0, 1)
                transform_weights(0, 0)
                out_and_next(0, 0)

            def body(b, s, half_next):
                correlate(b, s)
                transpose_y(b - 1, 1 - s)
                k_neg(b)
                a_and_router(b - 1)
                ffn_main(b - 1, range(0, 5))
                weights_back(b, s, 0)
                ffn_main(b - 1, range(5, 6))
                weights_back(b, s, 1)
                transpose_h(b - 1)
                ffn_main(b - 1, range(6, 7))
                transform_weights(b, s)
                ffn_main(b - 1, range(7, 8))
                lora(b - 1)
                out_and_next(b, s)

            def last():
                transpose_y(B - 1, (B - 1) % 2)
                a_and_router(B - 1)
                ffn_main(B - 1, range(KT))
                transpose_h(B - 1)
                lora(B - 1)

            batches(pe, first, body, last)


def attention_and_clamped_ffn(nc, ctx_in, ctx_t, g_x, g_f, w_t, bias, a_t, b_t, pscores, consts, x2_dram, out):
    ctx = ExitStack()
    with ctx:
        def sb(name, shape, dt=FP):
            return ctx.enter_context(nc.sbuf_tensor(name, shape, dt))

        def pb(name, cols):
            return ctx.enter_context(nc.psum_tensor(name, [P, cols], FP))

        def sem(name):
            return ctx.enter_context(nc.semaphore(name))

        TILES = D // P
        GT = 2
        GROUPS = TILES // GT
        GC = GT * P

        ident = sb("ident2", [P, P])
        wh, wl = sb("w1_hi", [P, KT, D], FR), sb("w1_lo", [P, KT, D], FR)
        ah, al = sb("a1_hi", [P, KT, ER], FR), sb("a1_lo", [P, KT, ER], FR)
        bh, bl = sb("b1_hi", [P, D], FR), sb("b1_lo", [P, D], FR)
        zbias = sb("z_bias", [P, D])
        pcol = sb("p_scores_rows", [P, 1])
        gates, tg = sb("gates2", [P, 2]), sb("tanh_gates2", [P, 2])
        pow_n, pow_p = sb("minus_half", [P, 1]), sb("plus_half", [P, 2])
        x2 = [sb(f"x2in_{s}", [P, D]) for s in range(2)]
        c = sb("ctx_stage", [P, D])
        q = sb("ln_out", [P, D])
        ch = [sb(f"c_hi_{s}", [P, D], FR) for s in range(2)]
        cl = [sb(f"c_lo_{s}", [P, D], FR) for s in range(2)]
        qh = [sb(f"q_hi_{s}", [P, D], FR) for s in range(2)]
        ql = [sb(f"q_lo_{s}", [P, D], FR) for s in range(2)]
        vh, vl = sb("v_t_hi", [P, KT, P], FR), sb("v_t_lo", [P, KT, P], FR)
        pr = [sb(f"probs_{s}", [P, D]) for s in range(2)]
        pth = [sb(f"probs_t_hi_{s}", [P, KT, GC], FR) for s in range(2)]
        ptl = [sb(f"probs_t_lo_{s}", [P, KT, GC], FR) for s in range(2)]
        nmx = sb("neg_row_max", [P, TILES])
        rsum = sb("row_sum", [P, TILES])
        rinv = sb("row_inv", [P, TILES])
        x3 = [sb(f"x3_{s}", [P, D]) for s in range(2)]
        z = sb("z", [P, D])
        yh, yl = sb("y_t_hi", [P, KT, P], FR), sb("y_t_lo", [P, KT, P], FR)
        bn = sb("bn2", [P, 2, 6])
        mv2, mv3 = sb("mean_var_x2", [P, 2]), sb("mean_var_x3", [P, 2])
        rs2, rs3 = sb("rstd_x2", [P, 1]), sb("rstd_x3", [P, 1])
        uth, utl = sb("u_t_hi", [P, P], FR), sb("u_t_lo", [P, P], FR)
        nrm = sb("square_sums", [P, 4])
        nrt = sb("norm_roots", [P, 2])
        gam = sb("gamma", [P, 1])
        m = sb("m", [P, D])

        ps_s = [pb(f"ps_s{s}", D) for s in range(2)]
        ps_t = [pb(f"ps_t{s}", HALF) for s in range(2)]
        ps_o = pb("ps_o", HALF)
        ps_f = pb("ps_f2", HALF)

        const_in, gates_in, small_in = sem("const2_in"), sem("gates2_in"), sem("small2_in")
        x2_in = [sem("x2_in0"), sem("x2_in1")]
        c_in, ct_in = sem("c2_in"), sem("ct2_in")
        stage_in = [sem("stage2_in0"), sem("stage2_in1")]
        stage_hi, stage_lo = sem("stage2_hi"), sem("stage2_lo")
        tanh_done, pow_ready, out_done = sem("tanh2_done"), sem("pow2_ready"), sem("out_done")
        mv2_r, mv3_r, rs2_r, rs3_r = sem("mv2_r"), sem("mv3_r"), sem("rs2_r"), sem("rs3_r")
        q_r, q_hi, q_lo = sem("q2_r"), sem("q2_hi"), sem("q2_lo")
        c_hi, c_lo, v_hi, v_lo = sem("c2_hi"), sem("c2_lo"), sem("v2_hi"), sem("v2_lo")
        s_mm, t_mm, av_mm = sem("s_mm"), sem("t_mm"), sem("av_mm")
        yt_mm, z_mm, ut_mm, m_mm = sem("yt2_mm"), sem("z_mm"), sem("ut_mm"), sem("m_mm")
        max_r, exp_r, inv_r, prob_r = sem("max_r"), sem("exp_r"), sem("inv_r"), sem("prob_r")
        t_hi, t_lo, x3_r = sem("t_hi"), sem("t_lo"), sem("x3_r")
        y_r, yt_hi, yt_lo = sem("y2_r"), sem("yt2_hi"), sem("yt2_lo")
        ut_hi, ut_lo, v_used = sem("ut_hi"), sem("ut_lo"), sem("v_used")
        m_sb, sq_m, z_r, sq_z, root_r, xz_r, out_r = (sem("m_sb"), sem("sq_m"), sem("z_r"), sem("sq_z"),
                                                     sem("root_r"), sem("x3_plus_z"), sem("out_r"))
        dve_q, dve_y, dve_g = sem("dve_q"), sem("dve_y"), sem("dve_g")
        pool_q, pool_y, pool_n = sem("pool_q"), sem("pool_y"), sem("pool_n")

        stage = [m, z]
        SPLITS = [(w_t[k], wh[:, k, :], wl[:, k, :]) for k in range(KT)]
        SPLITS += [(b_t, bh[:, :], bl[:, :]), (a_t, ah[:, :, :].rearrange("p k a -> p (k a)"),
                                               al[:, :, :].rearrange("p k a -> p (k a)"))]
        block = ctx.enter_context(nc.Block())

        def fixed(b, below):
            return isinstance(b, int) and b < below

        def splits_in(b, n):
            return range(len(SPLITS))[TILES * b + n:TILES * b + n + 1]

        def cols(h):
            return slice(h * HALF, (h + 1) * HALF)

        def all_batches(eng, batch):
            batch(0, 0, 0, False, False, True)
            batch(1, 1, 1, True, False, True)
            with eng.Fori(0, (B - 4) // 2) as p:
                for s in (0, 1):
                    batch(p * 2 + (s + 2), s, p + (s + 1), True, True, True)
            batch(B - 2, 0, (B - 1) // 2, True, True, True)
            batch(B - 1, 1, B // 2, True, True, False)

        @block.sync
        def _(sp):
            sp.dma_start(x2[0][:, :], x2_dram[0]).then_inc(x2_in[0], 16)
            sp.dma_start(c[:, :], ctx_in[0]).then_inc(c_in, 16)
            sp.dma_start(ident[:, :], consts[:, IDENT, :]).then_inc(const_in, 16)
            sp.dma_start(gates[:, 0:1], g_x[1:2].partition_broadcast(P)).then_inc(gates_in, 16)
            sp.dma_start(gates[:, 1:2], g_f[1:2].partition_broadcast(P)).then_inc(gates_in, 16)
            sp.dma_start(x2[1][:, :], x2_dram[1]).then_inc(x2_in[1], 16)
            for n in range(2):
                sp.dma_start(stage[n][:, :], SPLITS[n][0]).then_inc(stage_in[n], 16)
            sp.dma_start(zbias[:, :], bias.partition_broadcast(P)).then_inc(small_in, 16)
            sp.dma_start(pcol[:, :], pscores).then_inc(small_in, 16)

            def load_ctx_t(b):
                sp.wait_ge(c_lo, b + 1)
                sp.dma_start(c[:, :].rearrange("p (k c) -> p k c", c=P), ctx_t[b]).then_inc(ct_in, 16)

            def load_ctx(b):
                sp.wait_ge(v_lo, 2 * b)
                sp.dma_start(c[:, :], ctx_in[b]).then_inc(c_in, 16)

            def load_x2(b, s):
                sp.wait_ge(x3_r, GROUPS * (b - 1))
                sp.dma_start(x2[s][:, :], x2_dram[b]).then_inc(x2_in[s], 16)

            def store(b):
                sp.wait_ge(out_r, b + 1)
                sp.dma_start(out[b], z[:, :]).then_inc(out_done, 16)

            load_ctx_t(0)
            for n in range(2, len(SPLITS)):
                if n == 3:
                    load_ctx(1)
                if n == 6:
                    load_ctx_t(1)
                sp.wait_ge(stage_hi, n - 1)
                sp.wait_ge(stage_lo, n - 1)
                sp.dma_start(stage[n % 2][:, :], SPLITS[n][0]).then_inc(stage_in[n % 2], 16)

            def batch(b, s, half_next, ffn, fin, more):
                if ffn and more:
                    load_x2(b + 1, 1 - s)
                    load_ctx(b + 1)
                if ffn and more:
                    load_ctx_t(b + 1)
                if fin:
                    store(b - 2)

            all_batches(sp, batch)
            store(B - 2)
            store(B - 1)
            sp.wait_ge(out_done, 16 * B)

        @block.gpsimd
        def _(pool):
            chq, chy, chn = Chain(pool, pool_q, 1), Chain(pool, pool_y, 1), Chain(pool, pool_n, 1)
            nc.gpsimd.memset(pow_n[:, :], -0.5).then_inc(pow_ready, 1)
            nc.gpsimd.memset(pow_p[:, :], 0.5).then_inc(pow_ready, 1)
            pool.wait_ge(pow_ready, 2)

            def rstd_x2(b):
                chq.begin(b)
                pool.wait_ge(mv2_r, b + 1)
                pool.nop(nofuse=True)
                chq.add(nc.gpsimd.tensor_scalar(rs2[:, :], mv2[:, 1:2], LN_EPS, float(L), ALU.add, ALU.mult))
                chq.wait()
                nc.gpsimd.tensor_tensor(rs2[:, :], rs2[:, :], pow_n[:, :], ALU.pow).then_inc(rs2_r, 1)
                chq.end()

            def q_low(b, s):
                pool.wait_ge(q_hi, b + 1)
                nc.gpsimd.tensor_tensor(ql[s][:, :], q[:, :], qh[s][:, :].bitcast(FP), ALU.subtract).then_inc(q_lo, 1)

            def c_low(b, s):
                pool.wait_ge(c_hi, b + 1)
                nc.gpsimd.tensor_tensor(cl[s][:, :], c[:, :], ch[s][:, :].bitcast(FP),
                                        ALU.subtract).then_inc(c_lo, 1)

            def v_low(b, h):
                pool.wait_ge(v_hi, 2 * b + h + 1)
                nc.gpsimd.tensor_tensor(vl[:, 4 * h:4 * h + 4, :], c[:, cols(h)].rearrange("p (k c) -> p k c", c=P),
                                        vh[:, 4 * h:4 * h + 4, :].bitcast(FP), ALU.subtract).then_inc(v_lo, 1)

            def normalise(b, n):
                pool.wait_ge(inv_r, TILES * b + n + 1)
                pool.nop(nofuse=True)
                nc.gpsimd.tensor_scalar(pr[n % 2][:, :], pr[n % 2][:, :], rinv[:, n:n + 1], tg[:, 0:1],
                                        ALU.mult, ALU.mult).then_inc(prob_r, 1)

            def rstd_x3(b):
                chy.begin(b)
                pool.wait_ge(mv3_r, b + 1)
                pool.nop(nofuse=True)
                chy.add(nc.gpsimd.tensor_scalar(rs3[:, :], mv3[:, 1:2], LN_EPS, None, ALU.add))
                chy.wait()
                nc.gpsimd.tensor_tensor(rs3[:, :], rs3[:, :], pow_n[:, :], ALU.pow).then_inc(rs3_r, 1)
                chy.end()

            def roots(b):
                chn.begin(b)
                pool.wait_ge(sq_z, 2 * (b + 1))
                pool.wait_ge(sq_m, 2 * (b + 1))
                chn.add(nc.gpsimd.tensor_tensor(nrt[:, :], nrm[:, 0:2], nrm[:, 2:4], ALU.add))
                chn.wait()
                nc.gpsimd.tensor_tensor(nrt[:, :], nrt[:, :], pow_p[:, :], ALU.pow).then_inc(root_r, 1)
                chn.end()

            def batch(b, s, half_next, ffn, fin, more):
                for n in range(TILES - 1):
                    normalise(b, n + 1)
                    if n < 2:
                        v_low(b, n)
                    if n == 2 and ffn:
                        rstd_x3(b - 1)
                    if n == 2 and fin:
                        roots(b - 2)
                    if n == 3 and more:
                        c_low(b + 1, 1 - s)
                        rstd_x2(b + 1)
                    if n == 4 and more:
                        q_low(b + 1, 1 - s)
                if more:
                    normalise(b + 1, 0)

            rstd_x2(0)
            c_low(0, 0)
            pool.wait_ge(tanh_done, 1)
            normalise(0, 0)
            all_batches(pool, batch)
            rstd_x3(B - 1)
            roots(B - 2)
            roots(B - 1)

        @block.scalar
        def _(act):
            def q_high(b, s):
                act.wait_ge(q_r, b + 1)
                if not fixed(b, 2):
                    act.wait_ge(s_mm, TILES * (b - 1))
                nc.scalar.activation(qh[s][:, :], q[:, :], ACT.Copy).then_inc(q_hi, 1)

            def c_high(b, s):
                act.wait_ge(c_in, 16 * (b + 1))
                if not fixed(b, 2):
                    act.wait_ge(s_mm, TILES * (b - 1))
                nc.scalar.activation(ch[s][:, :], c[:, :], ACT.Copy).then_inc(c_hi, 1)

            def v_high(b, h):
                act.wait_ge(ct_in, 16 * (b + 1))
                if not fixed(b, 1):
                    if h == 0:
                        act.wait_ge(v_used, b)
                    else:
                        act.wait_ge(av_mm, GROUPS * b)
                nc.scalar.activation(vh[:, 4 * h:4 * h + 4, :], c[:, cols(h)].rearrange("p (k c) -> p k c", c=P),
                                     ACT.Copy).then_inc(v_hi, 1)

            def exps(b, n):
                act.wait_ge(max_r, TILES * b + n + 1)
                if not (fixed(b, 1) and n < 2):
                    act.wait_ge(t_mm, 2 * TILES * b + 2 * (n - 1))
                nc.scalar.activation(pr[n % 2][:, :], ps_s[n % 2][:, :], ACT.Exp, bias=nmx[:, n:n + 1],
                                     accum_out=rsum[:, n:n + 1]).then_inc(exp_r, 1)

            def tile_high(b, n):
                g = n // GT
                for h in range(2):
                    act.wait_ge(t_mm, 2 * (TILES * b + n) + h + 1)
                    if n % GT == 0 and not (fixed(b, 1) and g < 2):
                        act.wait_ge(av_mm, GROUPS * b + g - 1)
                    nc.scalar.activation(pth[g % 2][:, 4 * h:4 * h + 4, (n % GT) * P:(n % GT + 1) * P],
                                         ps_t[h][:, :].rearrange("p (k t) -> p k t", t=P),
                                         ACT.Copy).then_inc(t_hi, 1)

            def y_high(b):
                for h in range(2):
                    act.wait_ge(yt_mm, 2 * b + h + 1)
                    if not fixed(b, 1):
                        act.wait_ge(z_mm, 2 * b)
                    nc.scalar.activation(yh[:, 4 * h:4 * h + 4, :],
                                         ps_t[h][:, :].rearrange("p (k t) -> p k t", t=P),
                                         ACT.Copy).then_inc(yt_hi, 1)

            def u_high(b):
                act.wait_ge(ut_mm, b + 1)
                if fixed(b, 1):
                    act.wait_ge(small_in, 32)
                if not fixed(b, 1):
                    act.wait_ge(m_mm, 2 * b)
                nc.scalar.activation(uth[:, :], ps_f[:, 0:P], ACT.Copy, scale=pcol[:, 0:1]).then_inc(ut_hi, 1)

            def m_out(b, h):
                act.wait_ge(m_mm, 2 * b + h + 1)
                if not fixed(b, 1) and h == 0:
                    act.wait_ge(out_r, b)
                    act.wait_ge(root_r, b)
                nc.scalar.activation(m[:, cols(h)], ps_f[:, :], ACT.Copy).then_inc(m_sb, 1)
                act.wait_ge(m_sb, 2 * b + h + 1)
                nc.scalar.activation(ps_f[:, :], ps_f[:, :], ACT.Square,
                                     accum_out=nrm[:, 2 * h + 1:2 * h + 2]).then_inc(sq_m, 1)

            def z_squares(b, h):
                act.wait_ge(z_r, 2 * b + h + 1)
                nc.scalar.activation(ps_f[:, :], z[:, cols(h)], ACT.Square,
                                     accum_out=nrm[:, 2 * h:2 * h + 1]).then_inc(sq_z, 1)

            def split(n):
                act.wait_ge(stage_in[n % 2], 16 * (n // 2 + 1))
                nc.scalar.activation(SPLITS[n][1], stage[n % 2][:, :], ACT.Copy).then_inc(stage_hi, 1)

            def batch(b, s, half_next, ffn, fin, more):
                for n in range(TILES):
                    if n == 0 and fin:
                        z_squares(b - 2, 0)
                    if n >= 6 and ffn:
                        m_out(b - 1, n - 6)
                    tile_high(b, n)
                    if n == 3 and ffn:
                        y_high(b - 1)
                    if n == 5 and ffn:
                        u_high(b - 1)
                    if n < TILES - 2:
                        exps(b, n + 2)
                    elif more:
                        exps(b + 1, n + 2 - TILES)
                    if n == 2 and fin:
                        z_squares(b - 2, 1)
                    if n < 2:
                        v_high(b, n)
                    if n == 3 and more:
                        c_high(b + 1, 1 - s)
                    if n == 4 and more:
                        q_high(b + 1, 1 - s)
                    if fixed(b, 2) and splits_in(b, n):
                        split(splits_in(b, n)[0])

            c_high(0, 0)
            q_high(0, 0)
            act.wait_ge(gates_in, 32)
            nc.scalar.activation(tg[:, :], gates[:, :], ACT.Tanh).then_inc(tanh_done, 1)
            exps(0, 0)
            exps(0, 1)
            all_batches(act, batch)
            z_squares(B - 2, 0)
            z_squares(B - 2, 1)
            y_high(B - 1)
            u_high(B - 1)
            m_out(B - 1, 0)
            m_out(B - 1, 1)
            z_squares(B - 1, 0)
            z_squares(B - 1, 1)

        @block.vector
        def _(dve):
            chq, chy, chg = Chain(dve, dve_q, 2), Chain(dve, dve_y, 2), Chain(dve, dve_g, 4)

            def stats(src, mv, ready, ch):
                for h in range(2):
                    ch.add(nc.vector.bn_stats(bn[:, h, :], src[:, cols(h)]))
                ch.wait()
                dve.nop(nofuse=True)
                nc.vector.bn_aggr(mv[:, :], bn[:, :, :]).then_inc(ready, 1)

            def x2_stats(b, s, half):
                chq.begin(b)
                dve.wait_ge(x2_in[s], 16 * (half + 1))
                stats(x2[s], mv2, mv2_r, chq)
                chq.end()

            def ln_x2(b, s):
                dve.wait_ge(rs2_r, b + 1)
                if not fixed(b, 2):
                    dve.wait_ge(yt_mm, 2 * (b - 1))
                nc.vector.tensor_scalar(q[:, :], x2[s][:, :], mv2[:, 0:1], rs2[:, 0:1],
                                        ALU.subtract, ALU.mult).then_inc(q_r, 1)

            def x3_stats(b, s):
                chy.begin(b)
                dve.wait_ge(x3_r, GROUPS * (b + 1))
                stats(x3[s], mv3, mv3_r, chy)
                chy.end()

            def ln_x3(b, s, last):
                dve.wait_ge(rs3_r, b + 1)
                dve.wait_ge(q_lo, b + 1 if last else b + 2)
                nc.vector.tensor_scalar(q[:, :], x3[s][:, :], mv3[:, 0:1], rs3[:, 0:1],
                                        ALU.subtract, ALU.mult).then_inc(y_r, 1)

            def row_max(b, n):
                dve.wait_ge(s_mm, TILES * b + n + 1)
                if not fixed(b, 1):
                    dve.wait_ge(exp_r, TILES * (b - 1) + n + 1)
                nc.vector.tensor_reduce(nmx[:, n:n + 1], ps_s[n % 2][:, :], AX.X, ALU.max,
                                        negate=True).then_inc(max_r, 1)

            def inverse_sum(b, n):
                dve.wait_ge(exp_r, TILES * b + n + 1)
                if not fixed(b, 1):
                    dve.wait_ge(prob_r, TILES * (b - 1) + n + 1)
                nc.vector.reciprocal(rinv[:, n:n + 1], rsum[:, n:n + 1]).then_inc(inv_r, 1)

            def tile_low(b, n):
                g = n // GT
                for h in range(2):
                    dve.wait_ge(t_hi, 2 * (TILES * b + n) + h + 1)
                    part = (slice(None), slice(4 * h, 4 * h + 4), slice((n % GT) * P, (n % GT + 1) * P))
                    nc.vector.tensor_tensor(ptl[g % 2][part], ps_t[h][:, :].rearrange("p (k t) -> p k t", t=P),
                                            pth[g % 2][part].bitcast(FP), ALU.subtract).then_inc(t_lo, 1)

            def residual(b, s, g):
                dve.wait_ge(av_mm, GROUPS * b + g + 1)
                if g in (0, 2) and not fixed(b, 2):
                    dve.wait_ge(xz_r, 2 * (b - 1) - 1 + g // 2)
                part = slice(g * GC, (g + 1) * GC)
                nc.vector.tensor_tensor(x3[s][:, part], ps_o[:, 0:GC], x2[s][:, part], ALU.add).then_inc(x3_r, 1)

            def y_low(b):
                for h in range(2):
                    dve.wait_ge(yt_hi, 2 * b + h + 1)
                    nc.vector.tensor_tensor(yl[:, 4 * h:4 * h + 4, :],
                                            ps_t[h][:, :].rearrange("p (k t) -> p k t", t=P),
                                            yh[:, 4 * h:4 * h + 4, :].bitcast(FP), ALU.subtract).then_inc(yt_lo, 1)

            def add_bias(b, h):
                dve.wait_ge(z_mm, 2 * b + h + 1)
                if fixed(b, 1):
                    dve.wait_ge(small_in, 32)
                if not fixed(b, 1) and h == 0:
                    dve.wait_ge(out_done, 16 * b)
                nc.vector.tensor_tensor(z[:, cols(h)], ps_f[:, :], zbias[:, cols(h)], ALU.add).then_inc(z_r, 1)

            def u_low(b):
                dve.wait_ge(ut_hi, b + 1)
                nc.vector.scalar_tensor_tensor(utl[:, :], ps_f[:, 0:P], pcol[:, 0:1], uth[:, :].bitcast(FP),
                                               ALU.mult, ALU.subtract).then_inc(ut_lo, 1)

            def add_x3(b, s, h):
                dve.wait_ge(sq_z, 2 * b + h + 1)
                nc.vector.scalar_tensor_tensor(z[:, cols(h)], z[:, cols(h)], tg[:, 1:2], x3[s][:, cols(h)],
                                               ALU.mult, ALU.add).then_inc(xz_r, 1)

            def add_clamped_m(b):
                chg.begin(b)
                dve.wait_ge(root_r, b + 1)
                chg.add(nc.vector.tensor_scalar(gam[:, :], nrt[:, 1:2], EPS, None, ALU.add))
                chg.wait()
                chg.add(nc.vector.reciprocal(gam[:, :], gam[:, :]))
                chg.wait()
                chg.add(nc.vector.tensor_scalar(gam[:, :], gam[:, :], nrt[:, 0:1], C_CLAMP, ALU.mult, ALU.mult))
                chg.wait()
                chg.add(nc.vector.tensor_scalar(gam[:, :], gam[:, :], 1.0, tg[:, 1:2], ALU.min, ALU.mult))
                chg.wait()
                chg.end()
                dve.wait_ge(xz_r, 2 * (b + 1))
                nc.vector.scalar_tensor_tensor(z[:, :], m[:, :], gam[:, 0:1], z[:, :],
                                               ALU.mult, ALU.add).then_inc(out_r, 1)

            def split(n):
                dve.wait_ge(stage_hi, n + 1)
                nc.vector.tensor_tensor(SPLITS[n][2], stage[n % 2][:, :], SPLITS[n][1].bitcast(FP),
                                        ALU.subtract).then_inc(stage_lo, 1)

            def batch(b, s, half_next, ffn, fin, more):
                for n in range(TILES):
                    if n == 0 and fin:
                        add_bias(b - 2, 0)
                    if n == 2 and fin:
                        add_bias(b - 2, 1)
                    if n == 3:
                        tile_low(b, n)
                    if n == 6:
                        residual(b, s, 1)
                    if n == 0 and ffn:
                        residual(b - 1, 1 - s, 2)
                    if n < TILES - 1:
                        inverse_sum(b, n + 1)
                    elif more:
                        inverse_sum(b + 1, 0)
                    if n < TILES - 2:
                        row_max(b, n + 2)
                    elif more:
                        row_max(b + 1, n + 2 - TILES)
                    if n != 3:
                        tile_low(b, n)
                    if n == 3:
                        residual(b, s, 0)
                    if n == 1 and ffn:
                        residual(b - 1, 1 - s, 3)
                        x3_stats(b - 1, 1 - s)
                    if n == 2 and ffn:
                        ln_x3(b - 1, 1 - s, False)
                    if n == 1 and fin:
                        add_x3(b - 2, s, 0)
                    if n == 3 and ffn:
                        y_low(b - 1)
                    if n == 3 and more:
                        x2_stats(b + 1, 1 - s, half_next)
                    if n == 4 and more:
                        ln_x2(b + 1, 1 - s)
                    if n == 4 and fin:
                        add_x3(b - 2, s, 1)
                    if n == 5 and ffn:
                        u_low(b - 1)
                    if n == 5 and fin:
                        add_clamped_m(b - 2)
                    if fixed(b, 2) and splits_in(b, n):
                        split(splits_in(b, n)[0])

            x2_stats(0, 0, 0)
            ln_x2(0, 0)
            dve.wait_ge(q_hi, 1)
            nc.vector.tensor_tensor(ql[0][:, :], q[:, :], qh[0][:, :].bitcast(FP), ALU.subtract).then_inc(q_lo, 1)
            row_max(0, 0)
            row_max(0, 1)
            inverse_sum(0, 0)
            dve.wait_ge(tanh_done, 1)
            all_batches(dve, batch)
            add_bias(B - 2, 0)
            residual(B - 1, 1, 2)
            residual(B - 1, 1, 3)
            add_x3(B - 2, 0, 0)
            add_bias(B - 2, 1)
            x3_stats(B - 1, 1)
            ln_x3(B - 1, 1, True)
            add_x3(B - 2, 0, 1)
            y_low(B - 1)
            add_clamped_m(B - 2)
            u_low(B - 1)
            add_bias(B - 1, 0)
            add_x3(B - 1, 1, 0)
            add_bias(B - 1, 1)
            add_x3(B - 1, 1, 1)
            add_clamped_m(B - 1)

        @block.tensor
        def _(pe):
            def scores(b, s, n):
                if n == 0:
                    pe.wait_ge(q_lo, b + 1)
                    pe.wait_ge(c_lo, b + 1)
                if not (fixed(b, 1) and n < 2):
                    pe.wait_ge(exp_r, TILES * b + n - 1)
                blk = slice(n * P, (n + 1) * P)
                for h in range(2):
                    ins = exact3(nc, ps_s[n % 2][:, cols(h)], (ch[s][:, blk], cl[s][:, blk]),
                                 (qh[s][:, cols(h)], ql[s][:, cols(h)]), True, True)
                ins.then_inc(s_mm, 1)

            def transposes(b, n, behind_y):
                pe.wait_ge(prob_r, TILES * b + n + 1)
                for h in range(2):
                    if behind_y:
                        pe.wait_ge(yt_lo, 2 * (b - 1) + h + 1)
                    elif not (fixed(b, 1) and n == 0):
                        pe.wait_ge(t_lo, 2 * (TILES * b + n) + h - 1)
                    for k in range(4):
                        src = pr[n % 2][:, (4 * h + k) * P:(4 * h + k + 1) * P]
                        ins = nc.tensor.transpose(ps_t[h][:, k * P:(k + 1) * P], src, ident[:, :])
                    ins.then_inc(t_mm, 1)

            def values(b, g, part):
                if g == 0:
                    pe.wait_ge(v_lo, 2 * b + part + 1)
                if part == 0:
                    pe.wait_ge(t_lo, 2 * (TILES * b + GT * (g + 1)))
                    if not (fixed(b, 1) and g == 0):
                        pe.wait_ge(x3_r, GROUPS * b + g)
                for k in range(4 * part, 4 * part + 4):
                    ins = exact3(nc, ps_o[:, 0:GC], (vh[:, k, :], vl[:, k, :]),
                                 (pth[g % 2][:, k, :], ptl[g % 2][:, k, :]), k == 0, k == KT - 1)
                if part == 0 and g == GROUPS - 1:
                    ins.then_inc(v_used, 1)
                if part == 1:
                    ins.then_inc(av_mm, 1)

            def transposes_y(b, tiles_before):
                pe.wait_ge(y_r, b + 1)
                for h in range(2):
                    pe.wait_ge(t_lo, 2 * tiles_before + h - 1)
                    for k in range(4):
                        ins = nc.tensor.transpose(ps_t[h][:, k * P:(k + 1) * P],
                                                  q[:, (4 * h + k) * P:(4 * h + k + 1) * P], ident[:, :])
                    ins.then_inc(yt_mm, 1)

            def u_product(b):
                pe.wait_ge(yt_lo, 2 * (b + 1))
                pe.wait_ge(stage_lo, len(SPLITS))
                if not fixed(b, 1):
                    pe.wait_ge(sq_z, 2 * b)
                for k in range(KT):
                    ins = exact3(nc, ps_f[:, 0:P], (ah[:, k, :], al[:, k, :]), (yh[:, k, :], yl[:, k, :]),
                                 k == 0, k == KT - 1)
                ins.then_inc(ut_mm, 1)

            def m_product(b, h):
                if h == 0:
                    pe.wait_ge(ut_lo, b + 1)
                else:
                    pe.wait_ge(sq_m, 2 * b + 1)
                exact3(nc, ps_f[:, :], (uth[:, :], utl[:, :]), (bh[:, cols(h)], bl[:, cols(h)]),
                       True, True).then_inc(m_mm, 1)

            def z_product(b, h, ks):
                if ks[0] == 0:
                    if h == 0:
                        pe.wait_ge(sq_m, 2 * b + 2)
                    else:
                        pe.wait_ge(sq_z, 2 * b + 1)
                for k in ks:
                    ins = exact3(nc, ps_f[:, :], (yh[:, k, :], yl[:, k, :]),
                                 (wh[:, k, cols(h)], wl[:, k, cols(h)]), k == 0, k == KT - 1)
                if ks[-1] == KT - 1:
                    ins.then_inc(z_mm, 1)

            def batch(b, s, half_next, ffn, fin, more):
                for n in range(TILES):
                    if n < TILES - 2:
                        scores(b, s, n + 2)
                    elif more:
                        scores(b + 1, 1 - s, n + 2 - TILES)
                    if ffn and n == 6:
                        m_product(b - 1, 0)
                    transposes(b, n, ffn and n == 4)
                    if fin and n < 2:
                        z_product(b - 2, 1, range(4 * n, 4 * n + 4))
                    if ffn and n == 7:
                        z_product(b - 1, 0, range(0, 4))
                    if n < 2:
                        if ffn:
                            values(b - 1, GROUPS - 1, n)
                    else:
                        values(b, (n - 2) // 2, n % 2)
                    if ffn and n == 4:
                        u_product(b - 1)
                    if ffn and n == 3:
                        transposes_y(b - 1, TILES * b + 4)
                    if ffn and n == 6:
                        m_product(b - 1, 1)
                    if ffn and n == 7:
                        z_product(b - 1, 0, range(4, 8))

            pe.wait_ge(const_in, 16)
            scores(0, 0, 0)
            scores(0, 0, 1)
            all_batches(pe, batch)
            values(B - 1, GROUPS - 1, 0)
            values(B - 1, GROUPS - 1, 1)
            z_product(B - 2, 1, range(KT))
            transposes_y(B - 1, TILES * B)
            u_product(B - 1)
            m_product(B - 1, 0)
            m_product(B - 1, 1)
            z_product(B - 1, 0, range(KT))
            z_product(B - 1, 1, range(KT))


def build(nc, t):
    x2_dram = nc.dram_tensor("x2_dram", [B, L, D], FP, kind="Internal").ap()
    correlation_and_routed_ffn(nc, t["x"], t["ctx"], t["g_xattn"], t["g_ffn"],
                               t["w0"].rearrange("(k p) o -> k p o", p=P), t["b0"],
                               t["ar0"].rearrange("(k p) a -> p k a", p=P), t["rb0"], t["B0"], t["emap"],
                               t["consts"], x2_dram)
    attention_and_clamped_ffn(nc, t["ctx"], t["ctx_t"].rearrange("b (k p) c -> b p k c", p=P), t["g_xattn"],
                              t["g_ffn"], t["w1"].rearrange("(k p) o -> k p o", p=P), t["b1"], t["A1"],
                              t["B1"], t["p_scores"], t["consts"], x2_dram, t["out"])


def kernel(x, ctx_4096, g_xattn, g_ffn, L0_ffn_base_W, L0_ffn_base_b, L0_ffn_router_W, L0_ffn_router_b, L0_ffn_A,
           L0_ffn_B, L0_ffn_expert_map, L1_ffn_W, L1_ffn_b, L1_ffn_A, L1_ffn_B, L1_ffn_p_scores):
    import concourse.bacc as _bacc
    from concourse.bass_utils import run_bass_kernel_spmd as _run

    a0 = np.asarray(L0_ffn_A).reshape(ER, D).T
    pad = np.zeros((D, 1), np.float32)
    a1 = np.asarray(L1_ffn_A).transpose(1, 0, 2).reshape(KT, P, ER)
    lay = {
        "x": x, "ctx": ctx_4096, "ctx_t": np.asarray(ctx_4096).transpose(0, 2, 1),
        "g_xattn": g_xattn, "g_ffn": g_ffn,
        "w0": np.asarray(L0_ffn_base_W).T, "b0": L0_ffn_base_b,
        "ar0": np.concatenate([a0, np.asarray(L0_ffn_router_W).T, pad], axis=1), "rb0": L0_ffn_router_b,
        "B0": np.asarray(L0_ffn_B).transpose(0, 2, 1).reshape(ER, D), "emap": L0_ffn_expert_map,
        "w1": np.asarray(L1_ffn_W).T, "b1": L1_ffn_b,
        "A1": a1.transpose(1, 0, 2).reshape(P, KT * ER), "B1": np.asarray(L1_ffn_B).reshape(ER, D),
        "p_scores": np.repeat(np.asarray(L1_ffn_p_scores), R).reshape(ER, 1), "consts": constants(),
    }
    nc = _bacc.Bacc("TRN2", target_bir_lowering=False, num_devices=1)
    arrays, t = {}, {}
    for name, a in lay.items():
        a = np.ascontiguousarray(a)
        arrays[f"in_{name}"] = a
        t[name] = nc.dram_tensor(f"in_{name}", a.shape, mybir.dt.from_np(a.dtype), kind="ExternalInput").ap()
    t["out"] = nc.dram_tensor("out_0", (B, L, D), FP, kind="ExternalOutput").ap()
    build(nc, t)
    r = _run(nc, [arrays], core_ids=[0])
    return r.results[0]["out_0"]
```
